# Optimizing a Trainium2 kernel written in Bass

```python
import numpy as np
import jax
import jax.numpy as jnp

def _softmax(x, axis=-1):
    return jax.nn.softmax(x, axis=axis)

def _gelu(x):
    return jax.nn.gelu(x, approximate=True)

def _silu(x):
    return jax.nn.silu(x)

def _sigmoid(x):
    return jax.nn.sigmoid(x)

def _layernorm(x, axis=-1, eps=1e-05):
    m = jnp.mean(x, axis=axis, keepdims=True)
    v = jnp.var(x, axis=axis, keepdims=True)
    return (x - m) / jnp.sqrt(v + eps)

def _scatter_add(tgt, idx, src, axis=0):
    return tgt.at[idx].add(src)

def _segment_sum(src, seg, n):
    return jax.ops.segment_sum(src, seg, n)
kernel_name = 'mk_gps_d1_gnn_r32_a89311'

def setup_inputs(seed: int=0):
    np.random.seed(seed)
    _w = jnp.asarray

    def _rec_inputs():
        import jax
        import jax.numpy as jnp
        _gk = jax.random.key(seed)
        x = -0.0002117 + 1 * jax.random.normal(jax.random.fold_in(_gk, 1), (3125, 256), jnp.float32)
        _s = jax.random.randint(jax.random.fold_in(_gk, 2), (25000,), 0, 3125, jnp.int32)
        _d = jax.random.randint(jax.random.fold_in(_gk, 3), (25000,), 0, 3125, jnp.int32)
        _loop = jnp.arange(3125, dtype=jnp.int32)
        src = jnp.concatenate([_s, _d, _loop])
        dst = jnp.concatenate([_d, _s, _loop])
        _o = jnp.argsort(dst, stable=True)
        src = src[_o]
        dst = dst[_o]
        return (x, src, dst)
    x, src, dst = _rec_inputs()

    def _L0_gnn_setup():
        import jax, jax.numpy as jnp
        import numpy as np
        N, D_DIM, K, R = (3125, 256, 4, 16)
        E_RAND = 50000
        ETA, LAM, C = (0.5, 0.1, 0.5)
        key = jax.random.key(seed)
        k1, k2, k3, k4 = jax.random.split(key, 4)
        Z = jax.random.normal(k1, (N, D_DIM), jnp.float32)
        U = jax.random.normal(k2, (K, D_DIM, R), jnp.float32) / np.float32(np.sqrt(D_DIM))
        Dmat = jax.random.normal(k3, (D_DIM, D_DIM), jnp.float32) / np.float32(np.sqrt(D_DIM))
        head_w = jnp.ones((K,), jnp.float32) / K
        rnd = jax.random.randint(k4, (2, E_RAND), 0, N)
        loops = jnp.stack([jnp.arange(N), jnp.arange(N)])
        edge_index = jnp.concatenate([rnd, loops], axis=1)
        return {'Z': Z, 'U': U, 'Dmat': Dmat, 'head_w': head_w, 'edge_index': edge_index}
    _L0_gnn_all = _L0_gnn_setup()
    _L0_gnn_in = {k: v for k, v in _L0_gnn_all.items() if k in ('U', 'Dmat', 'head_w')}
    del _L0_gnn_all

    def _L0_mix_setup():
        import jax, jax.numpy as jnp
        import numpy as np
        MIDC = 256
        HEADS = 8
        HEADC = MIDC // HEADS
        EPS = 1e-05

        def _ln(x, gamma, beta):
            mu = jnp.mean(x, axis=-1, keepdims=True)
            var = jnp.var(x, axis=-1, keepdims=True)
            return (x - mu) * jax.lax.rsqrt(var + EPS) * gamma + beta
        key = jax.random.key(seed)
        ks = jax.random.split(key, 8)
        B, HW, C = (8, 128, MIDC)
        s = 1.0 / np.sqrt(C)
        return {'x': jax.random.normal(ks[0], (B, HW, C), jnp.float32), 'w_qkv': jax.random.normal(ks[1], (C, 3 * C), jnp.float32) * s, 'b_qkv': jnp.zeros((3 * C,), jnp.float32), 'kln_g': jnp.ones((HEADC,), jnp.float32), 'kln_b': jnp.zeros((HEADC,), jnp.float32), 'vln_g': jnp.ones((HEADC,), jnp.float32), 'vln_b': jnp.zeros((HEADC,), jnp.float32), 'w1': jax.random.normal(ks[2], (C, C), jnp.float32) * s, 'b1': jnp.zeros((C,), jnp.float32), 'w2': jax.random.normal(ks[3], (C, C), jnp.float32) * s, 'b2': jnp.zeros((C,), jnp.float32)}
    _L0_mix_all = _L0_mix_setup()
    _L0_mix_in = {k: v for k, v in _L0_mix_all.items() if k in ('w_qkv', 'b_qkv', 'kln_g', 'kln_b', 'vln_g', 'vln_b', 'w1', 'b1', 'w2', 'b2')}
    del _L0_mix_all

    def _L0_ffn_setup():
        import jax, jax.numpy as jnp
        import numpy as np
        E = 8
        K = 2
        D = 256
        H = 512
        DOUT = 256
        EPS = 1e-05
        key = jax.random.key(seed)
        ks = jax.random.split(key, 9)
        s = 0.02
        return {'x': jax.random.normal(ks[0], (4, 256, D), jnp.float32), 'gamma': 1.0 + 0.05 * jax.random.normal(ks[1], (D,), jnp.float32), 'beta': 0.05 * jax.random.normal(ks[2], (D,), jnp.float32), 'Wr': 0.01 * jax.random.normal(ks[3], (D, E), jnp.float32), 'br': jnp.zeros((E,), jnp.float32), 'W1': s * jax.random.normal(ks[4], (E, D, H), jnp.float32), 'b1': s * jax.random.normal(ks[5], (E, H), jnp.float32), 'W2': s * jax.random.normal(ks[6], (E, H, DOUT), jnp.float32), 'b2': s * jax.random.normal(ks[7], (E, DOUT), jnp.float32)}
    _L0_ffn_all = _L0_ffn_setup()
    _L0_ffn_in = {k: v for k, v in _L0_ffn_all.items() if k in ('gamma', 'beta', 'Wr', 'br', 'W1', 'b1', 'W2', 'b2')}
    del _L0_ffn_all
    return {'x': x, 'src': src, 'dst': dst, 'L0_gnn_U': _L0_gnn_in['U'], 'L0_gnn_Dmat': _L0_gnn_in['Dmat'], 'L0_gnn_head_w': _L0_gnn_in['head_w'], 'L0_mix_w_qkv': _L0_mix_in['w_qkv'], 'L0_mix_b_qkv': _L0_mix_in['b_qkv'], 'L0_mix_kln_g': _L0_mix_in['kln_g'], 'L0_mix_kln_b': _L0_mix_in['kln_b'], 'L0_mix_vln_g': _L0_mix_in['vln_g'], 'L0_mix_vln_b': _L0_mix_in['vln_b'], 'L0_mix_w1': _L0_mix_in['w1'], 'L0_mix_b1': _L0_mix_in['b1'], 'L0_mix_w2': _L0_mix_in['w2'], 'L0_mix_b2': _L0_mix_in['b2'], 'L0_ffn_gamma': _L0_ffn_in['gamma'], 'L0_ffn_beta': _L0_ffn_in['beta'], 'L0_ffn_Wr': _L0_ffn_in['Wr'], 'L0_ffn_br': _L0_ffn_in['br'], 'L0_ffn_W1': _L0_ffn_in['W1'], 'L0_ffn_b1': _L0_ffn_in['b1'], 'L0_ffn_W2': _L0_ffn_in['W2'], 'L0_ffn_b2': _L0_ffn_in['b2']}

def reference(x, src, dst, L0_gnn_U, L0_gnn_Dmat, L0_gnn_head_w, L0_mix_w_qkv, L0_mix_b_qkv, L0_mix_kln_g, L0_mix_kln_b, L0_mix_vln_g, L0_mix_vln_b, L0_mix_w1, L0_mix_b1, L0_mix_w2, L0_mix_b2, L0_ffn_gamma, L0_ffn_beta, L0_ffn_Wr, L0_ffn_br, L0_ffn_W1, L0_ffn_b1, L0_ffn_W2, L0_ffn_b2):
    import jax
    import jax.numpy as jnp

    def _L0_gnn_ref(Z, U, Dmat, head_w, edge_index):
        import jax, jax.numpy as jnp
        import numpy as np
        N, D_DIM, K, R = (3125, 256, 4, 16)
        E_RAND = 50000
        ETA, LAM, C = (0.5, 0.1, 0.5)
        src, dst = (edge_index[0], edge_index[1])
        scale = np.float32(np.sqrt(R))
        ZU = jnp.einsum('nd,kdr->knr', Z, U)
        zs = ZU[:, src, :]
        zd = ZU[:, dst, :]
        logits = (zs * zd).sum(-1) / scale
        seg_max = jax.vmap(lambda l: jax.ops.segment_max(l, dst, num_segments=N))(logits)
        exp_l = jnp.exp(logits - seg_max[:, dst])
        seg_sum = jax.vmap(lambda e: jax.ops.segment_sum(e, dst, num_segments=N))(exp_l)
        alpha = exp_l / (seg_sum[:, dst] + 1e-16)
        weighted = alpha[..., None] * zs
        agg = jax.vmap(lambda w_: jax.ops.segment_sum(w_, dst, num_segments=N))(weighted)
        w = jax.nn.softmax(head_w)
        ssa = jnp.einsum('k,knr,kdr->nd', w, agg, U)
        Z_half = (1.0 - C) * Z + C * ssa
        DZ = Z_half @ Dmat.T
        residual = Z_half - DZ @ Dmat
        grad_step = Z_half + ETA * (residual @ Dmat)
        return jax.nn.relu(grad_step - ETA * LAM)

    def _L0_mix_ref(x, w_qkv, b_qkv, kln_g, kln_b, vln_g, vln_b, w1, b1, w2, b2):
        import jax, jax.numpy as jnp
        import numpy as np
        MIDC = 256
        HEADS = 8
        HEADC = MIDC // HEADS
        EPS = 1e-05

        def _ln(x, gamma, beta):
            mu = jnp.mean(x, axis=-1, keepdims=True)
            var = jnp.var(x, axis=-1, keepdims=True)
            return (x - mu) * jax.lax.rsqrt(var + EPS) * gamma + beta
        B, HW, C = x.shape
        bias = x
        qkv = (x @ w_qkv + b_qkv).reshape(B, HW, HEADS, 3 * HEADC)
        qkv = qkv.transpose(0, 2, 1, 3)
        q, k, v = jnp.split(qkv, 3, axis=-1)
        k = _ln(k, kln_g, kln_b)
        v = _ln(v, vln_g, vln_b)
        kv = jnp.einsum('bhnd,bhne->bhde', k, v) / HW
        out = jnp.einsum('bhnd,bhde->bhne', q, kv)
        out = out.transpose(0, 2, 1, 3).reshape(B, HW, C)
        ret = out + bias
        h = jax.nn.gelu(ret @ w1 + b1, approximate=False)
        return h @ w2 + b2 + bias

    def _L0_ffn_ref(x, gamma, beta, Wr, br, W1, b1, W2, b2):
        import jax, jax.numpy as jnp
        import numpy as np
        E = 8
        K = 2
        D = 256
        H = 512
        DOUT = 256
        EPS = 1e-05
        mu = jnp.mean(x, axis=-1, keepdims=True)
        var = jnp.mean(jnp.square(x - mu), axis=-1, keepdims=True)
        xn = (x - mu) * jax.lax.rsqrt(var + EPS) * gamma + beta
        logits = jnp.einsum('bsd,de->bse', xn, Wr) + br
        top_vals, top_idx = jax.lax.top_k(logits, K)
        w = jax.nn.softmax(top_vals, axis=-1)
        w_full = jnp.einsum('bsk,bske->bse', w, jax.nn.one_hot(top_idx, E, dtype=w.dtype))
        y = jnp.zeros(x.shape[:-1] + (DOUT,), x.dtype)
        for e in range(E):
            h = jax.nn.gelu(jnp.einsum('bsd,dh->bsh', xn, W1[e]) + b1[e], approximate=False)
            y_e = jnp.einsum('bsh,hd->bsd', h, W2[e]) + b2[e]
            y = y + y_e * w_full[..., e, None]
        return y
    edge_index = jnp.stack([src, dst])
    xn = _layernorm(x, axis=-1)
    x = x + _L0_gnn_ref(xn, L0_gnn_U, L0_gnn_Dmat, L0_gnn_head_w, edge_index) + _L0_mix_ref(xn[None], L0_mix_w_qkv, L0_mix_b_qkv, L0_mix_kln_g, L0_mix_kln_b, L0_mix_vln_g, L0_mix_vln_b, L0_mix_w1, L0_mix_b1, L0_mix_w2, L0_mix_b2)[0]
    x = x + _L0_ffn_ref(_layernorm(x, axis=-1)[None], L0_ffn_gamma, L0_ffn_beta, L0_ffn_Wr, L0_ffn_br, L0_ffn_W1, L0_ffn_b1, L0_ffn_W2, L0_ffn_b2)[0]
    return x

_drawn_inputs = setup_inputs


def setup_inputs(seed=0):
    import zlib

    import numpy as np

    out = dict(_drawn_inputs(seed))
    spreads = {'L0_gnn_head_w': (0.25, 0.6),
     'L0_mix_b_qkv': (0.0, 0.288),
     'L0_mix_kln_g': (1.0, 0.6),
     'L0_mix_kln_b': (0.0, 0.49),
     'L0_mix_vln_g': (1.0, 0.6),
     'L0_mix_vln_b': (0.0, 0.433),
     'L0_mix_b1': (0.0, 0.285),
     'L0_mix_b2': (0.0, 0.1),
     'L0_ffn_br': (0.0, 0.338)}
    factors = {'L0_gnn_U': 3.443,
     'L0_ffn_gamma': 8.0,
     'L0_ffn_beta': 8.0,
     'L0_ffn_Wr': 3.513,
     'L0_ffn_b1': 29.352,
     'L0_ffn_b2': 8.0}
    for name, (base, spread) in spreads.items():
        noise = np.random.default_rng([zlib.crc32(name.encode()), seed]).standard_normal(out[name].shape)
        drawn = base * np.exp(spread * noise) if base else spread * noise
        out[name] = jnp.asarray(drawn.astype(out[name].dtype))
    for name, factor in factors.items():
        out[name] = (out[name] * factor).astype(out[name].dtype)
    return out
```

```python
from contextlib import ExitStack

import concourse.bass as bass
from concourse import mybir

F32, I32, U32, BF16 = mybir.dt.float32, mybir.dt.int32, mybir.dt.uint32, mybir.dt.bfloat16
ALU = mybir.AluOpType
ACT = mybir.ActivationFunctionType
AX = mybir.AxisListType.X

N, D, E = 3125, 256, 53125
K, R = 4, 16
KR = K * R
HEADS, HC = 8, 32
NX, H = 8, 512
T, P = 25, 125
GT = 5
NG = T // GT
GC = GT * P
CUTS = ((0, 3 * P), (3 * P, GC))
EC = 416
EP = 128 * EC
JB = 52
NB = EC // JB
SW = KR + 2 * K
SK = KR + K
LN_EPS, BIG = 1e-5, 1e30
ETA_LAM = 0.5 * 0.1
EDGE_STEPS = 2 * (KR + SK + 2 * K + 4)
TAIL_STEPS = 37
FULL = EC * 127


class Steps:

    def __init__(self, engine, sem):
        self.engine, self.sem, self.base, self.local = engine, sem, 0, 0
        self.reg, self.per = None, 0

    def __call__(self, instruction):
        instruction.then_inc(self.sem, 1)
        self.local += 1

    def value(self):
        if self.reg is None:
            return self.base + self.local
        return self.reg * self.per + (self.base + self.local)

    def settle(self):
        self.engine.wait_ge(self.sem, self.value())

    def enter(self, reg, per, first=0):
        self.base += self.local - first * per
        self.reg, self.per, self.local = reg, per, 0

    def leave(self, end):
        assert self.local == self.per, f"steps of a trip: {self.local}, not {self.per}"
        self.base += end * self.per
        self.reg, self.local = None, 0


def program(nc, a, out):
    zu_t = nc.dram_tensor("zu_t", (N, KR), F32, kind="Internal").ap()
    zd_t = nc.dram_tensor("zd_t", (EP + 128 * T, KR), F32, kind="Internal").ap()
    st_t = nc.dram_tensor("st_t", (EP, SW), F32, kind="Internal").ap()
    xt_t = nc.dram_tensor("xt_t", (N + 128, SW), F32, kind="Internal").ap()
    with ExitStack() as ctx:
        build(nc, ctx, a, out, zu_t, zd_t, st_t, xt_t)


def build(nc, ctx, a, out, zu_t, zd_t, st_t, xt_t):
    def sb(name, shape, dt=F32):
        return ctx.enter_context(nc.sbuf_tensor(name, shape, dt))

    def sem(name):
        return ctx.enter_context(nc.semaphore(name))

    x_sb = sb("x_sb", [128, T, D])
    xnT = sb("xnT", [128, NG, GT * D])
    mix_sb = xnT
    gx = sb("gx", [128, T, D])
    edge = sb("edge", [128, 3 * JB * KR + 2 * JB * SW])
    G = [edge[:, h * JB * KR:(h + 1) * JB * KR].rearrange("p (j f) -> p j f", f=KR) for h in (0, 1)]
    Zd_flat = edge[:, 2 * JB * KR:3 * JB * KR]
    Zd = Zd_flat.rearrange("p (j f) -> p j f", f=KR)
    o = 3 * JB * KR
    S_flat = [edge[:, o + h * JB * SW:o + (h + 1) * JB * SW] for h in (0, 1)]
    S = [s.rearrange("p (j f) -> p j f", f=SW) for s in S_flat]
    one_p = [s[:, 0:JB * P // 2].bitcast(BF16).rearrange("p (j f) -> p j f", f=P) for s in S_flat]
    zeros = Zd_flat
    W1 = edge[:, 0:NX * 2 * H].rearrange("p (e k m) -> p e k m", e=NX, k=2)
    W2 = edge[:, NX * 2 * H:2 * NX * 2 * H].rearrange("p (e k m) -> p e k m", e=NX, k=4)
    stage = sb("stage", [128, GT, D])
    xT_st = sb("xT_st", [128, 2, GC])
    hid = [sb(f"hid{i}", [128, 4, GC]) for i in (0, 1)]
    hid_flat = [h[:, :, :].rearrange("p a c -> p (a c)") for h in hid]
    kh = hid_flat[0][:, 0:4 * 258].rearrange("p (s g c) -> p s g c", s=4, g=2)
    vh = hid_flat[0][:, 1040:1040 + 4 * D].rearrange("p (s c) -> p s c", s=4)
    mixh = hid_flat[0][:, 0:2 * GC].rearrange("p (m c) -> p m c", m=2)
    zu_sb = hid_flat[1][:, 0:T * KR].rearrange("p (t f) -> p t f", f=KR)
    ng = hid_flat[0][:, 0:T * SW].rearrange("p (t f) -> p t f", f=SW)
    xc = hid_flat[1][:, 0:T * SW].rearrange("p (t f) -> p t f", f=SW)
    stage_flat = stage[:, :, :].rearrange("p a c -> p (a c)")
    sq = stage_flat[:, 0:4 * D].rearrange("p (s c) -> p s c", s=2)
    one_t = [s[:, 0:JB * (T + 1) // 2].bitcast(BF16).rearrange("p (j f) -> p j f", f=T + 1)
             for s in (stage_flat, hid_flat[1][:, T * KR:])]
    src_ix, dst_ix = sb("src_ix", [128, EC], I32), sb("dst_ix", [128, EC], I32)
    idxst = [sb(f"idxst{h}", [128, JB], I32) for h in (0, 1)]
    ns, negb = sb("ns", [128, EC]), sb("negb", [128, EC])
    dstf, dq, dr, df = ns, gx[:, 0:2, :].rearrange("p a c -> p (a c)")[:, 0:EC], \
        gx[:, 2:4, :].rearrange("p a c -> p (a c)")[:, 0:EC], gx[:, 4:6, :].rearrange("p a c -> p (a c)")[:, 0:EC]
    dstf = gx[:, 6:8, :].rearrange("p a c -> p (a c)")[:, 0:EC]
    dfi = gx[:, 8:10, :].rearrange("p a c -> p (a c)")[:, 0:EC].bitcast(I32)
    iota_p = gx[:, 10, 0:P]
    iota_t = gx[:, 11, 0:T + 1]
    dtd = gx[:, 12:14, :]
    ident, ones, zero = sb("ident", [128, 128]), sb("ones", [128, 128]), sb("zero", [128, 384])
    blockd, tri = sb("blockd", [128, 128]), sb("tri", [128, 128])
    eps = sb("eps", [128, 1])
    st, mv = sb("st", [128, GT, 6]), sb("mv", [128, GT, 2])
    std, rstd = sb("std", [128, GT]), sb("rstd", [128, GT])
    std2, fac = sb("std2", [128, GT]), sb("fac", [128, GT])
    NR = 42
    rows, cols = sb("rows", [NR, 128]), sb("cols", [128, NR])
    B1, MB1, BQ, GAM, BET, VG, VB = 0, 32, 34, 36, 38, 40, 41
    wq = hid_flat[0][:, 1552:1552 + 2 * D].rearrange("p (k c) -> p k c", k=2)
    dm = hid_flat[0][:, 1040:1040 + 2 * D].rearrange("p (k c) -> p k c", k=2)
    wqT = sb("wqT", [128, 2, D])
    wkv, kvb = sb("wkv", [128, 2, 2 * D]), sb("kvb", [1, 2 * D])
    cm, cmb = sb("cm", [128, 32]), sb("cmb", [1, 16])
    w1, w2, mb2 = sb("w1", [128, 2, D]), sb("w2", [128, 2, D]), sb("mb2", [1, D])
    gh = sb("gh", [128, 2, D])
    u_sb, ug = sb("u_sb", [128, 2, KR]), sb("ug", [64, D])
    hw, hwo, hws = sb("hw", [64, K]), sb("hwo", [64, 1]), sb("hws", [64, 4])
    kgr, kbr = sb("kgr", [128, 128]), sb("kbr", [128, 128])
    wr, brr, b2x = sb("wr", [128, 2, NX]), sb("brr", [128, NX]), sb("b2x", [NX, D])
    csb, ends = sb("csb", [128, T + 1]), sb("ends", [128, T])
    start, full, nid = sb("start", [128, T]), sb("full", [128, T]), sb("nid", [128, T])
    tmpn = sb("tmpn", [128, T])
    sidx, gidx = sb("sidx", [128, T], I32), sb("gidx", [128, T], I32)
    kss, kstd, krs = sb("kss", [128, 2, 16]), sb("kstd", [128, 2, 16]), sb("krs", [128, 2, 16])
    kva = stage_flat[:, 0:258].rearrange("p (k c) -> p k c", k=2)
    kvc = stage_flat[:, 258:514].rearrange("p (k c) -> p k c", k=2)
    t1 = stage_flat[:, 514:1026].rearrange("p (k c) -> p k c", k=2)
    kvs, sk = (hid_flat[1][:, T * SW + o:T * SW + o + 128] for o in (0, 128))
    weff, beff = w1, sb("beff", [128, 2])
    zlast, slast = sb("zlast", [128, KR]), sb("slast", [128, SK])
    xT_flat = xT_st[:, :, :].rearrange("p a c -> p (a c)")
    lg, d1, d2, ea = (xT_flat[:, o * JB * K:(o + 1) * JB * K].rearrange("p (j k) -> p j k", k=K) for o in range(4))
    mx = xT_flat[:, 4 * JB * K:(5 * JB + 1) * K].rearrange("p (j k) -> p j k", k=K)
    row = hid_flat[0][0:1, T * SW:T * SW + 5 * 128].rearrange("p (r c) -> p r c", r=5)
    rowi, dump_row = sb("rowi", [1, 2, 128], I32), sb("dump_row", [1, 128])
    fin, carry = stage_flat[:, 0:2 * SK], stage_flat[:, 2 * SK:2 * SK + SW]
    tgt = sb("tgt", [128, 1], I32)
    q = [stage_flat[0:SK, 208 + i * 130:208 + i * 130 + 129] for i in range(7)]
    nm, nw1, nw2, nden = (xT_flat[:, o * T * K:(o + 1) * T * K].rearrange("p (t k) -> p t k", k=K) for o in range(4))
    iota8 = sb("iota8", [128, NX])
    rl, r8, ri = sb("rl", [128, GT, NX]), sb("r8", [128, GT, 8]), sb("ri", [128, GT, 8], U32)
    rf, rd, rp = sb("rf", [128, GT, 2]), sb("rd", [128, GT, 2]), sb("rp", [128, GT, 2])
    wf, wg = sb("wf", [128, GT, NX]), sb("wg", [128, GT, NX])

    ps = [ctx.enter_context(nc.psum_tensor(f"ps{i}", [128, 512], F32)) for i in range(8)]

    gx_agg = xnT[:, 0:2, :].rearrange("p a c -> p (a c)")[:, 0:T * KR].rearrange("p (t f) -> p t f", f=KR)
    acc = xnT[:, 2, 0:2 * D].rearrange("p (s d) -> p s d", s=2)
    agg_st = xnT[:, 2, 2 * D:2 * D + GT * KR].rearrange("p (t f) -> p t f", f=KR)
    aggT, wfT = xnT[0:64, 3, 0:GC], xnT[0:NX, 4, 0:GC]

    zfirst_in = sem("zfirst_in")
    prod, kr_step, counted_block, y_used, cr_done, kv_summed = (
        sem("prod"), sem("kr_step"), sem("counted_block"), sem("y_used"), sem("cr_done"), sem("kv_summed"))
    x_in, u_in, edges_in, w_in, xw_in = sem("x_in"), sem("u_in"), sem("edges_in"), sem("w_in"), sem("xw_in")
    consts = sem("consts")
    pool_step, dve_step, act_step = sem("pool_step"), sem("dve_step"), sem("act_step")
    stats, stds = sem("stats"), sem("stds")
    xn_ready, xT_psum, xT_ready = sem("xn_ready"), sem("xT_psum"), sem("xT_ready")
    zu_psum, zu_ready, zu_stored = sem("zu_psum"), sem("zu_ready"), sem("zu_stored")
    zeroed, zeros_out = sem("zeroed"), sem("zeros_out")
    onehot, counted, counts_sb, based = sem("onehot"), sem("counted"), sem("counts_sb"), sem("based")
    places = sem("places")
    rows_psum, cols_ready = sem("rows_psum"), sem("cols_ready")
    wqT_psum, wqT_ready, dtd_psum, dtd_ready = sem("wqT_psum"), sem("wqT_ready"), sem("dtd_psum"), sem("dtd_ready")
    b_psum, gh_ready, ug_psum, hw_ready, hwe_ready, ug_ready = (
        sem("b_psum"), sem("gh_ready"), sem("ug_psum"), sem("hw_ready"), sem("hwe_ready"), sem("ug_ready"))
    wkv_ready = sem("wkv_ready")
    kx_ready, kv_psum, gx_psum, gx_ready = sem("kx_ready"), sem("kv_psum"), sem("gx_psum"), sem("gx_ready")
    sq_ready, ss_ready, ks_ready, kv_ready, kv_used = (
        sem("sq_ready"), sem("ss_ready"), sem("ks_ready"), sem("kv_ready"), sem("kv_used"))
    kvt_ready, t1_psum, t1_ready, we_psum, we_ready = (
        sem("kvt_ready"), sem("t1_psum"), sem("t1_ready"), sem("we_psum"), sem("we_ready"))
    mh_psum, mh_ready, mo_psum, mo_ready = sem("mh_psum"), sem("mh_ready"), sem("mo_psum"), sem("mo_ready")
    zd_scattered, zd_in, zd_free = sem("zd_scattered"), sem("zd_in"), sem("zd_free")
    g_in, g_free = [sem("g_in0"), sem("g_in1")], [sem("g_free0"), sem("g_free1")]
    e_diff, e_exp = sem("e_diff"), sem("e_exp")
    s_ready, s_out = sem("s_ready"), [sem("s_out0"), sem("s_out1")]
    fin_ready, fin_psum, q_ready, q_exp, cr_ready, cr_psum, cr_sb, cr_out = (
        sem("fin_ready"), sem("fin_psum"), sem("q_ready"), sem("q_exp"), sem("cr_ready"), sem("cr_psum"),
        sem("cr_sb"), sem("cr_out"))
    row_ready, row_psum, xt_init_ready, xt_init = sem("row_ready"), sem("row_psum"), sem("xt_init_ready"), sem("xt_init")
    ng_in, xc_in, merge_d, merge_e = sem("ng_in"), sem("xc_in"), sem("merge_d"), sem("merge_e")
    agg_ready, agg_psum, aggT_ready, y_psum, x2_ready = (
        sem("agg_ready"), sem("agg_psum"), sem("aggT_ready"), sem("y_psum"), sem("x2_ready"))
    stats2, stds2, z_ready, zT_psum, zT_ready = sem("stats2"), sem("stds2"), sem("z_ready"), sem("zT_psum"), sem("zT_ready")
    r_psum, r_read, r_diff, r_exp, wf_ready, wfT_psum, wfT_ready = (
        sem("r_psum"), sem("r_read"), sem("r_diff"), sem("r_exp"), sem("wf_ready"), sem("wfT_psum"), sem("wfT_ready"))
    b2_psum, b2_used, h_psum, h_ready, ye_psum, ye_used = (
        sem("b2_psum"), sem("b2_used"), sem("h_psum"), sem("h_ready"), sem("ye_psum"), sem("ye_used"))
    out_ready, stored = sem("out_ready"), sem("stored")

    x_v = a["x"].rearrange("(p t) d -> p t d", t=T)
    out_v = out.rearrange("(p t) d -> p t d", t=T)
    zu_v = zu_t.rearrange("(p t) f -> p t f", t=T)
    zd_v = zd_t[0:EP, :].rearrange("(p j) f -> p j f", j=EC)
    st_v = st_t.rearrange("(p j) f -> p j f", j=EC)
    xt_v = xt_t[0:N, :].rearrange("(p t) f -> p t f", t=T)
    w_qkv = a["L0_mix_w_qkv"].rearrange("(k c) (h m) -> k c h m", k=2, m=3 * HC)
    b_qkv = a["L0_mix_b_qkv"].rearrange("(a h m) -> a h m", a=1, m=3 * HC)
    XL = 2 * NG * 16
    SPLIT = ((0, 112), (112, P))

    spare = {name: sb(f"spare_{name}", [128, 1]) for name in ("dve", "pool")}

    def held(engine):
        if engine is nc.vector:
            nc.vector.memset(spare["dve"][:, :], 0.0)
        else:
            nc.gpsimd.tensor_tensor(spare["pool"][:, :], eps[:, :], eps[:, :], ALU.add)

    block = ctx.enter_context(nc.Block())

    @block.sync
    def _(sp):
        for g in range(NG):
            for lo, hi in SPLIT:
                sp.dma_start(x_sb[lo:hi, g * GT:(g + 1) * GT, :], x_v[lo:hi, g * GT:(g + 1) * GT, :]).then_inc(x_in, 16)
        for k in range(2):
            sp.dma_start(u_sb[:, k, :].rearrange("c (h r) -> c h r", h=K),
                         a["L0_gnn_U"][:, k * 128:(k + 1) * 128, :].rearrange("h c r -> c h r")).then_inc(u_in, 16)
        sp.wait_ge(zeroed, 1)
        for b in range(NB):
            sp.dma_start(zd_v[:, b * JB:(b + 1) * JB, :], Zd).then_inc(zeros_out, 16)
        sp.wait_ge(zu_ready, T)
        for lo, hi in SPLIT:
            sp.dma_start(zu_v[lo:hi, :, :], zu_sb[lo:hi, :, :]).then_inc(zu_stored, 16)
        sp.wait_ge(xt_init_ready, 2)
        for lo, hi in SPLIT:
            sp.dma_start(xt_v[lo:hi, :, :], xc[lo:hi, :, :]).then_inc(xt_init, 16)
        sp.wait_ge(zd_scattered, 16 * T)
        sp.dma_start(Zd, zd_v[:, 0:JB, :]).then_inc(zd_in, 16)

        def block_io(i, h, load):
            if load:
                sp.wait_ge(zd_free, i * 2 + (h + 1))
                sp.dma_start(Zd, zd_v[:, bass.ds(i * (2 * JB) + (h + 1) * JB, JB), :]).then_inc(zd_in, 16)
            sp.wait_ge(s_ready, i * 2 + (h + 1))
            sp.dma_start(st_v[:, bass.ds(i * (2 * JB) + h * JB, JB), :], S[h]).then_inc(s_out[h], 16)

        with sp.Fori(0, NB // 2 - 1) as i:
            block_io(i, 0, True)
            block_io(i, 1, True)
        block_io(NB // 2 - 1, 0, True)
        block_io(NB // 2 - 1, 1, False)
        sp.wait_ge(s_out[0], 16 * NB // 2)
        sp.wait_ge(s_out[1], 16 * NB // 2)
        for k in range(2):
            sp.dma_start(W1[:, :, k, :], a["L0_ffn_W1"][:, k * 128:(k + 1) * 128, :].rearrange("e c m -> c e m")).then_inc(xw_in, 16)
        for k in range(4):
            sp.dma_start(W2[:, :, k, :], a["L0_ffn_W2"][:, k * 128:(k + 1) * 128, :].rearrange("e c m -> c e m")).then_inc(xw_in, 16)
        sp.wait_ge(cr_out, 16)
        for lo, hi in SPLIT:
            sp.dma_start(xc[lo:hi, :, :], xt_v[lo:hi, :, :]).then_inc(xc_in, 16)
        with sp.Fori(0, NG) as g:
            sp.wait_ge(out_ready, g + 1)
            for lo, hi in SPLIT:
                sp.dma_start(out_v[lo:hi, bass.ds(g * GT, GT), :], x_sb[lo:hi, bass.ds(g * GT, GT), :]).then_inc(stored, 16)
        sp.wait_ge(stored, 2 * 16 * NG)

    W_LOADS = []

    def zu_copy(act, g, t):
        act.wait_ge(zu_psum, g * GT + (t + 1))
        nc.scalar.copy(zu_sb[0:P, g * GT + t, :], ps[2 + t % 2][0:P, 0:KR]).then_inc(zu_ready, 1)

    @block.scalar
    def _(act):
        def load(dst, src, s=w_in):
            act.dma_start(dst, src).then_inc(s, 16)
            if s is w_in:
                W_LOADS.append(1)

        act.wait_ge(consts, 1)
        load(dst_ix[0:112, :], a["dst"][0:112 * EC].rearrange("(p j) -> p j", j=EC), edges_in)
        load(dst_ix[112:127, :], a["dst"][112 * EC:FULL].rearrange("(p j) -> p j", j=EC), edges_in)

        load(dst_ix[127:128, 0:E - FULL], a["dst"][FULL:E].rearrange("(p j) -> p j", p=1), edges_in)
        load(src_ix[0:112, :], a["src"][0:112 * EC].rearrange("(p j) -> p j", j=EC), edges_in)
        load(src_ix[112:127, :], a["src"][112 * EC:FULL].rearrange("(p j) -> p j", j=EC), edges_in)
        load(src_ix[127:128, 0:E - FULL], a["src"][FULL:E].rearrange("(p j) -> p j", p=1), edges_in)
        with nc.allow_non_contiguous_dma(reason="first and last dst of each partition: 255 words"):
            load(rowi[0:1, 0, :], a["dst"][0:1 + 127 * EC:EC].rearrange("(p j) -> p j", p=1), edges_in)
            load(rowi[0:1, 1, 0:127], a["dst"][EC - 1:FULL:EC].rearrange("(p j) -> p j", p=1), edges_in)
        for k in range(2):
            load(dm[:, k, :], a["L0_gnn_Dmat"][k * 128:(k + 1) * 128, :])
            load(wq[:, k, :].rearrange("c (h m) -> c h m", m=HC), w_qkv[k, :, :, 0:HC])
            for part in (0, 1):
                load(wkv[:, k, part * D:(part + 1) * D].rearrange("c (h m) -> c h m", m=HC),
                     w_qkv[k, :, :, (part + 1) * HC:(part + 2) * HC])
            load(w1[:, k, :], a["L0_mix_w1"][k * 128:(k + 1) * 128, :])
            load(w2[:, k, :], a["L0_mix_w2"][k * 128:(k + 1) * 128, :])
            load(wr[:, k, :], a["L0_ffn_Wr"][k * 128:(k + 1) * 128, :])
        for part in (0, 1):
            load(kvb[0:1, part * D:(part + 1) * D].rearrange("a (h m) -> a h m", m=HC),
                 b_qkv[:, :, (part + 1) * HC:(part + 2) * HC])
        load(rows[B1:B1 + 32, :], a["L0_ffn_b1"].rearrange("e (m p) -> (e m) p", p=128))
        load(rows[MB1:MB1 + 2, :], a["L0_mix_b1"].rearrange("(m p) -> m p", p=128))
        for k in range(2):
            load(rows[BQ + k:BQ + k + 1, :].rearrange("a (h m) -> a h m", m=HC), b_qkv[:, 4 * k:4 * k + 4, 0:HC])
        load(rows[GAM:GAM + 2, :], a["L0_ffn_gamma"].rearrange("(m p) -> m p", p=128))
        load(rows[BET:BET + 2, :], a["L0_ffn_beta"].rearrange("(m p) -> m p", p=128))
        for r in range(4):
            load(rows[VG:VG + 1, r * HC:(r + 1) * HC], a["L0_mix_vln_g"].rearrange("(a m) -> a m", a=1))
            load(rows[VB:VB + 1, r * HC:(r + 1) * HC], a["L0_mix_vln_b"].rearrange("(a m) -> a m", a=1))
            load(kgr[:, r * HC:(r + 1) * HC], a["L0_mix_kln_g"].partition_broadcast(128))
            load(kbr[:, r * HC:(r + 1) * HC], a["L0_mix_kln_b"].partition_broadcast(128))
        load(mb2[0:1, :], a["L0_mix_b2"].rearrange("(a m) -> a m", a=1))
        load(brr[:, :], a["L0_ffn_br"].partition_broadcast(128))
        load(b2x[:, :], a["L0_ffn_b2"])
        load(hw[:, :], a["L0_gnn_head_w"].partition_broadcast(64))
        for k in range(K):
            load(hwo[k * R:(k + 1) * R, :], a["L0_gnn_head_w"][k:k + 1].partition_broadcast(R))

        act.wait_ge(consts, 2)
        with act.Fori(0, NG) as g:
            act.wait_ge(stats, g + 1)
            nc.scalar.activation(std[0:P, :], mv[0:P, :, 1], ACT.Sqrt, bias=eps[0:P, :]).then_inc(stds, 1)
            act.wait_ge(zu_psum, g * GT)
            for t in range(GT):
                act.wait_ge(xT_psum, g * GT + (t + 1))
                src = ps[t % 2][:, 0:2 * P].rearrange("p (k c) -> p k c", k=2)
                nc.scalar.copy(xT_st[:, :, t * P:(t + 1) * P], src)
                nc.scalar.copy(xnT[:, g, :][:, 0:2 * GC].rearrange("p (k c) -> p k c", k=2)[:, :, t * P:(t + 1) * P],
                               src).then_inc(xT_ready, 1)
                if t:
                    zu_copy(act, g, t - 1)
            zu_copy(act, g, GT - 1)

        act.wait_ge(rows_psum, 1)
        nc.scalar.copy(cols[:, :], ps[0][:, 0:NR]).then_inc(cols_ready, 1)
        act.wait_ge(wqT_psum, 1)
        nc.scalar.copy(wqT[:, :, :], ps[1][:, :].rearrange("p (k c) -> p k c", k=2)).then_inc(wqT_ready, 1)
        act.wait_ge(dtd_psum, 1)
        nc.scalar.copy(dtd, ps[2][:, :].rearrange("p (k c) -> p k c", k=2)).then_inc(dtd_ready, 1)
        act.wait_ge(hw_ready, 1)
        nc.scalar.activation(hws[:, 0:1], hwo[:, :], ACT.Exp, bias=hws[:, 3:4])
        nc.scalar.activation(hw[:, :], hw[:, :], ACT.Exp, bias=hws[:, 3:4], accum_out=hws[:, 1:2]).then_inc(hwe_ready, 1)

        act.wait_ge(counted, 1)
        act.wait_ge(based, 1)
        act.wait_ge(xn_ready, T)
        act.wait_ge(xT_psum, T)
        with act.Fori(0, NG) as g:
            for t in range(GT):
                act.wait_ge(gx_psum, g * GT)
                nc.scalar.copy(xT_st[:, :, t * P:(t + 1) * P],
                               xnT[:, g, :][:, 0:2 * GC].rearrange("p (k c) -> p k c", k=2)[:, :, t * P:(t + 1) * P]
                               ).then_inc(kx_ready, 1)
            for t in range(GT):
                act.wait_ge(kv_psum, g * GT + (t + 1))
                act.wait_ge(ss_ready, g * GT + (t - 1 if t >= 2 else 0))
                nc.scalar.square(sq[0:P, t % 2, :], ps[t % 2][0:P, :]).then_inc(sq_ready, 1)
                act.wait_ge(gx_psum, g * GT + (t + 1))
                nc.scalar.copy(gx[0:P, g * GT + t, :], ps[2 + t % 2][0:P, 0:D]).then_inc(gx_ready, 1)
                act.wait_ge(ss_ready, g * GT + (t + 1))
                nc.scalar.activation(kstd[0:P, t % 2, :], kss[0:P, t % 2, :], ACT.Sqrt,
                                     bias=eps[0:P, :], scale=1.0 / HC).then_inc(ks_ready, 1)

        def edge_exps(i, h):
            act.wait_ge(e_diff, i * 2 + (h + 1))
            nc.scalar.activation(S[h][:, :, KR:KR + K], d1[:, :, :], ACT.Exp, scale=0.25)
            nc.scalar.activation(ea[:, :, :], d2[:, :, :], ACT.Exp, scale=0.25).then_inc(e_exp, 1)

        act.wait_ge(t1_psum, 1)
        nc.scalar.copy(t1[:, :, :], ps[4][:, :].rearrange("p (k c) -> p k c", k=2)).then_inc(t1_ready, 1)
        act.wait_ge(we_ready, 1)
        with act.Fori(0, NG) as g:
            act.wait_ge(mo_psum, g * GT)
            for m in range(2):
                for c, (lo, hi) in enumerate(CUTS):
                    act.wait_ge(mh_psum, g * 4 + (2 * m + c + 1))
                    nc.scalar.activation(mixh[:, m, lo:hi], ps[2 * m + c][:, 0:hi - lo], ACT.Gelu,
                                         bias=beff[:, m:m + 1]).then_inc(mh_ready, 1)
            for t in range(GT):
                act.wait_ge(mo_psum, g * GT + (t + 1))
                nc.scalar.copy(mix_sb[0:P, g, t * D:(t + 1) * D], ps[4 + t % 2][0:P, 0:D]).then_inc(mo_ready, 1)
        with act.Fori(0, NB // 2) as i:
            edge_exps(i, 0)
            edge_exps(i, 1)

        act.wait_ge(q_ready, 1)
        nc.scalar.activation(q[3][:, 0:128], q[3][:, 0:128], ACT.Exp, scale=0.25)
        nc.scalar.activation(q[4][:, 0:128], q[4][:, 0:128], ACT.Exp, scale=0.25).then_inc(q_exp, 1)
        act.wait_ge(cr_psum, 1)
        nc.scalar.copy(carry[:, 0:SK], ps[0][:, 0:SK])
        nc.scalar.copy(carry[:, SK:SW], ps[1][:, KR:SK]).then_inc(cr_sb, 1)
        act.wait_ge(merge_d, 1)
        nc.scalar.activation(nw1[0:P, :, :], nw1[0:P, :, :], ACT.Exp, scale=0.25)
        nc.scalar.activation(nw2[0:P, :, :], nw2[0:P, :, :], ACT.Exp, scale=0.25).then_inc(merge_e, 1)

        act.wait_ge(cols_ready, 1)
        with act.Fori(0, NG) as g:
            act.wait_ge(agg_psum, g + 1)
            nc.scalar.copy(aggT[:, 0:4 * P], ps[6][0:64, 0:4 * P])
            nc.scalar.copy(aggT[:, 4 * P:GC], ps[7][0:64, 0:P]).then_inc(aggT_ready, 1)
            act.wait_ge(stats2, g + 1)
            nc.scalar.activation(std[0:P, :], mv[0:P, :, 1], ACT.Sqrt, bias=eps[0:P, :]).then_inc(stds2, 1)
            act.wait_ge(stats2, g + 1)
            act.wait_ge(r_read, g + 1)
            nc.scalar.activation(std2[0:P, :], fac[0:P, :], ACT.Sqrt, bias=eps[0:P, :]).then_inc(stds2, 1)
            act.wait_ge(r_diff, g + 1)
            nc.scalar.activation(rd[0:P, :, 1], rd[0:P, :, 0], ACT.Exp).then_inc(r_exp, 1)
            act.wait_ge(wfT_psum, g + 1)
            nc.scalar.copy(wfT[:, 0:4 * P], ps[6][0:NX, 0:4 * P])
            nc.scalar.copy(wfT[:, 4 * P:GC], ps[7][0:NX, 0:P]).then_inc(wfT_ready, 1)
            for e in range(NX):
                act.wait_ge(ye_psum, g * (NX * GT) + max(0, e - 1) * GT)
                for m in range(4):
                    for c, (lo, hi) in enumerate(CUTS):
                        act.wait_ge(h_psum, g * (8 * NX) + (8 * e + 2 * m + c + 1))
                        nc.scalar.activation(hid[e % 2][:, m, lo:hi], ps[2 * (m % 2) + c][:, 0:hi - lo], ACT.Gelu,
                                             bias=cols[:, B1 + 4 * e + m:B1 + 4 * e + m + 1]).then_inc(h_ready, 1)

    @block.gpsimd
    def _(pool):
        step = Steps(pool, pool_step)
        gp = nc.gpsimd
        step(gp.memset(dst_ix[:, :], N))
        step(gp.memset(src_ix[:, :], 0))
        step.settle()
        gp.memset(eps[:, :], LN_EPS).then_inc(consts, 1)
        step(gp.memset(ident[:, :], 0.0))
        gp.memset(Zd_flat, 0.0).then_inc(zeroed, 1)
        step(gp.memset(ones[:, :], 1.0))
        step(gp.memset(zero[:, :], 0.0))
        step.settle()
        step(gp.affine_select(out=ident[:, :], in_=ident[:, :], compare_op=ALU.not_equal, fill=1.0, base=0,
                              pattern=[[-1, 128]], channel_multiplier=1))
        step(gp.affine_select(out=tri[:, :], in_=ones[:, :], compare_op=ALU.is_gt, fill=0.0, base=0,
                              pattern=[[1, 128]], channel_multiplier=-1))
        step(gp.memset(blockd[:, :], 0.0))
        step.settle()
        for b in range(4):
            step(gp.memset(blockd[b * HC:(b + 1) * HC, b * HC:(b + 1) * HC], 1.0 / N))
            step.settle()
        step(gp.iota(iota_p, [[1, P]], base=0, channel_multiplier=0, allow_small_or_imprecise_dtypes=True))
        step(gp.iota(iota_t, [[1, T + 1]], base=0, channel_multiplier=0, allow_small_or_imprecise_dtypes=True))
        step(gp.iota(iota8[:, :], [[1, NX]], base=0, channel_multiplier=0, allow_small_or_imprecise_dtypes=True))
        step(gp.iota(nid[:, :], [[1, T]], base=0, channel_multiplier=T, allow_small_or_imprecise_dtypes=True))
        step.settle()
        step(gp.iota(dump_row[0:1, :], [[1, 128]], base=N, channel_multiplier=0, allow_small_or_imprecise_dtypes=True))
        step.settle()
        step(gp.iota(sidx[:, :], [[1, T]], base=EP, channel_multiplier=T))
        step(gp.memset(gidx[:, :], 0))
        step.settle()
        step(gp.memset(zu_sb[96:128, :, :], 0.0))
        step.settle()
        step(gp.memset(rowi[0:1, 1, 127:128], N))
        step.settle()
        step(gp.memset(slast[:, :], 0.0))
        step(gp.memset(kh[:, :, :, 128:129], 1.0))
        step.settle()
        gp.memset(hws[:, :], 0.0).then_inc(consts, 1)

        def gathers(i, h, first):
            if not first:
                pool.wait_ge(g_free[h], i)
            step(gp.tensor_copy(idxst[h][:, :], src_ix[:, bass.ds(i * (2 * JB) + h * JB, JB)]))
            step.settle()
            if not first:
                held(nc.gpsimd)
            for j in range(JB):
                gp.indirect_dma_start(G[h][:, j, :], None, zu_t,
                                      bass.IndirectOffsetOnAxis(ap=idxst[h][:, j:j + 1], axis=0)).then_inc(g_in[h], 16)

        pool.wait_ge(edges_in, 8 * 16)
        pool.wait_ge(zu_stored, 2 * 16)
        gp.indirect_dma_start(zlast[:, :], None, zu_t,
                              bass.IndirectOffsetOnAxis(ap=dst_ix[:, 0:1], axis=0)).then_inc(zfirst_in, 16)
        gathers(0, 0, True)
        gathers(0, 1, True)
        pool.wait_ge(zeros_out, 16 * NB)
        pool.wait_ge(places, 1)
        for t in range(T):
            gp.indirect_dma_start(zd_t, bass.IndirectOffsetOnAxis(ap=sidx[:, t:t + 1], axis=0),
                                  zu_sb[:, t, :], None).then_inc(zd_scattered, 16)
        pool.wait_ge(zd_scattered, 16 * T)
        gp.memset(xc[:, :, 0:SK], 0.0).then_inc(xt_init_ready, 1)
        gp.memset(xc[:, :, SK:SW], -BIG).then_inc(xt_init_ready, 1)
        with pool.Fori(1, NB // 2) as i:
            step.enter(i, 2, 1)
            gathers(i, 0, False)
            gathers(i, 1, False)
            step.leave(NB // 2)
        pool.wait_ge(s_out[0], 16 * NB // 2)
        pool.wait_ge(s_out[1], 16 * NB // 2)
        pool.wait_ge(mo_ready, T)
        for t in range(T):
            gp.indirect_dma_start(ng[:, t, :], None, st_t,
                                  bass.IndirectOffsetOnAxis(ap=gidx[:, t:t + 1], axis=0)).then_inc(ng_in, 16)
        pool.wait_ge(xt_init, 2 * 16)
        pool.wait_ge(cr_sb, 1)
        pool.wait_ge(cr_ready, 1)
        gp.indirect_dma_start(xt_t, bass.IndirectOffsetOnAxis(ap=tgt[:, 0:1], axis=0), carry[:, :], None).then_inc(cr_out, 16)
        pool.wait_ge(cr_out, 16)

    @block.vector
    def _(dve):
        step = Steps(dve, dve_step)
        v = nc.vector

        def bc(ap, shape):
            return ap.broadcast_to(shape)

        dve.wait_ge(x_in, XL)
        dve.wait_ge(consts, 2)
        with dve.Fori(0, NG) as g:
            step.enter(g, 3 * GT)
            for t in range(GT):
                step(v.bn_stats(st[0:P, t, :], x_sb[0:P, g * GT + t, :]))
            step.settle()
            held(nc.vector)
            for t in range(GT):
                if t < GT - 1:
                    step(v.bn_aggr(mv[0:P, t, :], st[0:P, t, :]))
                else:
                    v.bn_aggr(mv[0:P, t, :], st[0:P, t, :]).then_inc(stats, 1)
            dve.wait_ge(stds, g + 1)
            step(v.reciprocal(rstd[0:P, :], std[0:P, :]))
            step.settle()
            dve.wait_ge(xT_psum, g * GT)
            for t in range(GT):
                v.tensor_scalar(stage[0:P, t, :], x_sb[0:P, g * GT + t, :], mv[0:P, t, 0:1], rstd[0:P, t:t + 1],
                                ALU.subtract, ALU.mult).then_inc(xn_ready, 1)
                if t:
                    dve.wait_ge(xn_ready, g * GT + t)
                    step(v.tensor_tensor(x_sb[0:P, g * GT + (t - 1), :], x_sb[0:P, g * GT + (t - 1), :], stage[0:P, t - 1, :], ALU.add))
            dve.wait_ge(xn_ready, g * GT + GT)
            step(v.tensor_tensor(x_sb[0:P, g * GT + (GT - 1), :], x_sb[0:P, g * GT + (GT - 1), :], stage[0:P, GT - 1, :], ALU.add))
            step.leave(NG)

        dve.wait_ge(edges_in, 8 * 16)
        step(v.tensor_copy(dstf, dst_ix[:, :]))
        step(v.memset(ns[:, 0:1], 0.0))
        step.settle()
        step(v.tensor_tensor(ns[:, 1:EC], dstf[:, 1:EC], dstf[:, 0:EC - 1], ALU.is_equal))
        step(v.tensor_scalar(dq, dstf, 1.0 / T, 0.5 / T - 0.5, ALU.mult, ALU.add))
        step.settle()
        step(v.tensor_scalar(negb[:, :], ns[:, :], -1.0, BIG, ALU.add, ALU.mult))
        step(v.tensor_copy(dfi, dq))
        step.settle()
        step(v.tensor_copy(dq, dfi))
        step.settle()
        step(v.scalar_tensor_tensor(dr, dq, -float(T), dstf, ALU.mult, ALU.add))
        step.settle()
        step(v.tensor_scalar(df, dr, 0.0, None, ALU.is_lt))
        step.settle()
        step(v.tensor_tensor(dq, dq, df, ALU.subtract))
        step(v.scalar_tensor_tensor(dr, df, float(T), dr, ALU.mult, ALU.add))
        step.settle()
        step(v.tensor_scalar(df, dr, float(T), None, ALU.is_ge))
        step.settle()
        step(v.tensor_tensor(dq, dq, df, ALU.add))
        step(v.scalar_tensor_tensor(dr, df, -float(T), dr, ALU.mult, ALU.add))
        step.settle()

        dve.wait_ge(xT_psum, T)
        with dve.Fori(0, NB // 2) as i:
            for h in (0, 1):
                dve.wait_ge(counted_block, i * 2)
                at = bass.ds(i * (2 * JB) + h * JB, JB)
                v.tensor_tensor(one_p[h], bc(iota_p.unsqueeze(1), [128, JB, P]),
                                bc(dq[:, at].unsqueeze(2), [128, JB, P]), ALU.is_equal).then_inc(onehot, 1)
                v.tensor_tensor(one_t[h][:, :, :], bc(iota_t.unsqueeze(1), [128, JB, T + 1]),
                                bc(dr[:, at].unsqueeze(2), [128, JB, T + 1]), ALU.is_ge).then_inc(onehot, 1)

        dve.wait_ge(counted, 1)
        v.tensor_copy(csb[0:P, :], ps[4][0:P, 0:T + 1]).then_inc(counts_sb, 1)
        dve.wait_ge(based, 1)
        dve.wait_ge(counts_sb, 1)
        step(v.tensor_copy(start[0:P, 0:1], ps[5][0:P, 0:1]))
        step.settle()
        step(v.tensor_scalar(ends[0:P, :], csb[0:P, 0:T], start[0:P, 0:1], None, ALU.add))
        step.settle()
        step(v.tensor_copy(start[0:P, 1:T], ends[0:P, 0:T - 1]))
        step.settle()
        step(v.tensor_tensor(full[0:P, :], ends[0:P, :], start[0:P, :], ALU.is_gt))
        step(v.tensor_tensor(tmpn[0:P, :], start[0:P, :], nid[0:P, :], ALU.subtract))
        step(v.tensor_scalar(gidx[0:P, :], ends[0:P, :], -1.0, 0.0, ALU.add, ALU.max))
        step.settle()
        step(v.tensor_scalar(tmpn[0:P, :], tmpn[0:P, :], -float(EP), None, ALU.add))
        step.settle()
        step(v.tensor_tensor(tmpn[0:P, :], tmpn[0:P, :], full[0:P, :], ALU.mult))
        step.settle()
        step(v.scalar_tensor_tensor(tmpn[0:P, :], tmpn[0:P, :], float(EP), nid[0:P, :], ALU.add, ALU.add))
        step.settle()
        v.tensor_copy(sidx[0:P, :], tmpn[0:P, :]).then_inc(places, 1)

        dve.wait_ge(w_in, 16 * len(W_LOADS))
        k4 = wkv[:, :, :].rearrange("c k (h m) -> c (k h) m", m=HC)
        b4 = kvb[0:1, :].rearrange("c (h m) -> c h m", m=HC)
        step(v.tensor_reduce(cm[:, :], k4, AX.X, ALU.add))
        step(v.tensor_reduce(cmb[:, :], b4, AX.X, ALU.add))
        step(v.tensor_reduce(hws[:, 2:3], hw[:, :], AX.X, ALU.max))
        step.settle()
        step(v.tensor_scalar(cm[:, :], cm[:, :], 1.0 / HC, None, ALU.mult))
        step(v.tensor_scalar(cmb[:, :], cmb[:, :], 1.0 / HC, None, ALU.mult))
        v.tensor_scalar(hws[:, 3:4], hws[:, 2:3], -1.0, None, ALU.mult).then_inc(hw_ready, 1)
        step.settle()
        v.tensor_tensor(k4, k4, bc(cm[:, :].unsqueeze(2), [128, 32, HC]), ALU.subtract).then_inc(wkv_ready, 1)
        v.tensor_tensor(b4, b4, bc(cmb[:, :].unsqueeze(2), [1, 16, HC]), ALU.subtract).then_inc(wkv_ready, 1)
        dve.wait_ge(b_psum, 1)
        step(v.tensor_tensor(gh[:, :, :], dm[:, :, :], ps[3][:, :].rearrange("p (k c) -> p k c", k=2), ALU.subtract))
        step.settle()
        step(v.tensor_scalar(gh[:, :, :], gh[:, :, :], 0.25, None, ALU.mult))
        step.settle()
        for k in range(2):
            d = gh[:, k, k * 128:(k + 1) * 128]
            v.scalar_tensor_tensor(d, ident[:, :], 0.5, d, ALU.mult, ALU.add).then_inc(gh_ready, 1)
        dve.wait_ge(hwe_ready, 1)
        step(v.reciprocal(hws[:, 2:3], hws[:, 1:2]))
        step.settle()
        step(v.tensor_tensor(hws[:, 3:4], hws[:, 0:1], hws[:, 2:3], ALU.mult))
        step.settle()
        dve.wait_ge(ug_psum, 1)
        v.tensor_scalar(ug[:, :], ps[7][0:64, 0:D], hws[:, 3:4], None, ALU.mult).then_inc(ug_ready, 1)

        with dve.Fori(0, NG) as g:
            for t in range(GT):
                dve.wait_ge(sq_ready, g * GT + (t + 1))
                v.tensor_reduce(kss[0:P, t % 2, :], sq[0:P, t % 2, :].rearrange("p (h m) -> p h m", m=HC),
                                AX.X, ALU.add).then_inc(ss_ready, 1)
                dve.wait_ge(ks_ready, g * GT + (t + 1))
                step_kr = v.reciprocal(krs[0:P, t % 2, :], kstd[0:P, t % 2, :])
                step_kr.then_inc(kr_step, 1)
                dve.wait_ge(kr_step, g * GT + (t + 1))
                dve.wait_ge(kv_used, g * GT + (t - 3 if t >= 4 else 0))
                k_ps = ps[t % 2][0:P, 0:D].rearrange("p (a h m) -> p a h m", a=2, m=HC)
                r_ap = krs[0:P, t % 2, :]
                for hg in (0, 1):
                    v.tensor_tensor(kh[0:P, t % 4, hg, 0:128].rearrange("p (h m) -> p h m", m=HC), k_ps[:, hg],
                                    bc(r_ap[:, 4 * hg:4 * hg + 4].unsqueeze(2), [P, 4, HC]), ALU.mult).then_inc(kv_ready, 1)
                v.tensor_tensor(vh[0:P, t % 4, :].rearrange("p (h m) -> p h m", m=HC),
                                ps[t % 2][0:P, D:2 * D].rearrange("p (h m) -> p h m", m=HC),
                                bc(r_ap[:, 8:16].unsqueeze(2), [P, 8, HC]), ALU.mult).then_inc(kv_ready, 1)

        dve.wait_ge(kv_summed, 1)
        dve.wait_ge(cols_ready, 1)
        for hg in (0, 1):
            step(v.tensor_copy(kva[:, hg, :], ps[6 + hg][:, 0:129]))
            step(v.tensor_copy(sk[:, :], ps[6 + hg][:, 256:384]))
            step.settle()
            step(v.tensor_tensor(kvs[:, :], kva[:, hg, 0:128], kgr[:, :], ALU.mult))
            step(v.tensor_tensor(sk[:, :], sk[:, :], kgr[:, :], ALU.mult))
            step.settle()
            step(v.scalar_tensor_tensor(kvs[:, :], kbr[:, :], kva[:, hg, 128:129], kvs[:, :], ALU.mult, ALU.add))
            step(v.scalar_tensor_tensor(sk[:, :], kbr[:, :], float(N), sk[:, :], ALU.mult, ALU.add))
            step.settle()
            step(v.tensor_scalar(sk[:, :], sk[:, :], cols[:, VB:VB + 1], None, ALU.mult))
            step.settle()
            step(v.scalar_tensor_tensor(kvs[:, :], kvs[:, :], cols[:, VG:VG + 1], sk[:, :], ALU.mult, ALU.add))
            step.settle()
            v.tensor_tensor(kvc[:, hg, :], kvs[:, :], blockd[:, :], ALU.mult).then_inc(kvt_ready, 1)
            dve.wait_ge(kvt_ready, hg + 1)
        dve.wait_ge(we_psum, 1)
        w_ps = ps[5][:, :].rearrange("p (k c) -> p k c", k=2)
        step(v.tensor_tensor(weff[:, :, :], w1[:, :, :], w_ps, ALU.add))
        step.settle()
        v.tensor_tensor(beff[:, :], ps[4][:, 0:2], cols[:, MB1:MB1 + 2], ALU.add).then_inc(we_ready, 1)

        def edges(i, h):
            b1 = i * 2 + (h + 1)
            at = bass.ds(i * (2 * JB) + h * JB, JB)
            dve.wait_ge(zd_in, i * 32 + 16 * (h + 1))
            for f in range(KR):
                step(v.tensor_tensor_scan(Zd[:, :, f], ns[:, at], Zd[:, :, f], zlast[:, f:f + 1], ALU.mult, ALU.add))
            dve.wait_ge(g_in[h], i * (16 * JB) + 16 * JB)
            dve.wait_ge(s_out[h], i * 16)
            step.settle()
            step(v.tensor_copy(zlast[:, :], Zd[:, JB - 1, :]))
            v.tensor_tensor(S[h][:, :, 0:KR], G[h], Zd, ALU.mult).then_inc(prod, 1)
            dve.wait_ge(prod, b1)
            step.settle()
            v.tensor_reduce(lg[:, :, :], S[h][:, :, 0:KR].rearrange("p j (k r) -> p j k r", r=R), AX.X, ALU.add).then_inc(zd_free, 1)
            dve.wait_ge(zd_free, b1)
            for k in range(K):
                step(v.tensor_tensor_scan(mx[:, 1:JB + 1, k], negb[:, at], lg[:, :, k], mx[:, 0, k:k + 1], ALU.add, ALU.max))
            step.settle()
            step(v.tensor_tensor(d2[:, :, :], mx[:, 0:JB, :], mx[:, 1:JB + 1, :], ALU.subtract))
            step(v.tensor_tensor(d1[:, :, :], lg[:, :, :], mx[:, 1:JB + 1, :], ALU.subtract))
            step.settle()
            v.tensor_tensor(d2[:, :, :], d2[:, :, :], bc(negb[:, at].unsqueeze(2), [128, JB, K]), ALU.add).then_inc(e_diff, 1)
            dve.wait_ge(e_exp, b1)
            for k in range(K):
                step(v.tensor_tensor(S[h][:, :, k * R:(k + 1) * R], G[h][:, :, k * R:(k + 1) * R],
                                     bc(S[h][:, :, KR + k:KR + k + 1], [128, JB, R]), ALU.mult))
            step(v.tensor_copy(S[h][:, :, SK:SW], mx[:, 1:JB + 1, :]))
            step.settle()
            for f in range(SK):
                k = f // R if f < KR else f - KR
                if f == 0:
                    ins = v.tensor_tensor_scan(S[h][:, :, f], ea[:, :, k], S[h][:, :, f], slast[:, f:f + 1], ALU.mult, ALU.add)
                    ins.then_inc(g_free[h], 1)
                else:
                    step(v.tensor_tensor_scan(S[h][:, :, f], ea[:, :, k], S[h][:, :, f], slast[:, f:f + 1], ALU.mult, ALU.add))
            step(v.tensor_copy(mx[:, 0, :], mx[:, JB, :]))
            dve.wait_ge(g_free[h], i + 1)
            step.settle()
            v.tensor_copy(slast[:, :], S[h][:, JB - 1, 0:SK]).then_inc(s_ready, 1)
            dve.wait_ge(s_ready, b1)

        step(v.memset(mx[:, 0, :], 0.0))
        dve.wait_ge(zd_in, 16)
        dve.wait_ge(zfirst_in, 16)
        step(v.tensor_copy(Zd[:, 0, :], zlast[:, :]))
        step.settle()
        with dve.Fori(0, NB // 2) as i:
            step.enter(i, EDGE_STEPS)
            edges(i, 0)
            edges(i, 1)
            step.leave(NB // 2)

        dve.wait_ge(mo_ready, T)
        F_, L_, C_, SAME, GO = range(5)
        step(v.tensor_copy(row[0:1, F_, :], rowi[0:1, 0, :]))
        step(v.tensor_copy(row[0:1, L_, :], rowi[0:1, 1, :]))
        step(v.memset(row[0:1, C_, 0:1], 0.0))
        step(v.tensor_copy(fin[:, 0:SK], slast[:, :]))
        step(v.tensor_copy(fin[:, SK:SK + KR].rearrange("p (k r) -> p k r", r=R), bc(mx[:, 0, :].unsqueeze(2), [128, K, R])))
        step(v.tensor_copy(fin[:, SK + KR:2 * SK], mx[:, 0, :]))
        step.settle()
        v.memset(q[6][:, 0:1], 0.0).then_inc(fin_ready, 1)
        step(v.tensor_tensor(row[0:1, C_, 1:128], row[0:1, L_, 0:127], row[0:1, F_, 1:128], ALU.is_equal))
        step(v.tensor_tensor(row[0:1, SAME, :], row[0:1, F_, :], row[0:1, L_, :], ALU.is_equal))
        step.settle()
        step(v.memset(row[0:1, L_, 127:128], 0.0))
        step(v.tensor_tensor(row[0:1, GO, :], row[0:1, C_, :], row[0:1, SAME, :], ALU.mult))
        step(v.tensor_tensor(row[0:1, L_, 0:127], row[0:1, SAME, 0:127], row[0:1, C_, 1:128], ALU.mult))
        step(v.tensor_tensor(row[0:1, F_, :], row[0:1, F_, :], dump_row[0:1, :], ALU.subtract))
        step.settle()
        step(v.tensor_scalar(row[0:1, L_, :], row[0:1, L_, :], -1.0, 1.0, ALU.mult, ALU.add))
        step.settle()
        step(v.tensor_tensor(row[0:1, L_, :], row[0:1, L_, :], row[0:1, C_, :], ALU.mult))
        step.settle()
        step(v.tensor_tensor(row[0:1, F_, :], row[0:1, F_, :], row[0:1, L_, :], ALU.mult))
        step.settle()
        v.tensor_tensor(row[0:1, F_, :], row[0:1, F_, :], dump_row[0:1, :], ALU.add).then_inc(row_ready, 1)
        dve.wait_ge(row_psum, 1)
        step(v.tensor_copy(q[0][:, 0:128], ps[1][0:SK, 0:128]))
        v.tensor_copy(tgt[:, :], ps[2][:, 0:1]).then_inc(cr_ready, 1)
        dve.wait_ge(fin_psum, 1)
        step(v.tensor_copy(q[1][:, 0:128], ps[0][0:SK, 0:128]))
        step(v.tensor_copy(q[2][:, 0:128], ps[0][0:SK, 128:256]))
        step.settle()
        step(v.tensor_scalar(q[5][:, 0:128], q[0][:, 0:128], -1.0, BIG, ALU.add, ALU.mult))
        step(v.memset(q[6][:, 0:1], 0.0))
        step.settle()
        step(v.tensor_tensor_scan(q[6][:, 1:129], q[5][:, 0:128], q[2][:, 0:128], 0.0, ALU.add, ALU.max))
        step.settle()
        step(v.tensor_tensor(q[3][:, 0:128], q[6][:, 0:128], q[6][:, 1:129], ALU.subtract))
        step(v.tensor_tensor(q[4][:, 0:128], q[2][:, 0:128], q[6][:, 1:129], ALU.subtract))
        step.settle()
        v.tensor_tensor(q[3][:, 0:128], q[3][:, 0:128], q[5][:, 0:128], ALU.add).then_inc(q_ready, 1)
        dve.wait_ge(q_exp, 1)
        step(v.tensor_tensor(q[1][:, 0:128], q[1][:, 0:128], q[4][:, 0:128], ALU.mult))
        step(v.memset(q[2][:, 0:1], 0.0))
        step.settle()
        v.tensor_tensor_scan(q[2][:, 1:129], q[3][:, 0:128], q[1][:, 0:128], 0.0, ALU.mult, ALU.add).then_inc(cr_done, 1)

        dve.wait_ge(mo_ready, T)
        for g in range(NG):
            step(v.tensor_tensor(x_sb[0:P, g * GT:(g + 1) * GT, :].rearrange("p t d -> p (t d)"),
                                 x_sb[0:P, g * GT:(g + 1) * GT, :].rearrange("p t d -> p (t d)"), mix_sb[0:P, g, :], ALU.add))

        dve.wait_ge(ng_in, 16 * T)
        dve.wait_ge(xc_in, 2 * 16)
        step(v.tensor_tensor(nm[0:P, :, :], ng[0:P, :, SK:SW], xc[0:P, :, SK:SW], ALU.max))
        step.settle()
        step(v.tensor_tensor(nw1[0:P, :, :], ng[0:P, :, SK:SW], nm[0:P, :, :], ALU.subtract))
        step.settle()
        v.tensor_tensor(nw2[0:P, :, :], xc[0:P, :, SK:SW], nm[0:P, :, :], ALU.subtract).then_inc(merge_d, 1)
        dve.wait_ge(merge_e, 1)
        for k in range(K):
            for rows_, w_ in ((ng, nw1), (xc, nw2)):
                step(v.tensor_tensor(rows_[0:P, :, k * R:(k + 1) * R], rows_[0:P, :, k * R:(k + 1) * R],
                                     bc(w_[0:P, :, k:k + 1], [P, T, R]), ALU.mult))
        for rows_, w_ in ((ng, nw1), (xc, nw2)):
            step(v.tensor_tensor(rows_[0:P, :, KR:SK], rows_[0:P, :, KR:SK], w_[0:P, :, :], ALU.mult))
        step.settle()
        step(v.tensor_tensor(ng[0:P, :, 0:SK], ng[0:P, :, 0:SK], xc[0:P, :, 0:SK], ALU.add))
        step.settle()
        step(v.tensor_scalar(nden[0:P, :, :], ng[0:P, :, KR:SK], 1e-16, None, ALU.add))
        step.settle()
        step(v.reciprocal(nden[0:P, :, :], nden[0:P, :, :]))
        step.settle()
        step(v.tensor_tensor(nden[0:P, :, :], nden[0:P, :, :], bc(full[0:P, :].unsqueeze(2), [P, T, K]), ALU.mult))
        step.settle()
        for k in range(K):
            step(v.tensor_tensor(gx_agg[0:P, :, k * R:(k + 1) * R], ng[0:P, :, k * R:(k + 1) * R],
                                 bc(nden[0:P, :, k:k + 1], [P, T, R]), ALU.mult))
        step.settle()

        with dve.Fori(0, NG) as g:
            step.enter(g, TAIL_STEPS)
            dve.wait_ge(agg_psum, g)
            v.tensor_copy(agg_st[0:P, :, :], gx_agg[0:P, bass.ds(g * GT, GT), :]).then_inc(agg_ready, 1)
            for t in range(GT):
                xt = x_sb[0:P, g * GT + t, :]
                dve.wait_ge(y_psum, g * GT + (t + 1))
                v.scalar_tensor_tensor(acc[0:P, t % 2, :], ps[4 + t % 2][0:P, 0:D], -ETA_LAM, gx[0:P, g * GT + t, :],
                                       ALU.add, ALU.add).then_inc(y_used, 1)
                dve.wait_ge(y_used, g * GT + (t + 1))
                v.scalar_tensor_tensor(xt, acc[0:P, t % 2, :], 0.0, xt, ALU.max, ALU.add).then_inc(x2_ready, 1)
                dve.wait_ge(x2_ready, g * GT + (t + 1))
                held(nc.vector)
                step(v.bn_stats(st[0:P, t, :], xt))
            step.settle()
            held(nc.vector)
            for t in range(GT):
                if t < GT - 1:
                    step(v.bn_aggr(mv[0:P, t, :], st[0:P, t, :]))
                else:
                    v.bn_aggr(mv[0:P, t, :], st[0:P, t, :]).then_inc(stats2, 1)
            dve.wait_ge(stds2, g * 2 + 1)
            step(v.reciprocal(rstd[0:P, :], std[0:P, :]))
            step.settle()
            step(v.tensor_tensor(fac[0:P, :], rstd[0:P, :], rstd[0:P, :], ALU.mult))
            step.settle()
            v.tensor_tensor(fac[0:P, :], fac[0:P, :], mv[0:P, :, 1], ALU.mult).then_inc(r_read, 1)
            dve.wait_ge(stds2, g * 2 + 2)
            step(v.reciprocal(std2[0:P, :], std2[0:P, :]))
            step.settle()
            step(v.tensor_tensor(rstd[0:P, :], rstd[0:P, :], std2[0:P, :], ALU.mult))
            step.settle()
            for t in range(GT):
                v.tensor_scalar(stage[0:P, t, :], x_sb[0:P, g * GT + t, :], mv[0:P, t, 0:1], rstd[0:P, t:t + 1],
                                ALU.subtract, ALU.mult).then_inc(z_ready, 1)
            for t in range(GT):
                dve.wait_ge(zT_psum, g * GT + (t + 1))
                for k in (0, 1):
                    v.tensor_scalar(xT_st[:, k, t * P:(t + 1) * P], ps[6 + t % 2][:, k * P:(k + 1) * P],
                                    cols[:, GAM + k:GAM + k + 1], cols[:, BET + k:BET + k + 1], ALU.mult, ALU.add).then_inc(zT_ready, 1)
                dve.wait_ge(r_psum, g * GT + (t + 1))
                step(v.tensor_tensor(rl[0:P, t, :], ps[4 + t % 2][0:P, 256:256 + NX], brr[0:P, :], ALU.add))
            step.settle()
            held(nc.vector)
            for t in range(GT):
                step(v.max(r8[0:P, t, :], rl[0:P, t, :]))
            step.settle()
            held(nc.vector)
            for t in range(GT):
                step(v.max_index(ri[0:P, t, :], r8[0:P, t, :], rl[0:P, t, :]))
            step.settle()
            step(v.tensor_copy(rf[0:P, :, :], ri[0:P, :, 0:2]))
            v.tensor_tensor(rd[0:P, :, 0], r8[0:P, :, 1], r8[0:P, :, 0], ALU.subtract).then_inc(r_diff, 1)
            dve.wait_ge(r_exp, g + 1)
            step(v.tensor_scalar(rp[0:P, :, 0], rd[0:P, :, 1], 1.0, None, ALU.add))
            step.settle()
            step(v.reciprocal(rp[0:P, :, 0], rp[0:P, :, 0]))
            step.settle()
            step(v.tensor_tensor(rp[0:P, :, 1], rd[0:P, :, 1], rp[0:P, :, 0], ALU.mult))
            for w_, c in ((wf, 0), (wg, 1)):
                step(v.tensor_tensor(w_[0:P, :, :], bc(iota8[0:P, :].unsqueeze(1), [P, GT, NX]),
                                     bc(rf[0:P, :, c:c + 1], [P, GT, NX]), ALU.is_equal))
            step.settle()
            for w_, c in ((wf, 0), (wg, 1)):
                step(v.tensor_tensor(w_[0:P, :, :], w_[0:P, :, :], bc(rp[0:P, :, c:c + 1], [P, GT, NX]), ALU.mult))
            step.settle()
            v.tensor_tensor(wf[0:P, :, :], wf[0:P, :, :], wg[0:P, :, :], ALU.add).then_inc(wf_ready, 1)
            for t in range(GT):
                xt = x_sb[0:P, g * GT + t, :]
                dve.wait_ge(b2_psum, g * GT + (t + 1))
                v.tensor_tensor(xt, ps[4 + t % 2][0:P, 0:D], xt, ALU.add).then_inc(b2_used, 1)
            for e in range(NX):
                for t in range(GT):
                    xt = x_sb[0:P, g * GT + t, :]
                    n = e * GT + t + 1
                    dve.wait_ge(ye_psum, g * (NX * GT) + n)
                    if e:
                        dve.wait_ge(ye_used, g * (NX * GT) + (n - GT))
                    else:
                        dve.wait_ge(b2_used, g * GT + (t + 1))
                    v.scalar_tensor_tensor(xt, ps[4 + t % 2][0:P, 0:D], wf[0:P, t, e:e + 1], xt, ALU.mult, ALU.add).then_inc(ye_used, 1)
            dve.wait_ge(ye_used, g * (NX * GT) + NX * GT)
            step(v.tensor_copy(std2[0:1, 0:1], std[0:1, 0:1]))
            step.settle()
            v.tensor_copy(std2[0:1, 0:1], std[0:1, 0:1]).then_inc(out_ready, 1)
            step.leave(NG)

    @block.tensor
    def _(pe):
        mm, tr = nc.tensor.matmul, nc.tensor.transpose

        def x_tile(t, k):
            return xT_st[:, k, t * P:(t + 1) * P]

        pe.wait_ge(u_in, 2 * 16)
        pe.wait_ge(consts, 2)
        with pe.Fori(0, NG) as g:
            def project(t):
                pe.wait_ge(xT_ready, g * GT + (t + 1))
                pe.wait_ge(zu_ready, g * GT + (t - 1 if t >= 2 else 0))
                for k in (0, 1):
                    ins = mm(ps[2 + t % 2][0:P, 0:KR], x_tile(t, k), u_sb[:, k, :], start=k == 0, stop=k == 1)
                ins.then_inc(zu_psum, 1)

            for t in range(GT):
                pe.wait_ge(xn_ready, g * GT + (t + 1))
                pe.wait_ge(xT_ready, g * GT + (t - 1 if t >= 2 else 0))
                for k in (0, 1):
                    ins = tr(ps[t % 2][:, k * P:(k + 1) * P], stage[0:P, t, k * 128:(k + 1) * 128], ident[0:P, 0:P])
                ins.then_inc(xT_psum, 1)
                if t:
                    project(t - 1)
            project(GT - 1)

        pe.wait_ge(w_in, 16 * len(W_LOADS))
        pe.wait_ge(zu_ready, T)
        tr(ps[0][:, 0:NR], rows[:, :], ident[0:NR, 0:NR]).then_inc(rows_psum, 1)
        for dt_ in (0, 1):
            for ct in (0, 1):
                ins = tr(ps[1][:, dt_ * D + ct * 128:dt_ * D + (ct + 1) * 128], wq[:, ct, dt_ * 128:(dt_ + 1) * 128], ident[:, :])
        ins.then_inc(wqT_psum, 1)
        for r in (0, 1):
            for k in (0, 1):
                ins = mm(ps[2][:, r * D:(r + 1) * D], dm[:, k, r * 128:(r + 1) * 128], dm[:, k, :], start=k == 0, stop=k == 1)
        ins.then_inc(dtd_psum, 1)
        pe.wait_ge(dtd_ready, 1)
        for r in (0, 1):
            for k in (0, 1):
                ins = mm(ps[3][:, r * D:(r + 1) * D], dtd[:, k, r * 128:(r + 1) * 128], dm[:, k, :], start=k == 0, stop=k == 1)
        ins.then_inc(b_psum, 1)

        mm(ps[4][0:P, 0:T + 1], zero[:, 0:P], zero[:, 0:T + 1], start=True, stop=False, skip_group_check=True)
        with pe.Fori(0, NB // 2) as i:
            for h in (0, 1):
                pe.wait_ge(onehot, i * 4 + 2 * (h + 1))
                for j in range(JB):
                    ins = mm(ps[4][0:P, 0:T + 1], one_p[h][:, j, :], one_t[h][:, j, :], start=False, stop=False, skip_group_check=True)
                ins.then_inc(counted_block, 1)
        mm(ps[4][0:P, 0:T + 1], zero[:, 0:P], zero[:, 0:T + 1], start=False, stop=True, skip_group_check=True).then_inc(counted, 1)
        pe.wait_ge(counts_sb, 1)
        mm(ps[5][0:P, 0:1], tri[0:P, 0:P], csb[0:P, T:T + 1], start=True, stop=True).then_inc(based, 1)
        pe.wait_ge(gh_ready, 2)
        for k in (0, 1):
            ins = mm(ps[7][0:64, 0:D], u_sb[:, k, :], gh[:, k, :], start=k == 0, stop=k == 1)
        ins.then_inc(ug_psum, 1)
        pe.wait_ge(ug_ready, 1)

        pe.wait_ge(wkv_ready, 2)
        pe.wait_ge(cols_ready, 1)
        pe.wait_ge(wqT_ready, 1)
        for hg in (0, 1):
            mm(ps[6 + hg][:, 0:384], zero[:, 0:128], zero[:, 0:384], start=True, stop=False, skip_group_check=True)
        with pe.Fori(0, NG) as g:
            def product(t):
                pe.wait_ge(kv_ready, g * (3 * GT) + 3 * (t + 1))
                for hg in (0, 1):
                    v_ = vh[0:P, t % 4, hg * 128:(hg + 1) * 128]
                    mm(ps[6 + hg][:, 0:129], v_, kh[0:P, t % 4, hg, :], start=False, stop=False, skip_group_check=True)
                    ins = mm(ps[6 + hg][:, 256:384], ones[0:P, :], kh[0:P, t % 4, hg, 0:128], start=False, stop=False, skip_group_check=True)
                ins.then_inc(kv_used, 1)

            for t in range(GT):
                pe.wait_ge(kx_ready, g * GT + (t + 1))
                pe.wait_ge(kv_ready, g * (3 * GT) + (3 * (t - 1) if t >= 2 else 0))
                mm(ps[t % 2][0:P, :], ones[0:1, 0:P], kvb[0:1, :], start=True, stop=False)
                for k in (0, 1):
                    ins = mm(ps[t % 2][0:P, :], x_tile(t, k), wkv[:, k, :], start=False, stop=k == 1)
                ins.then_inc(kv_psum, 1)
                pe.wait_ge(gx_ready, g * GT + (t - 1 if t >= 2 else 0))
                for k in (0, 1):
                    ins = mm(ps[2 + t % 2][0:P, 0:D], x_tile(t, k), gh[:, k, :], start=k == 0, stop=k == 1)
                ins.then_inc(gx_psum, 1)
                if t:
                    product(t - 1)
            product(GT - 1)
        for hg in (0, 1):
            ins = mm(ps[6 + hg][:, 0:384], zero[:, 0:128], zero[:, 0:384], start=False, stop=True, skip_group_check=True)
        ins.then_inc(kv_summed, 1)

        pe.wait_ge(kvt_ready, 2)
        for hg in (0, 1):
            ins = mm(ps[4][:, hg * D:(hg + 1) * D], kvc[:, hg, :], w1[:, hg, :], start=True, stop=True)
        ins.then_inc(t1_psum, 1)
        pe.wait_ge(t1_ready, 1)
        for c in (0, 1):
            for k in (0, 1):
                ins = mm(ps[5][:, c * D:(c + 1) * D], wqT[:, k, c * 128:(c + 1) * 128], t1[:, k, :], start=k == 0, stop=k == 1)
        for m in (0, 1):
            for k in (0, 1):
                ins = mm(ps[4][:, m:m + 1], t1[:, k, m * 128:(m + 1) * 128], cols[:, BQ + k:BQ + k + 1], start=k == 0, stop=k == 1)
        ins.then_inc(we_psum, 1)

        pe.wait_ge(we_ready, 1)
        with pe.Fori(0, NG) as g:
            for m in (0, 1):
                for c, (lo, hi) in enumerate(CUTS):
                    pe.wait_ge(mh_ready, g * 4)
                    for k in (0, 1):
                        ins = mm(ps[2 * m + c][:, 0:hi - lo], weff[:, k, m * 128:(m + 1) * 128],
                                 xnT[:, g, :][:, k * GC + lo:k * GC + hi], start=k == 0, stop=k == 1)
                    ins.then_inc(mh_psum, 1)
            pe.wait_ge(mh_ready, g * 4 + 4)
            for t in range(GT):
                pe.wait_ge(mo_ready, g * GT + (t - 1 if t >= 2 else 0))
                mm(ps[4 + t % 2][0:P, 0:D], ones[0:1, 0:P], mb2[0:1, :], start=True, stop=False)
                for m in (0, 1):
                    ins = mm(ps[4 + t % 2][0:P, 0:D], mixh[:, m, t * P:(t + 1) * P], w2[:, m, :], start=False, stop=m == 1)
                ins.then_inc(mo_psum, 1)

        pe.wait_ge(mo_ready, T)
        pe.wait_ge(fin_ready, 1)
        tr(ps[0][0:SK, 0:128], fin[:, 0:SK], ident[:, :])
        tr(ps[0][0:SK, 128:256], fin[:, SK:2 * SK], ident[:, :]).then_inc(fin_psum, 1)
        pe.wait_ge(row_ready, 1)
        mm(ps[1][0:SK, 0:128], ones[0:1, 0:SK], row[0:1, 4, :], start=True, stop=True)
        mm(ps[2][:, 0:1], row[0:1, 0, :], ones[0:1, 0:1], start=True, stop=True).then_inc(row_psum, 1)
        pe.wait_ge(cr_done, 1)
        tr(ps[0][:, 0:SK], q[2][:, 0:128], ident[0:SK, 0:SK])
        tr(ps[1][:, 0:SK], q[6][:, 0:128], ident[0:SK, 0:SK]).then_inc(cr_psum, 1)

        pe.wait_ge(xw_in, 6 * 16)
        with pe.Fori(0, NG) as g:
            pe.wait_ge(ye_used, g * (NX * GT))
            pe.wait_ge(agg_ready, g + 1)
            mm(ps[6][0:64, 0:4], zero[:, 0:64], zero[:, 0:4], start=True, stop=True)
            for t in range(GT):
                ins = tr(ps[6 + t // 4][0:64, (t % 4) * P:(t % 4 + 1) * P], agg_st[0:P, t, :], ident[0:P, 0:P])
            ins.then_inc(agg_psum, 1)
            pe.wait_ge(aggT_ready, g + 1)
            for t in range(GT):
                pe.wait_ge(y_used, g * GT + (t - 1 if t >= 2 else 0))
                mm(ps[4 + t % 2][0:P, 0:D], aggT[:, t * P:(t + 1) * P], ug[:, :], start=True, stop=True).then_inc(y_psum, 1)
            pe.wait_ge(y_used, g * GT + GT)
            for t in range(GT):
                pe.wait_ge(z_ready, g * GT + (t + 1))
                pe.wait_ge(zT_ready, g * (2 * GT) + (2 * (t - 1) if t >= 2 else 0))
                for k in (0, 1):
                    ins = tr(ps[6 + t % 2][:, k * P:(k + 1) * P], stage[0:P, t, k * 128:(k + 1) * 128], ident[0:P, 0:P])
                ins.then_inc(zT_psum, 1)
                pe.wait_ge(zT_ready, g * (2 * GT) + 2 * (t + 1))
                for k in (0, 1):
                    ins = mm(ps[4 + t % 2][0:P, 256:256 + NX], x_tile(t, k), wr[:, k, :], start=k == 0, stop=k == 1)
                ins.then_inc(r_psum, 1)

            def up(e):
                for m in range(4):
                    for c, (lo, hi) in enumerate(CUTS):
                        n = 8 * e + 2 * m + c
                        pe.wait_ge(h_ready, g * (8 * NX) + max(0, n - 3))
                        for k in (0, 1):
                            ins = mm(ps[2 * (m % 2) + c][:, 0:hi - lo], W1[:, e, k, m * 128:(m + 1) * 128],
                                     xT_st[:, k, lo:hi], start=k == 0, stop=k == 1)
                        ins.then_inc(h_psum, 1)

            pe.wait_ge(wf_ready, g + 1)
            for t in range(GT):
                ins = tr(ps[6 + t // 4][0:NX, (t % 4) * P:(t % 4 + 1) * P], wf[0:P, t, :], ident[0:P, 0:P])
            ins.then_inc(wfT_psum, 1)
            pe.wait_ge(wfT_ready, g + 1)
            for t in range(GT):
                pe.wait_ge(b2_used, g * GT + (t - 1 if t >= 2 else 0))
                mm(ps[4 + t % 2][0:P, 0:D], wfT[:, t * P:(t + 1) * P], b2x[:, :], start=True, stop=True).then_inc(b2_psum, 1)
            pe.wait_ge(b2_used, g * GT + GT)
            up(0)
            for e in range(NX):
                if e < NX - 1:
                    up(e + 1)
                pe.wait_ge(h_ready, g * (8 * NX) + 8 * (e + 1))
                for t in range(GT):
                    n = e * GT + t
                    pe.wait_ge(ye_used, g * (NX * GT) + (n - 1 if n >= 2 and t >= 2 else max(0, n - (0 if t == 0 else 1))))
                    for m in range(4):
                        ins = mm(ps[4 + t % 2][0:P, 0:D], hid[e % 2][:, m, t * P:(t + 1) * P], W2[:, e, m, :],
                                 start=m == 0, stop=m == 3)
                    ins.then_inc(ye_psum, 1)


_INS = ['x', 'src', 'dst', 'L0_gnn_U', 'L0_gnn_Dmat', 'L0_gnn_head_w', 'L0_mix_w_qkv', 'L0_mix_b_qkv', 'L0_mix_kln_g',
        'L0_mix_kln_b', 'L0_mix_vln_g', 'L0_mix_vln_b', 'L0_mix_w1', 'L0_mix_b1', 'L0_mix_w2', 'L0_mix_b2',
        'L0_ffn_gamma', 'L0_ffn_beta', 'L0_ffn_Wr', 'L0_ffn_br', 'L0_ffn_W1', 'L0_ffn_b1', 'L0_ffn_W2', 'L0_ffn_b2']


def kernel(**inputs):
    import numpy as np
    import concourse.bacc as bacc
    from concourse import mybir as mb
    from concourse.bass_utils import run_bass_kernel_spmd

    nc = bacc.Bacc("TRN2", target_bir_lowering=False, num_devices=1)
    arrays, args = {}, {}
    for name in _INS:
        arr = np.ascontiguousarray(inputs[name])
        arrays[f"in_{name}"] = arr
        args[name] = nc.dram_tensor(f"in_{name}", arr.shape, mb.dt.from_np(arr.dtype), kind="ExternalInput").ap()
    out = nc.dram_tensor("out", (N, D), F32, kind="ExternalOutput").ap()
    program(nc, args, out)
    r = run_bass_kernel_spmd(nc, [arrays], core_ids=[0])
    return r.results[0]["out"]
```

```python
from contextlib import ExitStack

import concourse.bass as bass
from concourse import mybir

F32, I32, U32, BF16 = mybir.dt.float32, mybir.dt.int32, mybir.dt.uint32, mybir.dt.bfloat16
ALU = mybir.AluOpType
ACT = mybir.ActivationFunctionType
AX = mybir.AxisListType.X

N, D, E = 3125, 256, 53125
K, R = 4, 16
KR = K * R
HEADS, HC = 8, 32
NX, H = 8, 512
MIX_AT = 2
T, P = 25, 125
GT = 5
NG = T // GT
GC = GT * P
CUTS = ((0, 3 * P), (3 * P, GC))
EC = 416
EP = 128 * EC
JB = 26
JC = JB + 1
NB = EC // JB
GB = 4
NI = NB // GB
BX = 128
XB = (2 * N + NX * (BX - 1)) // BX
XQ = 4
XI = XB // XQ
assert XI * XQ == XB
TX = T * NX
SW = KR + 2 * K
SK = KR + K
LN_EPS, BIG = 1e-5, 1e30
ETA_LAM = 0.5 * 0.1
EDGE_STEPS = 9 * GB
TAIL_STEPS = 33
FULL = EC * 127


class Steps:

    def __init__(self, engine, sem):
        self.engine, self.sem, self.base, self.local = engine, sem, 0, 0
        self.reg, self.per = None, 0

    def __call__(self, instruction):
        instruction.then_inc(self.sem, 1)
        self.local += 1

    def value(self):
        if self.reg is None:
            return self.base + self.local
        return self.reg * self.per + (self.base + self.local)

    def settle(self):
        self.engine.wait_ge(self.sem, self.value())

    def enter(self, reg, per, first=0):
        self.base += self.local - first * per
        self.reg, self.per, self.local = reg, per, 0

    def leave(self, end):
        assert self.local == self.per, f"steps of a trip: {self.local}, not {self.per}"
        self.base += end * self.per
        self.reg, self.local = None, 0


def program(nc, a, out):
    zu_t = nc.dram_tensor("zu_t", (N, KR), F32, kind="Internal").ap()
    zd_t = nc.dram_tensor("zd_t", (EP + 128 * T, KR), F32, kind="Internal").ap()
    st_t = nc.dram_tensor("st_t", (EP, SW), F32, kind="Internal").ap()
    xt_t = nc.dram_tensor("xt_t", (N + 128, SW), F32, kind="Internal").ap()
    z_t = nc.dram_tensor("z_t", (N, D), F32, kind="Internal").ap()
    with ExitStack() as ctx:
        build(nc, ctx, a, out, zu_t, zd_t, st_t, xt_t, z_t)


def build(nc, ctx, a, out, zu_t, zd_t, st_t, xt_t, z_t):
    def sb(name, shape, dt=F32):
        return ctx.enter_context(nc.sbuf_tensor(name, shape, dt))

    def sem(name):
        return ctx.enter_context(nc.semaphore(name))

    def cutter(ap):
        at = [0]

        def take(*shape, dt=F32, rows=128):
            size = 1
            for n in shape:
                size *= n
            size = size // 2 if dt is BF16 else size
            view = ap[0:rows, at[0]:at[0] + size]
            at[0] += size
            assert at[0] <= ap.shape[1], (at[0], ap.shape)
            if dt is not F32:
                view = view.bitcast(dt)
            if len(shape) == 2:
                view = view.rearrange("p (a b) -> p a b", a=shape[0])
            if len(shape) == 3:
                view = view.rearrange("p (a b c) -> p a b c", a=shape[0], b=shape[1])
            return view
        return take

    x_sb = sb("x_sb", [128, T, D])
    xnT = sb("xnT", [128, NG, GT * D])
    mix_sb = xnT
    gx = sb("gx", [128, T, D])
    xn_flat = xnT[:, :, :].rearrange("p g c -> p (g c)")
    gx_flat = gx[:, :, :].rearrange("p t d -> p (t d)")
    edge = sb("edge", [128, GB * JB * KR + JB * KR + 2 * JC * KR + 2 * JC * SK + 2 * JB * SW])
    take = cutter(edge)
    G = [take(JB, KR) for _ in range(GB)]
    zraw = take(JB, KR)
    zt, keep = take(KR, JC), take(KR, JC)
    wt, decay = take(SK, JC), take(SK, JC)
    so = [take(JB, SW) for _ in (0, 1)]
    zt_f, keep_f, wt_f, decay_f = (v.rearrange("p f j -> p (f j)") for v in (zt, keep, wt, decay))
    take = cutter(edge[:, GB * JB * KR + JB * KR:])
    one_p = [take(JB, P, dt=BF16) for _ in (0, 1)]
    one_t = [take(JB, T + 1, dt=BF16) for _ in (0, 1)]
    take = cutter(edge)
    W1, W2 = take(NX, 2, H), take(NX, 4, D)
    stage = sb("stage", [128, GT, D])
    stage_flat = stage[:, :, :].rearrange("p a c -> p (a c)")
    xT_st = sb("xT_st", [128, 2, GC])
    xT_flat = xT_st[:, :, :].rearrange("p a c -> p (a c)")
    pools = sb("pools", [128, 4128])
    take = cutter(pools[:, 0:2072])
    kh, vh = take(4, 2, 129), take(4, D)
    mixh = pools[:, 0:2 * GC].rearrange("p (m c) -> p m c", m=2)
    ng = pools[:, 0:T * SW].rearrange("p (t f) -> p t f", f=SW)
    take = cutter(pools[:, 1032:2072])
    dm, wq = take(2, D), take(2, D)
    take = cutter(pools[:, 2072:])
    zu_sb = take(T, KR)
    take = cutter(pools[:, 2072:])
    xc = take(T, SW)
    kvs, sk = take(128), take(128)
    row = pools[0:1, 2072:2072 + 5 * 128].rearrange("p (r c) -> p r c", r=5)
    b1row = pools[:, 0:NX * H].rearrange("p (e m) -> p e m", e=NX)
    take = cutter(stage_flat)
    sq = take(2, 2 * D)
    take = cutter(stage_flat)
    kva, kvc, t1 = take(2, 129), take(2, 128), take(2, D)
    take = cutter(stage_flat)
    fin, carry = take(2 * SK), take(SW)
    q = [take(129, rows=SK) for _ in range(7)]
    take = cutter(xT_flat)
    nm, nw1, nw2, nden = (take(T, K) for _ in range(4))
    src_ix, dst_ix = sb("src_ix", [128, EC], I32), sb("dst_ix", [128, EC], I32)
    idxst = [sb(f"idxst{h}", [128, JB], I32) for h in range(GB)]
    ns, negb = sb("ns", [128, EC]), sb("negb", [128, EC])
    take = cutter(gx_flat)
    dstf, dq, dr, df, dfi = take(EC), take(EC), take(EC), take(EC), take(EC, dt=I32)
    iota_p, iota_t, dtd = take(P), take(T + 1), take(2, D)
    zeros = take(JB * KR)
    ident, ones, zero = sb("ident", [128, 128]), sb("ones", [128, 128]), sb("zero", [128, 384])
    blockd, tri = sb("blockd", [128, 128]), sb("tri", [128, 128])
    eps, steps_b = sb("eps", [128, 1]), sb("steps_b", [128, T])
    st, mv = sb("st", [128, GT, 6]), sb("mv", [128, GT, 2])
    std, rstd = sb("std", [128, GT]), sb("rstd", [128, GT])
    std2, fac = sb("std2", [128, GT]), sb("fac", [128, GT])
    NR = 10
    rows, cols = sb("rows", [NR, 128]), sb("cols", [128, NR])
    MB1, BQ, GAM, BET, VG, VB = 0, 2, 4, 6, 8, 9
    wqT = sb("wqT", [128, 2, D])
    wkv = sb("wkv", [128, 2, 2 * D])
    cm = sb("cm", [128, 32])
    w1, w2 = sb("w1", [128, 2, D]), sb("w2", [128, 2, D])
    lines = sb("lines", [128, 2 * D + 16])
    rowi = lines[0:1, 0:256].bitcast(I32).rearrange("p (r c) -> p r c", r=2)
    dump_row = lines[0:1, 256:384]
    kvb, cmb, mb2 = lines[32:33, 0:2 * D], lines[32:33, 2 * D:2 * D + 16], lines[64:65, 0:D]
    gh = sb("gh", [128, 2, D])
    u_sb, ug = sb("u_sb", [128, 2, KR]), sb("ug", [64, D])
    hw, hwo, hws = sb("hw", [64, K]), sb("hwo", [64, 1]), sb("hws", [64, 4])
    kgr, kbr = sb("kgr", [128, 128]), sb("kbr", [128, 128])
    wr, brr = sb("wr", [128, 2, NX]), sb("brr", [128, NX])
    csb, ends = sb("csb", [128, T + 1]), sb("ends", [128, T])
    start, full, nid = sb("start", [128, T]), sb("full", [128, T]), sb("nid", [128, T])
    tmpn = sb("tmpn", [128, T])
    sidx, gidx = sb("sidx", [128, T], I32), sb("gidx", [128, T], I32)
    kss, kstd, krs = sb("kss", [128, 2, 16]), sb("kstd", [128, 2, 16]), sb("krs", [128, 2, 16])
    weff, beff = w1, sb("beff", [128, 2])
    zlast = sb("zlast", [128, KR])
    take = cutter(wkv[:, :, :].rearrange("p k c -> p (k c)"))
    lg, mx, negx = (take(K, JC) for _ in range(3))
    lg_f, mx_f, negx_f = (v.rearrange("p k j -> p (k j)") for v in (lg, mx, negx))
    d1, d2 = take(K, JB), take(K, JB)
    rl, r8, ri = take(GT, NX), take(GT, 8), take(GT, 8, dt=U32)
    rf, rd, rp = take(T, 2), take(GT, 2), take(T, 2)
    tgt = sb("tgt", [128, 1], I32)
    take = cutter(xn_flat)
    gx_agg, acc, agg_st = take(T, KR), take(2, D), take(GT, KR)
    aggT = take(GC, rows=64)
    iota8 = sb("iota8", [128, NX])
    iota_lo, iota_b = sb("iota_lo", [128, BX]), sb("iota_b", [128, XB])
    nid1, dump = sb("nid1", [128, T]), sb("dump", [128, 1])
    take = cutter(xn_flat)
    ch0, ch1, chs, tot, rank, excl = (take(NX, T) for _ in range(6))
    slot, shi, slo, sfx = (take(2, T) for _ in range(4))
    sint = take(2, T, dt=I32)
    nblk, bend, bstart = take(NX), take(NX), take(NX)
    cmpb, cmpx = take(NX, T), take(XB, NX)
    b2row = take(NX, D)
    take = cutter(gx_flat)
    CH = 2 * GT
    oh_lo, oh_v = [], []
    for _ in (0, 1):
        oh_lo.append(take(2, GT, BX))
        oh_v.append(take(2, GT, 2 * XB))
    take = cutter(wqT[:, :, :].rearrange("p k c -> p (k c)"))
    sid, sw, sfill, spos = take(XB), take(XB), take(XB), take(XB)
    gix, six, eix = take(XB + XQ, dt=I32), take(XB, dt=I32), take(XB, dt=I32)
    gst = [sb(f"gst{h}", [128, 1], I32) for h in range(XQ)]
    sst = [sb(f"sst{h}", [128, 1], I32) for h in range(XQ)]
    take = cutter(gx_flat)
    xg, xb = [take(D) for _ in range(XQ)], [take(2, BX) for _ in (0, 1)]
    hb, hT = [take(H) for _ in (0, 1)], [take(4, BX) for _ in (0, 1)]
    yb = [take(D) for _ in range(XQ)]

    ps = [ctx.enter_context(nc.psum_tensor(f"ps{i}", [128, 512], F32)) for i in range(8)]

    yb_step = sem("yb_step")
    gx_agg_ready = sem("gx_agg_ready")
    zfirst_in = sem("zfirst_in")
    prod, kr_step, counted_block, y_used, cr_done, kv_summed = (
        sem("prod"), sem("kr_step"), sem("counted_block"), sem("y_used"), sem("cr_done"), sem("kv_summed"))
    x_in, u_in, edges_in, w_in, xw_in = sem("x_in"), sem("u_in"), sem("edges_in"), sem("w_in"), sem("xw_in")
    consts = sem("consts")
    pool_step, dve_step, act_step = sem("pool_step"), sem("dve_step"), sem("act_step")
    stats, stds = sem("stats"), sem("stds")
    xn_ready, xT_psum, xT_ready = sem("xn_ready"), sem("xT_psum"), sem("xT_ready")
    zu_psum, zu_ready, zu_stored = sem("zu_psum"), sem("zu_ready"), sem("zu_stored")
    zeroed, zeros_out = sem("zeroed"), sem("zeros_out")
    onehot, counted, counts_sb, based = sem("onehot"), sem("counted"), sem("counts_sb"), sem("based")
    places = sem("places")
    rows_psum, cols_ready = sem("rows_psum"), sem("cols_ready")
    wqT_psum, wqT_ready, dtd_psum, dtd_ready = sem("wqT_psum"), sem("wqT_ready"), sem("dtd_psum"), sem("dtd_ready")
    b_psum, gh_ready, ug_psum, hw_ready, hwe_ready, ug_ready = (
        sem("b_psum"), sem("gh_ready"), sem("ug_psum"), sem("hw_ready"), sem("hwe_ready"), sem("ug_ready"))
    wkv_ready = sem("wkv_ready")
    kx_ready, kv_psum, gx_psum, gx_ready = sem("kx_ready"), sem("kv_psum"), sem("gx_psum"), sem("gx_ready")
    sq_ready, ss_ready, ks_ready, kv_ready, kv_used = (
        sem("sq_ready"), sem("ss_ready"), sem("ks_ready"), sem("kv_ready"), sem("kv_used"))
    kvt_ready, t1_psum, t1_ready, we_psum, we_ready = (
        sem("kvt_ready"), sem("t1_psum"), sem("t1_ready"), sem("we_psum"), sem("we_ready"))
    mh_psum, mh_ready, mo_psum, mo_ready = sem("mh_psum"), sem("mh_ready"), sem("mo_psum"), sem("mo_ready")
    zd_scattered, zd_in, zraw_free = sem("zd_scattered"), sem("zd_in"), sem("zraw_free")
    g_in, g_free = [sem(f"g_in{h}") for h in range(GB)], [sem(f"g_free{h}") for h in range(GB)]
    fill_init, fill_ready, e_diff, e_exp = sem("fill_init"), sem("fill_ready"), sem("e_diff"), sem("e_exp")
    summed, so_ready, s_out = sem("summed"), sem("so_ready"), [sem("s_out0"), sem("s_out1")]
    fin_ready, fin_psum, q_ready, q_exp, cr_ready, cr_psum, cr_sb, cr_out = (
        sem("fin_ready"), sem("fin_psum"), sem("q_ready"), sem("q_exp"), sem("cr_ready"), sem("cr_psum"),
        sem("cr_sb"), sem("cr_out"))
    row_ready, row_psum, xt_init_ready, xt_init = sem("row_ready"), sem("row_psum"), sem("xt_init_ready"), sem("xt_init")
    ng_in, xc_in, merge_d, merge_e = sem("ng_in"), sem("xc_in"), sem("merge_d"), sem("merge_e")
    agg_ready, agg_psum, aggT_ready, y_psum, x2_ready = (
        sem("agg_ready"), sem("agg_psum"), sem("aggT_ready"), sem("y_psum"), sem("x2_ready"))
    stats2, stds2, z_ready, zT_psum, zT_ready = sem("stats2"), sem("stds2"), sem("z_ready"), sem("zT_psum"), sem("zT_ready")
    z_out, x2_out = sem("z_out"), sem("x2_out")
    r_psum, r_read, r_diff, r_exp = sem("r_psum"), sem("r_read"), sem("r_diff"), sem("r_exp")
    nodes_done, b1_in, b2_in = sem("nodes_done"), sem("b1_in"), sem("b2_in")
    choices, ranked_psum, oh_ready, oh_used, slots_psum, slots_ready = (
        sem("choices"), sem("ranked_psum"), sem("oh_ready"), sem("oh_used"), sem("slots_psum"), sem("slots_ready"))
    xg_in = [sem(f"xg_in{h}") for h in range(XQ)]
    xg_psum, xb_ready, h_psum, hb_ready, hg_ready, hT_psum, hT_ready, ye_psum, yb_ready, added = (
        sem("xg_psum"), sem("xb_ready"), sem("h_psum"), sem("hb_ready"), sem("hg_ready"), sem("hT_psum"),
        sem("hT_ready"), sem("ye_psum"), sem("yb_ready"), sem("added"))

    x_v = a["x"].rearrange("(p t) d -> p t d", t=T)
    out_v = out[0:N, :].rearrange("(p t) d -> p t d", t=T)
    z_v = z_t.rearrange("(p t) d -> p t d", t=T)
    zu_v = zu_t.rearrange("(p t) f -> p t f", t=T)
    zd_v = zd_t[0:EP, :].rearrange("(p j) f -> p j f", j=EC)
    st_v = st_t.rearrange("(p j) f -> p j f", j=EC)
    xt_v = xt_t[0:N, :].rearrange("(p t) f -> p t f", t=T)
    w_qkv = a["L0_mix_w_qkv"].rearrange("(k c) (h m) -> k c h m", k=2, m=3 * HC)
    b_qkv = a["L0_mix_b_qkv"].rearrange("(a h m) -> a h m", a=1, m=3 * HC)
    XL = 2 * NG * 16
    SPLIT = ((0, 112), (112, P))

    spare = {name: sb(f"spare_{name}", [128, 1]) for name in ("dve", "pool")}

    def held(engine):
        if engine is nc.vector:
            nc.vector.memset(spare["dve"][:, :], 0.0)
        else:
            nc.gpsimd.tensor_tensor(spare["pool"][:, :], eps[:, :], eps[:, :], ALU.add)

    block = ctx.enter_context(nc.Block())

    @block.sync
    def _(sp):
        for g in range(NG):
            for lo, hi in SPLIT:
                sp.dma_start(x_sb[lo:hi, g * GT:(g + 1) * GT, :], x_v[lo:hi, g * GT:(g + 1) * GT, :]).then_inc(x_in, 16)
        for k in range(2):
            sp.dma_start(u_sb[:, k, :].rearrange("c (h r) -> c h r", h=K),
                         a["L0_gnn_U"][:, k * 128:(k + 1) * 128, :].rearrange("h c r -> c h r")).then_inc(u_in, 16)
        sp.wait_ge(zeroed, 1)
        for b in range(NB):
            sp.dma_start(zd_v[:, b * JB:(b + 1) * JB, :], zeros.rearrange("p (j f) -> p j f", f=KR)).then_inc(zeros_out, 16)
        sp.wait_ge(zu_ready, T)
        for lo, hi in SPLIT:
            sp.dma_start(zu_v[lo:hi, :, :], zu_sb[lo:hi, :, :]).then_inc(zu_stored, 16)
        sp.wait_ge(xt_init_ready, 2)
        for lo, hi in SPLIT:
            sp.dma_start(xt_v[lo:hi, :, :], xc[lo:hi, :, :]).then_inc(xt_init, 16)
        sp.wait_ge(zd_scattered, 16 * T)
        sp.wait_ge(fill_init, 1)
        sp.dma_start(zraw, zd_v[:, 0:JB, :]).then_inc(zd_in, 16)

        def block_io(i, h, load):
            if load:
                sp.wait_ge(zraw_free, i * GB + (h + 1))
                sp.dma_start(zraw, zd_v[:, bass.ds(i * (GB * JB) + (h + 1) * JB, JB), :]).then_inc(zd_in, 16)
            sp.wait_ge(so_ready, i * GB + (h + 1))
            sp.dma_start(st_v[:, bass.ds(i * (GB * JB) + h * JB, JB), :], so[h % 2]).then_inc(s_out[h % 2], 16)

        with sp.Fori(0, NI - 1) as i:
            for h in range(GB):
                block_io(i, h, True)
        for h in range(GB):
            block_io(NI - 1, h, h < GB - 1)
        sp.wait_ge(s_out[0], 16 * NB // 2)
        sp.wait_ge(s_out[1], 16 * NB // 2)
        sp.wait_ge(fin_ready, 1)
        for k in range(2):
            sp.dma_start(W1[:, :, k, :], a["L0_ffn_W1"][:, k * 128:(k + 1) * 128, :].rearrange("e c m -> c e m")).then_inc(xw_in, 16)
        for k in range(4):
            sp.dma_start(W2[:, :, k, :], a["L0_ffn_W2"][:, k * 128:(k + 1) * 128, :].rearrange("e c m -> c e m")).then_inc(xw_in, 16)
        sp.wait_ge(cr_out, 16)
        for lo, hi in SPLIT:
            sp.dma_start(xc[lo:hi, :, :], xt_v[lo:hi, :, :]).then_inc(xc_in, 16)
        sp.wait_ge(gx_agg_ready, K)
        sp.dma_start(b1row, a["L0_ffn_b1"].partition_broadcast(128)).then_inc(b1_in, 16)
        with sp.Fori(0, NG) as g:
            sp.wait_ge(z_ready, g * GT + GT)
            for lo, hi in SPLIT:
                sp.dma_start(z_v[lo:hi, bass.ds(g * GT, GT), :], stage[lo:hi, :, :]).then_inc(z_out, 16)
            for lo, hi in SPLIT:
                sp.dma_start(out_v[lo:hi, bass.ds(g * GT, GT), :], x_sb[lo:hi, bass.ds(g * GT, GT), :]).then_inc(x2_out, 16)
        sp.wait_ge(nodes_done, 1)
        sp.dma_start(b2row, a["L0_ffn_b2"].partition_broadcast(128)).then_inc(b2_in, 16)
        sp.wait_ge(x2_out, 2 * 16 * NG)
        sp.wait_ge(added, 16 * XB)

    W_LOADS = []

    def zu_copy(act, g, t):
        act.wait_ge(zu_psum, g * GT + (t + 1))
        nc.scalar.copy(zu_sb[0:P, g * GT + t, :], ps[2 + t % 2][0:P, 0:KR]).then_inc(zu_ready, 1)

    @block.scalar
    def _(act):
        def load(dst, src, s=w_in):
            act.dma_start(dst, src).then_inc(s, 16)
            if s is w_in:
                W_LOADS.append(1)

        act.wait_ge(consts, 1)
        load(dst_ix[0:112, :], a["dst"][0:112 * EC].rearrange("(p j) -> p j", j=EC), edges_in)
        load(dst_ix[112:127, :], a["dst"][112 * EC:FULL].rearrange("(p j) -> p j", j=EC), edges_in)

        load(dst_ix[127:128, 0:E - FULL], a["dst"][FULL:E].rearrange("(p j) -> p j", p=1), edges_in)
        load(src_ix[0:112, :], a["src"][0:112 * EC].rearrange("(p j) -> p j", j=EC), edges_in)
        load(src_ix[112:127, :], a["src"][112 * EC:FULL].rearrange("(p j) -> p j", j=EC), edges_in)
        load(src_ix[127:128, 0:E - FULL], a["src"][FULL:E].rearrange("(p j) -> p j", p=1), edges_in)
        with nc.allow_non_contiguous_dma(reason="first and last dst of each partition: 255 words"):
            load(rowi[0:1, 0, :], a["dst"][0:1 + 127 * EC:EC].rearrange("(p j) -> p j", p=1), edges_in)
            load(rowi[0:1, 1, 0:127], a["dst"][EC - 1:FULL:EC].rearrange("(p j) -> p j", p=1), edges_in)
        for k in range(2):
            load(dm[:, k, :], a["L0_gnn_Dmat"][k * 128:(k + 1) * 128, :])
            load(wq[:, k, :].rearrange("c (h m) -> c h m", m=HC), w_qkv[k, :, :, 0:HC])
            for part in (0, 1):
                load(wkv[:, k, part * D:(part + 1) * D].rearrange("c (h m) -> c h m", m=HC),
                     w_qkv[k, :, :, (part + 1) * HC:(part + 2) * HC])
            load(w1[:, k, :], a["L0_mix_w1"][k * 128:(k + 1) * 128, :])
            load(w2[:, k, :], a["L0_mix_w2"][k * 128:(k + 1) * 128, :])
            load(wr[:, k, :], a["L0_ffn_Wr"][k * 128:(k + 1) * 128, :])
        for part in (0, 1):
            load(kvb[:, part * D:(part + 1) * D].rearrange("a (h m) -> a h m", m=HC),
                 b_qkv[:, :, (part + 1) * HC:(part + 2) * HC])
        load(rows[MB1:MB1 + 2, :], a["L0_mix_b1"].rearrange("(m p) -> m p", p=128))
        for k in range(2):
            load(rows[BQ + k:BQ + k + 1, :].rearrange("a (h m) -> a h m", m=HC), b_qkv[:, 4 * k:4 * k + 4, 0:HC])
        load(rows[GAM:GAM + 2, :], a["L0_ffn_gamma"].rearrange("(m p) -> m p", p=128))
        load(rows[BET:BET + 2, :], a["L0_ffn_beta"].rearrange("(m p) -> m p", p=128))
        for r in range(4):
            load(rows[VG:VG + 1, r * HC:(r + 1) * HC], a["L0_mix_vln_g"].rearrange("(a m) -> a m", a=1))
            load(rows[VB:VB + 1, r * HC:(r + 1) * HC], a["L0_mix_vln_b"].rearrange("(a m) -> a m", a=1))
            load(kgr[:, r * HC:(r + 1) * HC], a["L0_mix_kln_g"].partition_broadcast(128))
            load(kbr[:, r * HC:(r + 1) * HC], a["L0_mix_kln_b"].partition_broadcast(128))
        load(mb2, a["L0_mix_b2"].rearrange("(a m) -> a m", a=1))
        load(brr[:, :], a["L0_ffn_br"].partition_broadcast(128))
        load(hw[:, :], a["L0_gnn_head_w"].partition_broadcast(64))
        for k in range(K):
            load(hwo[k * R:(k + 1) * R, :], a["L0_gnn_head_w"][k:k + 1].partition_broadcast(R))

        act.wait_ge(consts, 2)
        with act.Fori(0, NG) as g:
            act.wait_ge(stats, g + 1)
            nc.scalar.activation(std[0:P, :], mv[0:P, :, 1], ACT.Sqrt, bias=eps[0:P, :]).then_inc(stds, 1)
            act.wait_ge(zu_psum, g * GT)
            for t in range(GT):
                act.wait_ge(xT_psum, g * GT + (t + 1))
                src = ps[t % 2][:, 0:2 * P].rearrange("p (k c) -> p k c", k=2)
                nc.scalar.copy(xT_st[:, :, t * P:(t + 1) * P], src)
                nc.scalar.copy(xnT[:, g, :][:, 0:2 * GC].rearrange("p (k c) -> p k c", k=2)[:, :, t * P:(t + 1) * P],
                               src).then_inc(xT_ready, 1)
                if t:
                    zu_copy(act, g, t - 1)
            zu_copy(act, g, GT - 1)

        act.wait_ge(rows_psum, 1)
        nc.scalar.copy(cols[:, :], ps[0][:, 0:NR]).then_inc(cols_ready, 1)
        act.wait_ge(wqT_psum, 1)
        nc.scalar.copy(wqT[:, :, :], ps[1][:, :].rearrange("p (k c) -> p k c", k=2)).then_inc(wqT_ready, 1)
        act.wait_ge(dtd_psum, 1)
        nc.scalar.copy(dtd, ps[2][:, :].rearrange("p (k c) -> p k c", k=2)).then_inc(dtd_ready, 1)
        act.wait_ge(hw_ready, 1)
        nc.scalar.activation(hws[:, 0:1], hwo[:, :], ACT.Exp, bias=hws[:, 3:4])
        nc.scalar.activation(hw[:, :], hw[:, :], ACT.Exp, bias=hws[:, 3:4], accum_out=hws[:, 1:2]).then_inc(hwe_ready, 1)

        act.wait_ge(zeros_out, 16 * NB)
        act.wait_ge(counted, 1)
        act.wait_ge(based, 1)
        act.wait_ge(xn_ready, T)
        act.wait_ge(xT_psum, T)
        with act.Fori(0, NG) as g:
            for t in range(GT):
                act.wait_ge(gx_psum, g * GT)
                nc.scalar.copy(xT_st[:, :, t * P:(t + 1) * P],
                               xnT[:, g, :][:, 0:2 * GC].rearrange("p (k c) -> p k c", k=2)[:, :, t * P:(t + 1) * P]
                               ).then_inc(kx_ready, 1)
            for t in range(GT):
                act.wait_ge(kv_psum, g * GT + (t + 1))
                act.wait_ge(ss_ready, g * GT + (t - 1 if t >= 2 else 0))
                nc.scalar.square(sq[0:P, t % 2, :], ps[t % 2][0:P, :]).then_inc(sq_ready, 1)
                act.wait_ge(gx_psum, g * GT + (t + 1))
                nc.scalar.copy(gx[0:P, g * GT + t, :], ps[2 + t % 2][0:P, 0:D]).then_inc(gx_ready, 1)
                act.wait_ge(ss_ready, g * GT + (t + 1))
                nc.scalar.activation(kstd[0:P, t % 2, :], kss[0:P, t % 2, :], ACT.Sqrt,
                                     bias=eps[0:P, :], scale=1.0 / HC).then_inc(ks_ready, 1)

        act.wait_ge(t1_psum, 1)
        nc.scalar.copy(t1, ps[4][:, :].rearrange("p (k c) -> p k c", k=2)).then_inc(t1_ready, 1)

        def feature(ap):
            return ap.rearrange("p j f -> p f j")

        def fill(i, h):
            at = bass.ds(i * (GB * JB) + h * JB, JB)
            act.wait_ge(zd_in, i * (16 * GB) + 16 * (h + 1))
            nc.scalar.copy(zt[:, :, 1:JC], feature(zraw)).then_inc(zraw_free, 1)
            nc.scalar.copy(keep[:, :, 1:JC], ns[:, at].unsqueeze(1).broadcast_to([128, KR, JB]))
            nc.scalar.copy(negx[:, :, 1:JC], negb[:, at].unsqueeze(1).broadcast_to([128, K, JB])).then_inc(fill_ready, 1)

        def exps(i, h):
            act.wait_ge(e_diff, i * GB + (h + 1))
            nc.scalar.activation(wt[:, KR:SK, 1:JC], d1[:, :, :], ACT.Exp, scale=0.25)
            nc.scalar.activation(decay[:, 0:KR, 1:JC].rearrange("p (k r) j -> p k r j", k=K),
                                 d2[:, :, :].unsqueeze(2).broadcast_to([128, K, R, JB]), ACT.Exp, scale=0.25)
            nc.scalar.activation(decay[:, KR:SK, 1:JC], d2[:, :, :], ACT.Exp, scale=0.25).then_inc(e_exp, 1)

        def sums_out(i, h):
            act.wait_ge(summed, i * GB + (h + 1))
            act.wait_ge(s_out[h % 2], i * (8 * GB) + 16 * (h // 2))
            nc.scalar.copy(feature(so[h % 2][:, :, 0:SK]), wt[:, :, 1:JC])
            nc.scalar.copy(feature(so[h % 2][:, :, SK:SW]), mx[:, :, 1:JC]).then_inc(so_ready, 1)

        def edge_block(i, h, more=True):
            exps(i, h)
            if more:
                fill(i, h + 1)
            sums_out(i, h)

        act.wait_ge(fill_init, 1)
        act.wait_ge(zfirst_in, 16)
        act.wait_ge(zd_in, 16)
        nc.scalar.copy(zraw[:, 0, :], zlast[:, :]).then_inc(act_step, 1)
        act.wait_ge(act_step, 1)
        fill(0, 0)
        with act.Fori(0, MIX_AT) as i:
            for h in range(GB):
                edge_block(i, h)
        act.wait_ge(we_ready, 1)
        with act.Fori(0, NG) as g:
            act.wait_ge(mo_psum, g * GT)
            for m in range(2):
                for c, (lo, hi) in enumerate(CUTS):
                    act.wait_ge(mh_psum, g * 4 + (2 * m + c + 1))
                    nc.scalar.activation(mixh[:, m, lo:hi], ps[2 * m + c][:, 0:hi - lo], ACT.Gelu,
                                         bias=beff[:, m:m + 1]).then_inc(mh_ready, 1)
            for t in range(GT):
                act.wait_ge(mo_psum, g * GT + (t + 1))
                nc.scalar.copy(mix_sb[0:P, g, t * D:(t + 1) * D], ps[4 + t % 2][0:P, 0:D]).then_inc(mo_ready, 1)
        with act.Fori(MIX_AT, NI - 1) as i:
            for h in range(GB):
                edge_block(i, h)
        for h in range(GB):
            edge_block(NI - 1, h, h < GB - 1)

        act.wait_ge(q_ready, 1)
        nc.scalar.activation(q[3][:, 0:128], q[3][:, 0:128], ACT.Exp, scale=0.25)
        nc.scalar.activation(q[4][:, 0:128], q[4][:, 0:128], ACT.Exp, scale=0.25).then_inc(q_exp, 1)
        act.wait_ge(cr_psum, 1)
        nc.scalar.copy(carry[:, 0:SK], ps[0][:, 0:SK])
        nc.scalar.copy(carry[:, SK:SW], ps[1][:, KR:SK]).then_inc(cr_sb, 1)
        act.wait_ge(merge_d, 1)
        nc.scalar.activation(nw1[0:P, :, :], nw1[0:P, :, :], ACT.Exp, scale=0.25)
        nc.scalar.activation(nw2[0:P, :, :], nw2[0:P, :, :], ACT.Exp, scale=0.25).then_inc(merge_e, 1)

        act.wait_ge(cols_ready, 1)
        with act.Fori(0, NG) as g:
            act.wait_ge(agg_psum, g + 1)
            nc.scalar.copy(aggT[:, 0:4 * P], ps[6][0:64, 0:4 * P])
            nc.scalar.copy(aggT[:, 4 * P:GC], ps[7][0:64, 0:P]).then_inc(aggT_ready, 1)
            act.wait_ge(stats2, g + 1)
            nc.scalar.activation(std[0:P, :], mv[0:P, :, 1], ACT.Sqrt, bias=eps[0:P, :]).then_inc(stds2, 1)
            act.wait_ge(stats2, g + 1)
            act.wait_ge(r_read, g + 1)
            nc.scalar.activation(std2[0:P, :], fac[0:P, :], ACT.Sqrt, bias=eps[0:P, :]).then_inc(stds2, 1)
            act.wait_ge(r_diff, g + 1)
            nc.scalar.activation(rd[0:P, :, 1], rd[0:P, :, 0], ACT.Exp).then_inc(r_exp, 1)

        def hidden(i, h):
            act.wait_ge(hb_ready, i * XQ + (h + 1))
            nc.scalar.activation(hb[h % 2], hb[h % 2], ACT.Gelu).then_inc(hg_ready, 1)

        def hidden_T(i, h):
            act.wait_ge(hT_psum, i * XQ + (h + 1))
            nc.scalar.copy(hT[h % 2], ps[4 + h % 2][:, :].rearrange("p (m c) -> p m c", m=4)).then_inc(hT_ready, 1)

        hidden(0, 0)
        for h in range(1, XQ):
            hidden(0, h)
            hidden_T(0, h - 1)
        with act.Fori(1, XI) as i:
            for h in range(XQ):
                hidden(i, h)
                hidden_T(i, h - 1)
        hidden_T(XI - 1, XQ - 1)

    @block.gpsimd
    def _(pool):
        step = Steps(pool, pool_step)
        gp = nc.gpsimd
        step(gp.memset(dst_ix[:, :], N))
        step(gp.memset(src_ix[:, :], 0))
        step.settle()
        gp.memset(eps[:, :], LN_EPS).then_inc(consts, 1)
        step(gp.memset(ident[:, :], 0.0))
        gp.memset(zeros, 0.0).then_inc(zeroed, 1)
        step(gp.memset(ones[:, :], 1.0))
        step(gp.memset(zero[:, :], 0.0))
        step.settle()
        step(gp.affine_select(out=ident[:, :], in_=ident[:, :], compare_op=ALU.not_equal, fill=1.0, base=0,
                              pattern=[[-1, 128]], channel_multiplier=1))
        step(gp.affine_select(out=tri[:, :], in_=ones[:, :], compare_op=ALU.is_gt, fill=0.0, base=0,
                              pattern=[[1, 128]], channel_multiplier=-1))
        step(gp.memset(blockd[:, :], 0.0))
        step.settle()
        for b in range(4):
            step(gp.memset(blockd[b * HC:(b + 1) * HC, b * HC:(b + 1) * HC], 1.0 / N))
            step.settle()
        step(gp.iota(iota_p, [[1, P]], base=0, channel_multiplier=0, allow_small_or_imprecise_dtypes=True))
        step(gp.iota(iota_t, [[1, T + 1]], base=0, channel_multiplier=0, allow_small_or_imprecise_dtypes=True))
        step(gp.iota(steps_b[:, :], [[BX, T]], base=0, channel_multiplier=0, allow_small_or_imprecise_dtypes=True))
        step(gp.iota(iota8[:, :], [[1, NX]], base=0, channel_multiplier=0, allow_small_or_imprecise_dtypes=True))
        step(gp.iota(nid[:, :], [[1, T]], base=0, channel_multiplier=T, allow_small_or_imprecise_dtypes=True))
        step.settle()
        step(gp.iota(dump_row, [[1, 128]], base=N, channel_multiplier=0, allow_small_or_imprecise_dtypes=True))
        step.settle()
        step(gp.iota(sidx[:, :], [[1, T]], base=EP, channel_multiplier=T))
        step(gp.memset(gidx[:, :], 0))
        step.settle()
        step(gp.memset(zu_sb[96:128, :, :], 0.0))
        step.settle()
        step(gp.memset(rowi[0:1, 1, 127:128], N))
        step.settle()
        step(gp.iota(iota_lo[:, :], [[1, BX]], base=0, channel_multiplier=0, allow_small_or_imprecise_dtypes=True))
        step(gp.iota(iota_b[:, :], [[1, XB]], base=0, channel_multiplier=0, allow_small_or_imprecise_dtypes=True))
        step(gp.iota(nid1[:, :], [[1, T]], base=1, channel_multiplier=T, allow_small_or_imprecise_dtypes=True))
        step(gp.iota(dump[:, :], [[1, 1]], base=N, channel_multiplier=1, allow_small_or_imprecise_dtypes=True))
        step(gp.memset(kh[:, :, :, 128:129], 1.0))
        step.settle()
        gp.memset(hws[:, :], 0.0).then_inc(consts, 1)

        def gathers(i, h, first):
            if not first:
                pool.wait_ge(g_free[h], i)
            step(gp.tensor_copy(idxst[h][:, :], src_ix[:, bass.ds(i * (GB * JB) + h * JB, JB)]))
            step.settle()
            if not first:
                held(nc.gpsimd)
            for j in range(JB):
                gp.indirect_dma_start(G[h][:, j, :], None, zu_t,
                                      bass.IndirectOffsetOnAxis(ap=idxst[h][:, j:j + 1], axis=0)).then_inc(g_in[h], 16)

        pool.wait_ge(edges_in, 8 * 16)
        pool.wait_ge(zu_stored, 2 * 16)
        gp.indirect_dma_start(zlast[:, :], None, zu_t,
                              bass.IndirectOffsetOnAxis(ap=dst_ix[:, 0:1], axis=0)).then_inc(zfirst_in, 16)
        for h in range(GB - 1):
            gathers(0, h, True)
        pool.wait_ge(zeros_out, 16 * NB)
        pool.wait_ge(places, 1)
        for t in range(T):
            gp.indirect_dma_start(zd_t, bass.IndirectOffsetOnAxis(ap=sidx[:, t:t + 1], axis=0),
                                  zu_sb[:, t, :], None).then_inc(zd_scattered, 16)
        gathers(0, GB - 1, True)
        pool.wait_ge(zd_scattered, 16 * T)
        gp.memset(xc[:, :, 0:SK], 0.0).then_inc(xt_init_ready, 1)
        gp.memset(xc[:, :, SK:SW], -BIG).then_inc(xt_init_ready, 1)
        with pool.Fori(1, NI) as i:
            step.enter(i, GB, 1)
            for h in range(GB):
                gathers(i, h, False)
            step.leave(NI)
        pool.wait_ge(s_out[0], 16 * NB // 2)
        pool.wait_ge(s_out[1], 16 * NB // 2)
        pool.wait_ge(mo_ready, T)
        for t in range(T):
            gp.indirect_dma_start(ng[:, t, :], None, st_t,
                                  bass.IndirectOffsetOnAxis(ap=gidx[:, t:t + 1], axis=0)).then_inc(ng_in, 16)
        pool.wait_ge(xt_init, 2 * 16)
        pool.wait_ge(cr_sb, 1)
        pool.wait_ge(cr_ready, 1)
        gp.indirect_dma_start(xt_t, bass.IndirectOffsetOnAxis(ap=tgt[:, 0:1], axis=0), carry[:, :], None).then_inc(cr_out, 16)
        pool.wait_ge(cr_out, 16)

        def rows_in(i, h, first=False):
            if not first:
                pool.wait_ge(xg_psum, i * XQ + (h - XQ + 1))
            step(gp.tensor_copy(gst[h % XQ][:, :], gix[:, bass.ds(i * XQ + h, 1)]))
            step.settle()
            if not first:
                held(nc.gpsimd)
            gp.indirect_dma_start(xg[h % XQ], None, z_t,
                                  bass.IndirectOffsetOnAxis(ap=gst[h % XQ][:, 0:1], axis=0)).then_inc(xg_in[h % XQ], 16)

        def rows_out(i, h):
            step(gp.tensor_copy(sst[h][:, :], six[:, bass.ds(i * XQ + h, 1)]))
            step.settle()
            pool.wait_ge(yb_ready, i * XQ + (h + 1))
            pool.wait_ge(added, i * (16 * XQ) + 16 * h)
            held(nc.gpsimd)
            gp.indirect_dma_start(out, bass.IndirectOffsetOnAxis(ap=sst[h][:, 0:1], axis=0), yb[h], None,
                                  compute_op=ALU.add, bounds_check=N + 127).then_inc(added, 16)

        pool.wait_ge(slots_ready, 1)
        pool.wait_ge(z_out, 2 * 16 * NG)
        pool.wait_ge(x2_out, 2 * 16 * NG)
        for h in range(XQ):
            rows_in(0, h, True)
        with pool.Fori(0, XI) as i:
            step.enter(i, 2 * XQ)
            for h in range(XQ):
                rows_in(i, h + XQ)
                rows_out(i, h)
            step.leave(XI)
        for h in range(XQ):
            pool.wait_ge(xg_in[h], 16 * (XI + 1))
        pool.wait_ge(added, 16 * XB)

    @block.vector
    def _(dve):
        step = Steps(dve, dve_step)
        v = nc.vector

        def bc(ap, shape):
            return ap.broadcast_to(shape)

        dve.wait_ge(x_in, XL)
        dve.wait_ge(consts, 2)
        with dve.Fori(0, NG) as g:
            step.enter(g, 3 * GT)
            for t in range(GT):
                step(v.bn_stats(st[0:P, t, :], x_sb[0:P, g * GT + t, :]))
            step.settle()
            held(nc.vector)
            for t in range(GT):
                if t < GT - 1:
                    step(v.bn_aggr(mv[0:P, t, :], st[0:P, t, :]))
                else:
                    v.bn_aggr(mv[0:P, t, :], st[0:P, t, :]).then_inc(stats, 1)
            dve.wait_ge(stds, g + 1)
            step(v.reciprocal(rstd[0:P, :], std[0:P, :]))
            step.settle()
            dve.wait_ge(xT_psum, g * GT)
            for t in range(GT):
                v.tensor_scalar(stage[0:P, t, :], x_sb[0:P, g * GT + t, :], mv[0:P, t, 0:1], rstd[0:P, t:t + 1],
                                ALU.subtract, ALU.mult).then_inc(xn_ready, 1)
                if t:
                    dve.wait_ge(xn_ready, g * GT + t)
                    step(v.tensor_tensor(x_sb[0:P, g * GT + (t - 1), :], x_sb[0:P, g * GT + (t - 1), :], stage[0:P, t - 1, :], ALU.add))
            dve.wait_ge(xn_ready, g * GT + GT)
            step(v.tensor_tensor(x_sb[0:P, g * GT + (GT - 1), :], x_sb[0:P, g * GT + (GT - 1), :], stage[0:P, GT - 1, :], ALU.add))
            step.leave(NG)

        dve.wait_ge(edges_in, 8 * 16)
        step(v.tensor_copy(dstf, dst_ix[:, :]))
        step(v.memset(ns[:, 0:1], 0.0))
        step.settle()
        step(v.tensor_tensor(ns[:, 1:EC], dstf[:, 1:EC], dstf[:, 0:EC - 1], ALU.is_equal))
        step(v.tensor_scalar(dq, dstf, 1.0 / T, 0.5 / T - 0.5, ALU.mult, ALU.add))
        step.settle()
        step(v.tensor_scalar(negb[:, :], ns[:, :], -1.0, BIG, ALU.add, ALU.mult))
        step(v.tensor_copy(dfi, dq))
        step.settle()
        step(v.tensor_copy(dq, dfi))
        step.settle()
        step(v.scalar_tensor_tensor(dr, dq, -float(T), dstf, ALU.mult, ALU.add))
        step.settle()
        step(v.tensor_scalar(df, dr, 0.0, None, ALU.is_lt))
        step.settle()
        step(v.tensor_tensor(dq, dq, df, ALU.subtract))
        step(v.scalar_tensor_tensor(dr, df, float(T), dr, ALU.mult, ALU.add))
        step.settle()
        step(v.tensor_scalar(df, dr, float(T), None, ALU.is_ge))
        step.settle()
        step(v.tensor_tensor(dq, dq, df, ALU.add))
        step(v.scalar_tensor_tensor(dr, df, -float(T), dr, ALU.mult, ALU.add))
        step.settle()

        dve.wait_ge(xT_psum, T)
        with dve.Fori(0, NB // 2) as i:
            for h in (0, 1):
                dve.wait_ge(counted_block, i * 2)
                at = bass.ds(i * (2 * JB) + h * JB, JB)
                v.tensor_tensor(one_p[h], bc(iota_p.unsqueeze(1), [128, JB, P]),
                                bc(dq[:, at].unsqueeze(2), [128, JB, P]), ALU.is_equal).then_inc(onehot, 1)
                v.tensor_tensor(one_t[h][:, :, :], bc(iota_t.unsqueeze(1), [128, JB, T + 1]),
                                bc(dr[:, at].unsqueeze(2), [128, JB, T + 1]), ALU.is_ge).then_inc(onehot, 1)

        dve.wait_ge(counted, 1)
        v.tensor_copy(csb[0:P, :], ps[4][0:P, 0:T + 1]).then_inc(counts_sb, 1)
        dve.wait_ge(based, 1)
        dve.wait_ge(counts_sb, 1)
        step(v.tensor_copy(start[0:P, 0:1], ps[5][0:P, 0:1]))
        step.settle()
        step(v.tensor_scalar(ends[0:P, :], csb[0:P, 0:T], start[0:P, 0:1], None, ALU.add))
        step.settle()
        step(v.tensor_copy(start[0:P, 1:T], ends[0:P, 0:T - 1]))
        step.settle()
        step(v.tensor_tensor(full[0:P, :], ends[0:P, :], start[0:P, :], ALU.is_gt))
        step(v.tensor_tensor(tmpn[0:P, :], start[0:P, :], nid[0:P, :], ALU.subtract))
        step(v.tensor_scalar(gidx[0:P, :], ends[0:P, :], -1.0, 0.0, ALU.add, ALU.max))
        step.settle()
        step(v.tensor_scalar(tmpn[0:P, :], tmpn[0:P, :], -float(EP), None, ALU.add))
        step.settle()
        step(v.tensor_tensor(tmpn[0:P, :], tmpn[0:P, :], full[0:P, :], ALU.mult))
        step.settle()
        step(v.scalar_tensor_tensor(tmpn[0:P, :], tmpn[0:P, :], float(EP), nid[0:P, :], ALU.add, ALU.add))
        step.settle()
        v.tensor_copy(sidx[0:P, :], tmpn[0:P, :]).then_inc(places, 1)

        dve.wait_ge(w_in, 16 * len(W_LOADS))
        k4 = wkv[:, :, :].rearrange("c k (h m) -> c (k h) m", m=HC)
        b4 = kvb[:, :].rearrange("c (h m) -> c h m", m=HC)
        step(v.tensor_reduce(cm[:, :], k4, AX.X, ALU.add))
        step(v.tensor_reduce(cmb, b4, AX.X, ALU.add))
        step(v.tensor_reduce(hws[:, 2:3], hw[:, :], AX.X, ALU.max))
        step.settle()
        step(v.tensor_scalar(cm[:, :], cm[:, :], 1.0 / HC, None, ALU.mult))
        step(v.tensor_scalar(cmb, cmb, 1.0 / HC, None, ALU.mult))
        v.tensor_scalar(hws[:, 3:4], hws[:, 2:3], -1.0, None, ALU.mult).then_inc(hw_ready, 1)
        step.settle()
        v.tensor_tensor(k4, k4, bc(cm[:, :].unsqueeze(2), [128, 32, HC]), ALU.subtract).then_inc(wkv_ready, 1)
        v.tensor_tensor(b4, b4, bc(cmb.unsqueeze(2), [1, 16, HC]), ALU.subtract).then_inc(wkv_ready, 1)
        dve.wait_ge(b_psum, 1)
        step(v.tensor_tensor(gh[:, :, :], dm[:, :, :], ps[3][:, :].rearrange("p (k c) -> p k c", k=2), ALU.subtract))
        step.settle()
        step(v.tensor_scalar(gh[:, :, :], gh[:, :, :], 0.25, None, ALU.mult))
        step.settle()
        for k in range(2):
            d = gh[:, k, k * 128:(k + 1) * 128]
            v.scalar_tensor_tensor(d, ident[:, :], 0.5, d, ALU.mult, ALU.add).then_inc(gh_ready, 1)
        dve.wait_ge(hwe_ready, 1)
        step(v.reciprocal(hws[:, 2:3], hws[:, 1:2]))
        step.settle()
        step(v.tensor_tensor(hws[:, 3:4], hws[:, 0:1], hws[:, 2:3], ALU.mult))
        step.settle()
        dve.wait_ge(ug_psum, 1)
        v.tensor_scalar(ug[:, :], ps[7][0:64, 0:D], hws[:, 3:4], None, ALU.mult).then_inc(ug_ready, 1)

        with dve.Fori(0, NG) as g:
            for t in range(GT):
                dve.wait_ge(sq_ready, g * GT + (t + 1))
                v.tensor_reduce(kss[0:P, t % 2, :], sq[0:P, t % 2, :].rearrange("p (h m) -> p h m", m=HC),
                                AX.X, ALU.add).then_inc(ss_ready, 1)
                dve.wait_ge(ks_ready, g * GT + (t + 1))
                step_kr = v.reciprocal(krs[0:P, t % 2, :], kstd[0:P, t % 2, :])
                step_kr.then_inc(kr_step, 1)
                dve.wait_ge(kr_step, g * GT + (t + 1))
                dve.wait_ge(kv_used, g * GT + (t - 3 if t >= 4 else 0))
                k_ps = ps[t % 2][0:P, 0:D].rearrange("p (a h m) -> p a h m", a=2, m=HC)
                r_ap = krs[0:P, t % 2, :]
                for hg in (0, 1):
                    v.tensor_tensor(kh[0:P, t % 4, hg, 0:128].rearrange("p (h m) -> p h m", m=HC), k_ps[:, hg],
                                    bc(r_ap[:, 4 * hg:4 * hg + 4].unsqueeze(2), [P, 4, HC]), ALU.mult).then_inc(kv_ready, 1)
                v.tensor_tensor(vh[0:P, t % 4, :].rearrange("p (h m) -> p h m", m=HC),
                                ps[t % 2][0:P, D:2 * D].rearrange("p (h m) -> p h m", m=HC),
                                bc(r_ap[:, 8:16].unsqueeze(2), [P, 8, HC]), ALU.mult).then_inc(kv_ready, 1)

        dve.wait_ge(kv_summed, 1)
        dve.wait_ge(cols_ready, 1)
        for hg in (0, 1):
            step(v.tensor_copy(kva[:, hg, :], ps[6 + hg][:, 0:129]))
            step(v.tensor_copy(sk[:, :], ps[6 + hg][:, 256:384]))
            step.settle()
            step(v.tensor_tensor(kvs[:, :], kva[:, hg, 0:128], kgr[:, :], ALU.mult))
            step(v.tensor_tensor(sk[:, :], sk[:, :], kgr[:, :], ALU.mult))
            step.settle()
            step(v.scalar_tensor_tensor(kvs[:, :], kbr[:, :], kva[:, hg, 128:129], kvs[:, :], ALU.mult, ALU.add))
            step(v.scalar_tensor_tensor(sk[:, :], kbr[:, :], float(N), sk[:, :], ALU.mult, ALU.add))
            step.settle()
            step(v.tensor_scalar(sk[:, :], sk[:, :], cols[:, VB:VB + 1], None, ALU.mult))
            step.settle()
            step(v.scalar_tensor_tensor(kvs[:, :], kvs[:, :], cols[:, VG:VG + 1], sk[:, :], ALU.mult, ALU.add))
            step.settle()
            v.tensor_tensor(kvc[:, hg, :], kvs[:, :], blockd[:, :], ALU.mult).then_inc(kvt_ready, 1)
            dve.wait_ge(kvt_ready, hg + 1)
        dve.wait_ge(we_psum, 1)
        w_ps = ps[5][:, :].rearrange("p (k c) -> p k c", k=2)
        step(v.tensor_tensor(weff[:, :, :], w1[:, :, :], w_ps, ALU.add))
        step.settle()
        v.tensor_tensor(beff[:, :], ps[4][:, 0:2], cols[:, MB1:MB1 + 2], ALU.add).then_inc(we_ready, 1)

        def edges(i, h):
            n = i * GB + (h + 1)
            dve.wait_ge(fill_ready, n)
            step(v.tensor_tensor_scan(zt_f, keep_f, zt_f, 0.0, ALU.mult, ALU.add))
            dve.wait_ge(g_in[h], i * (16 * JB) + 16 * JB)
            dve.wait_ge(so_ready, i * GB + h)
            step.settle()
            step(v.tensor_tensor(wt[:, 0:KR, 1:JC], G[h].rearrange("p j f -> p f j"), zt[:, :, 1:JC], ALU.mult))
            step(v.tensor_copy(zt[:, :, 0:1], zt[:, :, JB:JC]))
            step.settle()
            step(v.tensor_reduce(lg[:, :, 1:JC], wt[:, 0:KR, 1:JC].rearrange("p (k r) j -> p k j r", k=K), AX.X, ALU.add))
            step.settle()
            step(v.tensor_tensor_scan(mx_f, negx_f, lg_f, 0.0, ALU.add, ALU.max))
            step.settle()
            step(v.tensor_tensor(d2[:, :, :], mx[:, :, 0:JB], mx[:, :, 1:JC], ALU.subtract))
            step(v.tensor_tensor(d1[:, :, :], lg[:, :, 1:JC], mx[:, :, 1:JC], ALU.subtract))
            step.settle()
            v.tensor_tensor(d2[:, :, :], d2[:, :, :], negx[:, :, 1:JC], ALU.add).then_inc(e_diff, 1)
            step(v.tensor_copy(lg[:, :, 0:1], mx[:, :, JB:JC]))
            dve.wait_ge(e_exp, n)
            v.tensor_tensor(wt[:, 0:KR, 1:JC].rearrange("p (k r) j -> p k r j", k=K),
                            G[h].rearrange("p j (k r) -> p k r j", k=K),
                            bc(wt[:, KR:SK, 1:JC].unsqueeze(2), [128, K, R, JB]), ALU.mult).then_inc(g_free[h], 1)
            dve.wait_ge(g_free[h], i + 1)
            v.tensor_tensor_scan(wt_f, decay_f, wt_f, 0.0, ALU.mult, ALU.add).then_inc(summed, 1)
            dve.wait_ge(summed, n)
            step(v.tensor_copy(wt[:, :, 0:1], wt[:, :, JB:JC]))

        for ap in (zt[:, :, 0:1], keep[:, :, 0:1], wt[:, :, 0:1], decay[:, :, 0:1], lg[:, :, 0:1]):
            step(v.memset(ap, 0.0))
        v.memset(negx[:, :, 0:1], -BIG).then_inc(fill_init, 1)
        with dve.Fori(0, NI) as i:
            step.enter(i, EDGE_STEPS)
            for h in range(GB):
                edges(i, h)
            step.leave(NI)
        step.settle()

        dve.wait_ge(xt_init, 2 * 16)
        F_, L_, C_, SAME, GO = range(5)
        step(v.tensor_copy(row[0:1, F_, :], rowi[0:1, 0, :]))
        step(v.tensor_copy(row[0:1, L_, :], rowi[0:1, 1, :]))
        step(v.memset(row[0:1, C_, 0:1], 0.0))
        step(v.tensor_copy(fin[:, 0:SK], wt[:, :, 0]))
        step(v.tensor_copy(fin[:, SK:SK + KR].rearrange("p (k r) -> p k r", r=R), bc(lg[:, :, 0:1], [128, K, R])))
        step(v.tensor_copy(fin[:, SK + KR:2 * SK], lg[:, :, 0]))
        step.settle()
        v.memset(q[6][:, 0:1], 0.0).then_inc(fin_ready, 1)
        step(v.tensor_tensor(row[0:1, C_, 1:128], row[0:1, L_, 0:127], row[0:1, F_, 1:128], ALU.is_equal))
        step(v.tensor_tensor(row[0:1, SAME, :], row[0:1, F_, :], row[0:1, L_, :], ALU.is_equal))
        step.settle()
        step(v.memset(row[0:1, L_, 127:128], 0.0))
        step(v.tensor_tensor(row[0:1, GO, :], row[0:1, C_, :], row[0:1, SAME, :], ALU.mult))
        step(v.tensor_tensor(row[0:1, L_, 0:127], row[0:1, SAME, 0:127], row[0:1, C_, 1:128], ALU.mult))
        step(v.tensor_tensor(row[0:1, F_, :], row[0:1, F_, :], dump_row, ALU.subtract))
        step.settle()
        step(v.tensor_scalar(row[0:1, L_, :], row[0:1, L_, :], -1.0, 1.0, ALU.mult, ALU.add))
        step.settle()
        step(v.tensor_tensor(row[0:1, L_, :], row[0:1, L_, :], row[0:1, C_, :], ALU.mult))
        step.settle()
        step(v.tensor_tensor(row[0:1, F_, :], row[0:1, F_, :], row[0:1, L_, :], ALU.mult))
        step.settle()
        v.tensor_tensor(row[0:1, F_, :], row[0:1, F_, :], dump_row, ALU.add).then_inc(row_ready, 1)
        dve.wait_ge(row_psum, 1)
        step(v.tensor_copy(q[0][:, 0:128], ps[1][0:SK, 0:128]))
        v.tensor_copy(tgt[:, :], ps[2][:, 0:1]).then_inc(cr_ready, 1)
        dve.wait_ge(fin_psum, 1)
        step(v.tensor_copy(q[1][:, 0:128], ps[0][0:SK, 0:128]))
        step(v.tensor_copy(q[2][:, 0:128], ps[0][0:SK, 128:256]))
        step.settle()
        step(v.tensor_scalar(q[5][:, 0:128], q[0][:, 0:128], -1.0, BIG, ALU.add, ALU.mult))
        step(v.memset(q[6][:, 0:1], 0.0))
        step.settle()
        step(v.tensor_tensor_scan(q[6][:, 1:129], q[5][:, 0:128], q[2][:, 0:128], 0.0, ALU.add, ALU.max))
        step.settle()
        step(v.tensor_tensor(q[3][:, 0:128], q[6][:, 0:128], q[6][:, 1:129], ALU.subtract))
        step(v.tensor_tensor(q[4][:, 0:128], q[2][:, 0:128], q[6][:, 1:129], ALU.subtract))
        step.settle()
        v.tensor_tensor(q[3][:, 0:128], q[3][:, 0:128], q[5][:, 0:128], ALU.add).then_inc(q_ready, 1)
        dve.wait_ge(q_exp, 1)
        step(v.tensor_tensor(q[1][:, 0:128], q[1][:, 0:128], q[4][:, 0:128], ALU.mult))
        step(v.memset(q[2][:, 0:1], 0.0))
        step.settle()
        v.tensor_tensor_scan(q[2][:, 1:129], q[3][:, 0:128], q[1][:, 0:128], 0.0, ALU.mult, ALU.add).then_inc(cr_done, 1)

        dve.wait_ge(mo_ready, T)
        for g in range(NG):
            step(v.tensor_tensor(x_sb[0:P, g * GT:(g + 1) * GT, :].rearrange("p t d -> p (t d)"),
                                 x_sb[0:P, g * GT:(g + 1) * GT, :].rearrange("p t d -> p (t d)"), mix_sb[0:P, g, :], ALU.add))

        dve.wait_ge(ng_in, 16 * T)
        dve.wait_ge(xc_in, 2 * 16)
        step(v.tensor_tensor(nm[0:P, :, :], ng[0:P, :, SK:SW], xc[0:P, :, SK:SW], ALU.max))
        step.settle()
        step(v.tensor_tensor(nw1[0:P, :, :], ng[0:P, :, SK:SW], nm[0:P, :, :], ALU.subtract))
        step.settle()
        v.tensor_tensor(nw2[0:P, :, :], xc[0:P, :, SK:SW], nm[0:P, :, :], ALU.subtract).then_inc(merge_d, 1)
        dve.wait_ge(merge_e, 1)
        for k in range(K):
            for rows_, w_ in ((ng, nw1), (xc, nw2)):
                step(v.tensor_tensor(rows_[0:P, :, k * R:(k + 1) * R], rows_[0:P, :, k * R:(k + 1) * R],
                                     bc(w_[0:P, :, k:k + 1], [P, T, R]), ALU.mult))
        for rows_, w_ in ((ng, nw1), (xc, nw2)):
            step(v.tensor_tensor(rows_[0:P, :, KR:SK], rows_[0:P, :, KR:SK], w_[0:P, :, :], ALU.mult))
        step.settle()
        step(v.tensor_tensor(ng[0:P, :, 0:SK], ng[0:P, :, 0:SK], xc[0:P, :, 0:SK], ALU.add))
        step.settle()
        step(v.tensor_scalar(nden[0:P, :, :], ng[0:P, :, KR:SK], 1e-16, None, ALU.add))
        step.settle()
        step(v.reciprocal(nden[0:P, :, :], nden[0:P, :, :]))
        step.settle()
        step(v.tensor_tensor(nden[0:P, :, :], nden[0:P, :, :], bc(full[0:P, :].unsqueeze(2), [P, T, K]), ALU.mult))
        step.settle()
        for k in range(K):
            v.tensor_tensor(gx_agg[0:P, :, k * R:(k + 1) * R], ng[0:P, :, k * R:(k + 1) * R],
                            bc(nden[0:P, :, k:k + 1], [P, T, R]), ALU.mult).then_inc(gx_agg_ready, 1)
        dve.wait_ge(gx_agg_ready, K)

        with dve.Fori(0, NG) as g:
            step.enter(g, TAIL_STEPS)
            dve.wait_ge(agg_psum, g)
            v.tensor_copy(agg_st[0:P, :, :], gx_agg[0:P, bass.ds(g * GT, GT), :]).then_inc(agg_ready, 1)
            for t in range(GT):
                xt = x_sb[0:P, g * GT + t, :]
                dve.wait_ge(y_psum, g * GT + (t + 1))
                v.scalar_tensor_tensor(acc[0:P, t % 2, :], ps[4 + t % 2][0:P, 0:D], -ETA_LAM, gx[0:P, g * GT + t, :],
                                       ALU.add, ALU.add).then_inc(y_used, 1)
                dve.wait_ge(y_used, g * GT + (t + 1))
                v.scalar_tensor_tensor(xt, acc[0:P, t % 2, :], 0.0, xt, ALU.max, ALU.add).then_inc(x2_ready, 1)
                dve.wait_ge(x2_ready, g * GT + (t + 1))
                held(nc.vector)
                step(v.bn_stats(st[0:P, t, :], xt))
            step.settle()
            held(nc.vector)
            for t in range(GT):
                if t < GT - 1:
                    step(v.bn_aggr(mv[0:P, t, :], st[0:P, t, :]))
                else:
                    v.bn_aggr(mv[0:P, t, :], st[0:P, t, :]).then_inc(stats2, 1)
            dve.wait_ge(stds2, g * 2 + 1)
            step(v.reciprocal(rstd[0:P, :], std[0:P, :]))
            step.settle()
            step(v.tensor_tensor(fac[0:P, :], rstd[0:P, :], rstd[0:P, :], ALU.mult))
            step.settle()
            v.tensor_tensor(fac[0:P, :], fac[0:P, :], mv[0:P, :, 1], ALU.mult).then_inc(r_read, 1)
            dve.wait_ge(stds2, g * 2 + 2)
            step(v.reciprocal(std2[0:P, :], std2[0:P, :]))
            step.settle()
            step(v.tensor_tensor(rstd[0:P, :], rstd[0:P, :], std2[0:P, :], ALU.mult))
            step.settle()
            dve.wait_ge(z_out, g * 32)
            for t in range(GT):
                v.tensor_scalar(stage[0:P, t, :], x_sb[0:P, g * GT + t, :], mv[0:P, t, 0:1], rstd[0:P, t:t + 1],
                                ALU.subtract, ALU.mult).then_inc(z_ready, 1)
            for t in range(GT):
                dve.wait_ge(zT_psum, g * GT + (t + 1))
                for k in (0, 1):
                    v.tensor_scalar(xT_st[:, k, t * P:(t + 1) * P], ps[6 + t % 2][:, k * P:(k + 1) * P],
                                    cols[:, GAM + k:GAM + k + 1], cols[:, BET + k:BET + k + 1], ALU.mult, ALU.add).then_inc(zT_ready, 1)
                dve.wait_ge(r_psum, g * GT + (t + 1))
                step(v.tensor_tensor(rl[0:P, t, :], ps[4 + t % 2][0:P, 256:256 + NX], brr[0:P, :], ALU.add))
            step.settle()
            held(nc.vector)
            for t in range(GT):
                step(v.max(r8[0:P, t, :], rl[0:P, t, :]))
            step.settle()
            held(nc.vector)
            for t in range(GT):
                step(v.max_index(ri[0:P, t, :], r8[0:P, t, :], rl[0:P, t, :]))
            step.settle()
            mine = bass.ds(g * GT, GT)
            step(v.tensor_copy(rf[0:P, mine, :], ri[0:P, :, 0:2]))
            v.tensor_tensor(rd[0:P, :, 0], r8[0:P, :, 1], r8[0:P, :, 0], ALU.subtract).then_inc(r_diff, 1)
            dve.wait_ge(r_exp, g + 1)
            step(v.tensor_scalar(fac[0:P, :], rd[0:P, :, 1], 1.0, None, ALU.add))
            step.settle()
            step(v.reciprocal(std2[0:P, :], fac[0:P, :]))
            step.settle()
            step(v.tensor_copy(rp[0:P, mine, 0], std2[0:P, :]))
            step(v.tensor_tensor(rp[0:P, mine, 1], rd[0:P, :, 1], std2[0:P, :], ALU.mult))
            step.leave(NG)
        step.settle()
        v.memset(std2[0:1, 0:1], 0.0).then_inc(nodes_done, 1)

        step(v.memset(gix[:, :], 0))

        def te(ap):
            return ap.rearrange("p e t -> p t e")

        step(v.tensor_tensor(te(ch0[0:P]), bc(iota8[0:P, :].unsqueeze(1), [P, T, NX]), bc(rf[0:P, :, 0:1], [P, T, NX]), ALU.is_equal))
        step(v.tensor_tensor(te(ch1[0:P]), bc(iota8[0:P, :].unsqueeze(1), [P, T, NX]), bc(rf[0:P, :, 1:2], [P, T, NX]), ALU.is_equal))
        step.settle()
        v.tensor_tensor(chs[0:P], ch0[0:P], ch1[0:P], ALU.add).then_inc(choices, 1)
        dve.wait_ge(ranked_psum, 1)
        step(v.tensor_copy(tot, ps[1][:, 0:TX].rearrange("p (e t) -> p e t", t=T)))
        step.settle()
        for e in range(NX):
            step(v.tensor_tensor_scan(excl[:, e, :], ones[:, 0:T], tot[:, e, :], 0.0, ALU.mult, ALU.add))
        step.settle()
        step(v.tensor_tensor(cmpb, bc(excl[:, :, T - 1:T], [128, NX, T]), bc(steps_b[:, :].unsqueeze(1), [128, NX, T]), ALU.is_gt))
        step(v.tensor_tensor(tot, excl, tot, ALU.subtract))
        step.settle()
        step(v.tensor_reduce(nblk, cmpb, AX.X, ALU.add))
        step(v.tensor_tensor(rank[0:P], ps[0][0:P, 0:TX].rearrange("p (e t) -> p e t", t=T), tot[0:P], ALU.add))
        step.settle()
        step(v.tensor_tensor_scan(bend, ones[:, 0:NX], nblk, 0.0, ALU.mult, ALU.add))
        step.settle()
        step(v.tensor_tensor(bstart, bend, nblk, ALU.subtract))
        step(v.tensor_tensor(cmpx, bc(iota_b[:, :].unsqueeze(2), [128, XB, NX]), bc(bend.unsqueeze(1), [128, XB, NX]), ALU.is_ge))
        step.settle()
        step(v.tensor_reduce(spos[:, :], cmpx, AX.X, ALU.add))
        step(v.tensor_scalar(bstart, bstart, float(BX), None, ALU.mult))
        step.settle()
        step(v.tensor_scalar(eix[:, :], spos[:, :], float(NX - 1), None, ALU.min))
        step(v.tensor_tensor(rank[0:P], rank[0:P], bc(bstart[0:P].unsqueeze(2), [P, NX, T]), ALU.add))
        step.settle()
        step(v.tensor_tensor(ch0[0:P], ch0[0:P], rank[0:P], ALU.mult))
        step(v.tensor_tensor(ch1[0:P], ch1[0:P], rank[0:P], ALU.mult))
        step.settle()
        step(v.tensor_reduce(slot[0:P, 0, :], te(ch0[0:P]), AX.X, ALU.add))
        step(v.tensor_reduce(slot[0:P, 1, :], te(ch1[0:P]), AX.X, ALU.add))
        step.settle()
        sl, hi_, lo_, fx = slot[0:P], shi[0:P], slo[0:P], sfx[0:P]
        step(v.tensor_scalar(hi_, sl, 1.0 / BX, 0.5 / BX - 0.5, ALU.mult, ALU.add))
        step.settle()
        step(v.tensor_copy(sint[0:P], hi_))
        step.settle()
        step(v.tensor_copy(hi_, sint[0:P]))
        step.settle()
        step(v.scalar_tensor_tensor(lo_, hi_, -float(BX), sl, ALU.mult, ALU.add))
        step.settle()
        step(v.tensor_scalar(fx, lo_, 0.0, None, ALU.is_lt))
        step.settle()
        step(v.tensor_tensor(hi_, hi_, fx, ALU.subtract))
        step(v.scalar_tensor_tensor(lo_, fx, float(BX), lo_, ALU.mult, ALU.add))
        step.settle()
        step(v.tensor_scalar(fx, lo_, float(BX), None, ALU.is_ge))
        step.settle()
        step(v.tensor_tensor(hi_, hi_, fx, ALU.add))
        step(v.scalar_tensor_tensor(lo_, fx, -float(BX), lo_, ALU.mult, ALU.add))
        step.settle()
        for g in range(NG):
            h = g % 2
            if g >= 2:
                dve.wait_ge(oh_used, g - 1)
            mine = slice(g * GT, (g + 1) * GT)
            for c in (0, 1):
                step(v.tensor_tensor(oh_lo[h][0:P, c], bc(iota_lo[0:P, :].unsqueeze(1), [P, GT, BX]),
                                     bc(slo[0:P, c, mine].unsqueeze(2), [P, GT, BX]), ALU.is_equal))
                step(v.tensor_tensor(oh_v[h][0:P, c, :, 0:XB], bc(iota_b[0:P, :].unsqueeze(1), [P, GT, XB]),
                                     bc(shi[0:P, c, mine].unsqueeze(2), [P, GT, XB]), ALU.is_equal))
            step.settle()
            for c in (0, 1):
                step(v.tensor_tensor(oh_v[h][0:P, c, :, XB:2 * XB], oh_v[h][0:P, c, :, 0:XB],
                                     bc(rp[0:P, mine, c:c + 1], [P, GT, XB]), ALU.mult))
            step.settle()
            for c in (0, 1):
                v.tensor_tensor(oh_v[h][0:P, c, :, 0:XB], oh_v[h][0:P, c, :, 0:XB],
                                bc(nid1[0:P, mine].unsqueeze(2), [P, GT, XB]), ALU.mult).then_inc(oh_ready, 1)
        dve.wait_ge(slots_psum, 1)
        step(v.tensor_copy(sid[:, :], ps[2][:, 0:XB]))
        step(v.tensor_copy(sw[:, :], ps[2][:, XB:2 * XB]))
        step.settle()
        step(v.tensor_scalar(gix[:, 0:XB], sid[:, :], -1.0, 0.0, ALU.add, ALU.max))
        step(v.tensor_scalar(sfill[:, :], sid[:, :], 0.5, None, ALU.is_gt))
        step(v.tensor_scalar(spos[:, :], sid[:, :], dump[:, 0:1], 1.0, ALU.subtract, ALU.subtract))
        step.settle()
        step(v.tensor_tensor(spos[:, :], spos[:, :], sfill[:, :], ALU.mult))
        step.settle()
        v.tensor_scalar(six[:, :], spos[:, :], dump[:, 0:1], None, ALU.add).then_inc(slots_ready, 1)

        dve.wait_ge(b1_in, 16)
        dve.wait_ge(b2_in, 16)
        dve.wait_ge(slots_ready, 1)

        def rows_T(i, h):
            dve.wait_ge(xg_psum, i * XQ + (h + 1))
            for k in (0, 1):
                v.tensor_scalar(xb[h % 2][:, k, :], ps[h % 2][:, k * BX:(k + 1) * BX], cols[:, GAM + k:GAM + k + 1],
                                cols[:, BET + k:BET + k + 1], ALU.mult, ALU.add).then_inc(xb_ready, 1)

        def first_bias(i, h):
            e = dve.value_load(eix[0:1, bass.ds(i * XQ + h, 1)], min_val=0, max_val=NX - 1)
            dve.wait_ge(h_psum, i * XQ + (h + 1))
            v.tensor_tensor(hb[h % 2], ps[2 + h % 2][:, :], b1row[:, bass.ds(e, 1), :].rearrange("p e m -> p (e m)"),
                            ALU.add).then_inc(hb_ready, 1)

        def rows_y(i, h, first=False):
            e = dve.value_load(eix[0:1, bass.ds(i * XQ + h, 1)], min_val=0, max_val=NX - 1)
            dve.wait_ge(ye_psum, i * XQ + (h + 1))
            if not first:
                dve.wait_ge(added, i * (16 * XQ) + 16 * (h - XQ + 1))
            y = yb[h % XQ]
            v.tensor_tensor(y, ps[6 + h % 2][:, 0:D], b2row[:, bass.ds(e, 1), :].rearrange("p e m -> p (e m)"),
                            ALU.add).then_inc(yb_step, 1)
            dve.wait_ge(yb_step, i * XQ + (h + 1))
            v.tensor_scalar(y, y, sw[:, bass.ds(i * XQ + h, 1)], None, ALU.mult).then_inc(yb_ready, 1)

        rows_T(0, 0)
        for h in range(XQ):
            first_bias(0, h)
            rows_T(0, h + 1)
            if h >= 2:
                rows_y(0, h - 2, True)
        for h in range(XQ):
            first_bias(1, h)
            rows_T(1, h + 1)
            rows_y(1, h - 2, h < 2)
        with dve.Fori(2, XI) as i:
            for h in range(XQ):
                first_bias(i, h)
                rows_T(i, h + 1)
                rows_y(i, h - 2)
        rows_y(XI - 1, XQ - 2)
        rows_y(XI - 1, XQ - 1)

    @block.tensor
    def _(pe):
        mm, tr = nc.tensor.matmul, nc.tensor.transpose

        def x_tile(t, k):
            return xT_st[:, k, t * P:(t + 1) * P]

        pe.wait_ge(u_in, 2 * 16)
        pe.wait_ge(consts, 2)
        with pe.Fori(0, NG) as g:
            def project(t):
                pe.wait_ge(xT_ready, g * GT + (t + 1))
                pe.wait_ge(zu_ready, g * GT + (t - 1 if t >= 2 else 0))
                for k in (0, 1):
                    ins = mm(ps[2 + t % 2][0:P, 0:KR], x_tile(t, k), u_sb[:, k, :], start=k == 0, stop=k == 1)
                ins.then_inc(zu_psum, 1)

            for t in range(GT):
                pe.wait_ge(xn_ready, g * GT + (t + 1))
                pe.wait_ge(xT_ready, g * GT + (t - 1 if t >= 2 else 0))
                for k in (0, 1):
                    ins = tr(ps[t % 2][:, k * P:(k + 1) * P], stage[0:P, t, k * 128:(k + 1) * 128], ident[0:P, 0:P])
                ins.then_inc(xT_psum, 1)
                if t:
                    project(t - 1)
            project(GT - 1)

        pe.wait_ge(w_in, 16 * len(W_LOADS))
        pe.wait_ge(zu_ready, T)
        tr(ps[0][:, 0:NR], rows[:, :], ident[0:NR, 0:NR]).then_inc(rows_psum, 1)
        for dt_ in (0, 1):
            for ct in (0, 1):
                ins = tr(ps[1][:, dt_ * D + ct * 128:dt_ * D + (ct + 1) * 128], wq[:, ct, dt_ * 128:(dt_ + 1) * 128], ident[:, :])
        ins.then_inc(wqT_psum, 1)
        for r in (0, 1):
            for k in (0, 1):
                ins = mm(ps[2][:, r * D:(r + 1) * D], dm[:, k, r * 128:(r + 1) * 128], dm[:, k, :], start=k == 0, stop=k == 1)
        ins.then_inc(dtd_psum, 1)
        pe.wait_ge(dtd_ready, 1)
        for r in (0, 1):
            for k in (0, 1):
                ins = mm(ps[3][:, r * D:(r + 1) * D], dtd[:, k, r * 128:(r + 1) * 128], dm[:, k, :], start=k == 0, stop=k == 1)
        ins.then_inc(b_psum, 1)

        mm(ps[4][0:P, 0:T + 1], zero[:, 0:P], zero[:, 0:T + 1], start=True, stop=False, skip_group_check=True)
        with pe.Fori(0, NB // 2) as i:
            for h in (0, 1):
                pe.wait_ge(onehot, i * 4 + 2 * (h + 1))
                for j in range(JB):
                    ins = mm(ps[4][0:P, 0:T + 1], one_p[h][:, j, :], one_t[h][:, j, :], start=False, stop=False, skip_group_check=True)
                ins.then_inc(counted_block, 1)
        mm(ps[4][0:P, 0:T + 1], zero[:, 0:P], zero[:, 0:T + 1], start=False, stop=True, skip_group_check=True).then_inc(counted, 1)
        pe.wait_ge(counts_sb, 1)
        mm(ps[5][0:P, 0:1], tri[0:P, 0:P], csb[0:P, T:T + 1], start=True, stop=True).then_inc(based, 1)
        pe.wait_ge(gh_ready, 2)
        for k in (0, 1):
            ins = mm(ps[7][0:64, 0:D], u_sb[:, k, :], gh[:, k, :], start=k == 0, stop=k == 1)
        ins.then_inc(ug_psum, 1)
        pe.wait_ge(ug_ready, 1)

        pe.wait_ge(wkv_ready, 2)
        pe.wait_ge(cols_ready, 1)
        pe.wait_ge(wqT_ready, 1)
        for hg in (0, 1):
            mm(ps[6 + hg][:, 0:384], zero[:, 0:128], zero[:, 0:384], start=True, stop=False, skip_group_check=True)
        with pe.Fori(0, NG) as g:
            def product(t):
                pe.wait_ge(kv_ready, g * (3 * GT) + 3 * (t + 1))
                for hg in (0, 1):
                    v_ = vh[0:P, t % 4, hg * 128:(hg + 1) * 128]
                    mm(ps[6 + hg][:, 0:129], v_, kh[0:P, t % 4, hg, :], start=False, stop=False, skip_group_check=True)
                    ins = mm(ps[6 + hg][:, 256:384], ones[0:P, :], kh[0:P, t % 4, hg, 0:128], start=False, stop=False, skip_group_check=True)
                ins.then_inc(kv_used, 1)

            for t in range(GT):
                pe.wait_ge(kx_ready, g * GT + (t + 1))
                pe.wait_ge(kv_ready, g * (3 * GT) + (3 * (t - 1) if t >= 2 else 0))
                mm(ps[t % 2][0:P, :], ones[32:33, 0:P], kvb[:, :], start=True, stop=False)
                for k in (0, 1):
                    ins = mm(ps[t % 2][0:P, :], x_tile(t, k), wkv[:, k, :], start=False, stop=k == 1)
                ins.then_inc(kv_psum, 1)
                pe.wait_ge(gx_ready, g * GT + (t - 1 if t >= 2 else 0))
                for k in (0, 1):
                    ins = mm(ps[2 + t % 2][0:P, 0:D], x_tile(t, k), gh[:, k, :], start=k == 0, stop=k == 1)
                ins.then_inc(gx_psum, 1)
                if t:
                    product(t - 1)
            product(GT - 1)
        for hg in (0, 1):
            ins = mm(ps[6 + hg][:, 0:384], zero[:, 0:128], zero[:, 0:384], start=False, stop=True, skip_group_check=True)
        ins.then_inc(kv_summed, 1)

        pe.wait_ge(kvt_ready, 2)
        for hg in (0, 1):
            ins = mm(ps[4][:, hg * D:(hg + 1) * D], kvc[:, hg, :], w1[:, hg, :], start=True, stop=True)
        ins.then_inc(t1_psum, 1)
        pe.wait_ge(t1_ready, 1)
        for c in (0, 1):
            for k in (0, 1):
                ins = mm(ps[5][:, c * D:(c + 1) * D], wqT[:, k, c * 128:(c + 1) * 128], t1[:, k, :], start=k == 0, stop=k == 1)
        for m in (0, 1):
            for k in (0, 1):
                ins = mm(ps[4][:, m:m + 1], t1[:, k, m * 128:(m + 1) * 128], cols[:, BQ + k:BQ + k + 1], start=k == 0, stop=k == 1)
        ins.then_inc(we_psum, 1)

        pe.wait_ge(we_ready, 1)
        with pe.Fori(0, NG) as g:
            for m in (0, 1):
                for c, (lo, hi) in enumerate(CUTS):
                    pe.wait_ge(mh_ready, g * 4)
                    for k in (0, 1):
                        ins = mm(ps[2 * m + c][:, 0:hi - lo], weff[:, k, m * 128:(m + 1) * 128],
                                 xnT[:, g, :][:, k * GC + lo:k * GC + hi], start=k == 0, stop=k == 1)
                    ins.then_inc(mh_psum, 1)
            pe.wait_ge(mh_ready, g * 4 + 4)
            for t in range(GT):
                pe.wait_ge(mo_ready, g * GT + (t - 1 if t >= 2 else 0))
                mm(ps[4 + t % 2][0:P, 0:D], ones[64:65, 0:P], mb2, start=True, stop=False)
                for m in (0, 1):
                    ins = mm(ps[4 + t % 2][0:P, 0:D], mixh[:, m, t * P:(t + 1) * P], w2[:, m, :], start=False, stop=m == 1)
                ins.then_inc(mo_psum, 1)

        pe.wait_ge(mo_ready, T)
        pe.wait_ge(fin_ready, 1)
        tr(ps[0][0:SK, 0:128], fin[:, 0:SK], ident[:, :])
        tr(ps[0][0:SK, 128:256], fin[:, SK:2 * SK], ident[:, :]).then_inc(fin_psum, 1)
        pe.wait_ge(row_ready, 1)
        mm(ps[1][0:SK, 0:128], ones[0:1, 0:SK], row[0:1, 4, :], start=True, stop=True)
        mm(ps[2][:, 0:1], row[0:1, 0, :], ones[0:1, 0:1], start=True, stop=True).then_inc(row_psum, 1)
        pe.wait_ge(cr_done, 1)
        tr(ps[0][:, 0:SK], q[2][:, 0:128], ident[0:SK, 0:SK])
        tr(ps[1][:, 0:SK], q[6][:, 0:128], ident[0:SK, 0:SK]).then_inc(cr_psum, 1)

        pe.wait_ge(xw_in, 6 * 16)
        with pe.Fori(0, NG) as g:
            pe.wait_ge(agg_ready, g + 1)
            mm(ps[6][0:64, 0:4], zero[:, 0:64], zero[:, 0:4], start=True, stop=True)
            for t in range(GT):
                ins = tr(ps[6 + t // 4][0:64, (t % 4) * P:(t % 4 + 1) * P], agg_st[0:P, t, :], ident[0:P, 0:P])
            ins.then_inc(agg_psum, 1)
            pe.wait_ge(aggT_ready, g + 1)
            for t in range(GT):
                pe.wait_ge(y_used, g * GT + (t - 1 if t >= 2 else 0))
                mm(ps[4 + t % 2][0:P, 0:D], aggT[:, t * P:(t + 1) * P], ug[:, :], start=True, stop=True).then_inc(y_psum, 1)
            pe.wait_ge(y_used, g * GT + GT)
            for t in range(GT):
                pe.wait_ge(z_ready, g * GT + (t + 1))
                pe.wait_ge(zT_ready, g * (2 * GT) + (2 * (t - 1) if t >= 2 else 0))
                for k in (0, 1):
                    ins = tr(ps[6 + t % 2][:, k * P:(k + 1) * P], stage[0:P, t, k * 128:(k + 1) * 128], ident[0:P, 0:P])
                ins.then_inc(zT_psum, 1)
                pe.wait_ge(zT_ready, g * (2 * GT) + 2 * (t + 1))
                for k in (0, 1):
                    ins = mm(ps[4 + t % 2][0:P, 256:256 + NX], x_tile(t, k), wr[:, k, :], start=k == 0, stop=k == 1)
                ins.then_inc(r_psum, 1)

        pe.wait_ge(choices, 1)
        mm(ps[0][0:P, 0:TX], tri[0:P, 0:P], chs[0:P].rearrange("p e t -> p (e t)"), start=True, stop=True)
        mm(ps[1][:, 0:TX], ones[0:P, :], chs[0:P].rearrange("p e t -> p (e t)"), start=True, stop=True).then_inc(ranked_psum, 1)
        for g in range(NG):
            pe.wait_ge(oh_ready, 2 * (g + 1))
            for c in (0, 1):
                for t in range(GT):
                    first, last = g == 0 and c == 0 and t == 0, g == NG - 1 and c == 1 and t == GT - 1
                    ins = mm(ps[2][:, 0:2 * XB], oh_lo[g % 2][0:P, c, t, :], oh_v[g % 2][0:P, c, t, :], start=first, stop=last)
            ins.then_inc(oh_used if g < NG - 1 else slots_psum, 1)

        pe.wait_ge(slots_ready, 1)
        pe.wait_ge(xw_in, 6 * 16)

        def rows_T(i, h, first=False):
            pe.wait_ge(xg_in[h % XQ], i * 16 + 16 * (h // XQ + 1))
            if not first:
                pe.wait_ge(xb_ready, i * (2 * XQ) + 2 * (h - 1))
            for k in (0, 1):
                ins = tr(ps[h % 2][:, k * BX:(k + 1) * BX], xg[h % XQ][:, k * 128:(k + 1) * 128], ident[:, :])
            ins.then_inc(xg_psum, 1)

        def hidden(i, h, first=False):
            e = pe.value_load(eix[0:1, bass.ds(i * XQ + h, 1)], min_val=0, max_val=NX - 1)
            pe.wait_ge(xb_ready, i * (2 * XQ) + 2 * (h + 1))
            if not first:
                pe.wait_ge(hb_ready, i * XQ + (h - 1))
            for k in (0, 1):
                ins = mm(ps[2 + h % 2][:, :], xb[h % 2][:, k, :], W1[:, bass.ds(e, 1), k, :].rearrange("p e m -> p (e m)"),
                         start=k == 0, stop=k == 1)
            ins.then_inc(h_psum, 1)

        def hidden_T(i, h, first=False):
            pe.wait_ge(hg_ready, i * XQ + (h + 1))
            if not first:
                pe.wait_ge(hT_ready, i * XQ + (h - 1))
            for m in range(4):
                ins = tr(ps[4 + h % 2][:, m * BX:(m + 1) * BX], hb[h % 2][:, m * 128:(m + 1) * 128], ident[:, :])
            ins.then_inc(hT_psum, 1)

        def results(i, h, first=False):
            e = pe.value_load(eix[0:1, bass.ds(i * XQ + h, 1)], min_val=0, max_val=NX - 1)
            pe.wait_ge(hT_ready, i * XQ + (h + 1))
            if not first:
                pe.wait_ge(yb_step, i * XQ + (h - 1))
            for m in range(4):
                ins = mm(ps[6 + h % 2][:, 0:D], hT[h % 2][:, m, :], W2[:, bass.ds(e, 1), m, :].rearrange("p e m -> p (e m)"),
                         start=m == 0, stop=m == 3)
            ins.then_inc(ye_psum, 1)

        rows_T(0, 0, True)
        for h in range(XQ):
            hidden(0, h, h < 2)
            if h >= 2:
                results(0, h - 2, h < 4)
            rows_T(0, h + 1, h + 1 < 2)
            if h >= 1:
                hidden_T(0, h - 1, h < 3)
        with pe.Fori(1, XI) as i:
            for h in range(XQ):
                hidden(i, h)
                results(i, h - 2)
                rows_T(i, h + 1)
                hidden_T(i, h - 1)
        results(XI - 1, XQ - 2)
        hidden_T(XI - 1, XQ - 1)
        results(XI - 1, XQ - 1)


_INS = ['x', 'src', 'dst', 'L0_gnn_U', 'L0_gnn_Dmat', 'L0_gnn_head_w', 'L0_mix_w_qkv', 'L0_mix_b_qkv', 'L0_mix_kln_g',
        'L0_mix_kln_b', 'L0_mix_vln_g', 'L0_mix_vln_b', 'L0_mix_w1', 'L0_mix_b1', 'L0_mix_w2', 'L0_mix_b2',
        'L0_ffn_gamma', 'L0_ffn_beta', 'L0_ffn_Wr', 'L0_ffn_br', 'L0_ffn_W1', 'L0_ffn_b1', 'L0_ffn_W2', 'L0_ffn_b2']


def kernel(**inputs):
    import numpy as np
    import concourse.bacc as bacc
    from concourse import mybir as mb
    from concourse.bass_utils import run_bass_kernel_spmd

    nc = bacc.Bacc("TRN2", target_bir_lowering=False, num_devices=1)
    arrays, args = {}, {}
    for name in _INS:
        arr = np.ascontiguousarray(inputs[name])
        arrays[f"in_{name}"] = arr
        args[name] = nc.dram_tensor(f"in_{name}", arr.shape, mb.dt.from_np(arr.dtype), kind="ExternalInput").ap()
    out = nc.dram_tensor("out", (N + 128, D), F32, kind="ExternalOutput").ap()
    program(nc, args, out)
    r = run_bass_kernel_spmd(nc, [arrays], core_ids=[0])
    return r.results[0]["out"][0:N]
```

```python
from contextlib import ExitStack

import concourse.bass as bass
from concourse import mybir

F32, I32, BF16 = mybir.dt.float32, mybir.dt.int32, mybir.dt.bfloat16
ALU = mybir.AluOpType
ACT = mybir.ActivationFunctionType
AX = mybir.AxisListType.X

N, D, E = 3125, 256, 53125
K, R = 4, 16
KR = K * R
HC = 32
NX, H = 8, 512
KV_TRIPS = 2
T, P = 25, 125
GT = 5
NG = T // GT
GC = GT * P
CUTS = ((0, 3 * P), (3 * P, GC))
EC = 416
EP = 128 * EC
JB = 26
JC = JB + 1
NB = EC // JB
GB = 4
NI = NB // GB
assert 1 + 2 * KV_TRIPS == NG and NI == KV_TRIPS + 2
BX = 128
XB = (2 * N + NX * (BX - 1)) // BX
XQ = 4
XI = XB // XQ
assert XI * XQ == XB
TX = T * NX
SW = KR + 2 * K
SK = KR + K
LN_EPS, BIG = 1e-5, 1e30
ETA_LAM = 0.5 * 0.1
EDGE_STEPS = 9 * GB
FULL = EC * 127


class Steps:

    def __init__(self, engine, sem):
        self.engine, self.sem, self.base, self.local = engine, sem, 0, 0
        self.reg, self.per = None, 0

    def __call__(self, instruction):
        instruction.then_inc(self.sem, 1)
        self.local += 1

    def value(self):
        if self.reg is None:
            return self.base + self.local
        return self.reg * self.per + (self.base + self.local)

    def settle(self):
        self.engine.wait_ge(self.sem, self.value())

    def enter(self, reg, per, first=0):
        self.base += self.local - first * per
        self.reg, self.per, self.local = reg, per, 0

    def leave(self, end):
        assert self.local == self.per, f"steps of a trip: {self.local}, not {self.per}"
        self.base += end * self.per
        self.reg, self.local = None, 0


def program(nc, a, out):
    zu_t = nc.dram_tensor("zu_t", (N, KR), F32, kind="Internal").ap()
    zd_t = nc.dram_tensor("zd_t", (EP + 128 * T, KR), F32, kind="Internal").ap()
    st_t = nc.dram_tensor("st_t", (EP, SW), F32, kind="Internal").ap()
    xt_t = nc.dram_tensor("xt_t", (N + 128, SW), F32, kind="Internal").ap()
    z_t = nc.dram_tensor("z_t", (N, D), F32, kind="Internal").ap()
    with ExitStack() as ctx:
        build(nc, ctx, a, out, zu_t, zd_t, st_t, xt_t, z_t)


def build(nc, ctx, a, out, zu_t, zd_t, st_t, xt_t, z_t):
    def sb(name, shape, dt=F32):
        return ctx.enter_context(nc.sbuf_tensor(name, shape, dt))

    def sem(name):
        return ctx.enter_context(nc.semaphore(name))

    def cutter(ap):
        at = [0]

        def take(*shape, dt=F32, rows=128):
            size = 1
            for n in shape:
                size *= n
            size = size // 2 if dt is BF16 else size
            view = ap[0:rows, at[0]:at[0] + size]
            at[0] += size
            assert at[0] <= ap.shape[1], (at[0], ap.shape)
            if dt is not F32:
                view = view.bitcast(dt)
            if len(shape) == 2:
                view = view.rearrange("p (a b) -> p a b", a=shape[0])
            if len(shape) == 3:
                view = view.rearrange("p (a b c) -> p a b c", a=shape[0], b=shape[1])
            return view
        return take

    x_sb = sb("x_sb", [128, T, D])
    xnT = sb("xnT", [128, NG, GT * D])
    mix_sb = xnT
    gx = sb("gx", [128, T, D])
    xn_flat = xnT[:, :, :].rearrange("p g c -> p (g c)")
    gx_flat = gx[:, :, :].rearrange("p t d -> p (t d)")
    edge = sb("edge", [128, GB * JB * KR + JB * KR + 2 * JC * KR + 2 * JC * SK + 2 * JB * SW])
    take = cutter(edge)
    G = [take(JB, KR) for _ in range(GB)]
    zraw = take(JB, KR)
    zt, keep = take(KR, JC), take(KR, JC)
    wt, decay = take(SK, JC), take(SK, JC)
    so = [take(JB, SW) for _ in (0, 1)]
    zt_f, keep_f, wt_f, decay_f = (v.rearrange("p f j -> p (f j)") for v in (zt, keep, wt, decay))
    take = cutter(edge[:, GB * JB * KR + JB * KR:])
    one_p = [take(JB, P, dt=BF16) for _ in (0, 1)]
    one_t = [take(JB, T + 1, dt=BF16) for _ in (0, 1)]
    take = cutter(edge)
    W1, W2 = take(NX, 2, H), take(NX, 4, D)
    stage = sb("stage", [128, GT, D])
    stage_flat = stage[:, :, :].rearrange("p a c -> p (a c)")
    xT_st = sb("xT_st", [128, 2, GC])
    xT_flat = xT_st[:, :, :].rearrange("p a c -> p (a c)")
    pools = sb("pools", [128, 4128])
    take = cutter(pools[:, 0:2072])
    kh, vh = take(4, 2, 129), take(4, D)
    mixh = pools[:, 0:2 * GC].rearrange("p (m c) -> p m c", m=2)
    ng = pools[:, 0:T * SW].rearrange("p (t f) -> p t f", f=SW)
    take = cutter(pools[:, 1032:2072])
    dm, wq = take(2, D), take(2, D)
    take = cutter(pools[:, 2072:])
    zu_sb = take(T, KR)
    take = cutter(pools[:, 2072:])
    xc = take(T, SW)
    kvs, sk = take(128), take(128)
    row = pools[0:1, 2072:2072 + 5 * 128].rearrange("p (r c) -> p r c", r=5)
    b1row = pools[:, 0:NX * H].rearrange("p (e m) -> p e m", e=NX)
    take = cutter(stage_flat)
    sq = take(2, 2 * D)
    take = cutter(stage_flat)
    kva, kvc, t1 = take(2, 129), take(2, 128), take(2, D)
    take = cutter(stage_flat)
    fin, carry = take(2 * SK), take(SW)
    q = [take(129, rows=SK) for _ in range(7)]
    take = cutter(xT_flat)
    nm, nden, nden2 = (take(GT, K) for _ in range(3))
    nw = take(2, GT * K)
    src_ix, dst_ix = sb("src_ix", [128, EC], I32), sb("dst_ix", [128, EC], I32)
    idxst = [sb(f"idxst{h}", [128, JB], I32) for h in range(GB)]
    ns = sb("ns", [128, EC])
    take = cutter(gx_flat)
    dstf, dq, dr, df, dfi = take(EC), take(EC), take(EC), take(EC), take(EC, dt=I32)
    iota_p, iota_t, dtd = take(P), take(T + 1), take(2, D)
    zeros = take(JB * KR)
    ident, ones, zero = sb("ident", [128, 128]), sb("ones", [128, 128]), sb("zero", [128, 384])
    blockd, tri = sb("blockd", [128, 128]), sb("tri", [128, 128])
    eps, steps_b, shrink = sb("eps", [128, 1]), sb("steps_b", [128, T]), sb("shrink", [128, 1])
    st, mv = sb("st", [128, 2 * GT, 6]), sb("mv", [128, T, 2])
    std, rstd = sb("std", [128, T]), sb("rstd", [128, T])
    std2, fac = sb("std2", [128, T]), sb("fac", [128, T])
    NR = 10
    rows, cols = sb("rows", [NR, 128]), sb("cols", [128, NR])
    MB1, BQ, GAM, BET, VG, VB = 0, 2, 4, 6, 8, 9
    wqT = sb("wqT", [128, 2, D])
    wkv = sb("wkv", [128, 2, 2 * D])
    cm = sb("cm", [128, 32])
    w1, w2 = sb("w1", [128, 2, D]), sb("w2", [128, 2, D])
    lines = sb("lines", [128, 2 * D + 16])
    rowi = lines[0:1, 0:256].bitcast(I32).rearrange("p (r c) -> p r c", r=2)
    dump_row = lines[0:1, 256:384]
    kvb, cmb, mb2 = lines[32:33, 0:2 * D], lines[32:33, 2 * D:2 * D + 16], lines[64:65, 0:D]
    gh = sb("gh", [128, 2, D])
    u_sb, ug = sb("u_sb", [128, 2, KR]), sb("ug", [64, D])
    hw, hwo, hws = sb("hw", [64, K]), sb("hwo", [64, 1]), sb("hws", [64, 4])
    kgr, kbr = sb("kgr", [128, 128]), sb("kbr", [128, 128])
    wr, brr = sb("wr", [128, 2, NX]), sb("brr", [128, NX])
    csb, ends = sb("csb", [128, T + 1]), sb("ends", [128, T])
    start, full, nid = sb("start", [128, T]), sb("full", [128, T]), sb("nid", [128, T])
    tmpn = sb("tmpn", [128, T])
    sidx, gidx = sb("sidx", [128, T], I32), sb("gidx", [128, T], I32)
    kss, kstd, krs = sb("kss", [128, 2, 16]), sb("kstd", [128, 2, 16]), sb("krs", [128, 2, 16])
    weff, beff = w1, sb("beff", [128, 2])
    zlast = sb("zlast", [128, KR])
    take = cutter(dst_ix[:, :].bitcast(F32))
    lg, mx, negx = (take(K, JC) for _ in range(3))
    lg_f, mx_f, negx_f = (v.rearrange("p k j -> p (k j)") for v in (lg, mx, negx))
    d1, d2 = sb("d1", [128, K, JB]), sb("d2", [128, K, JB])
    take = cutter(wkv[:, :, :].rearrange("p k c -> p (k c)"))
    rl, rt = take(T, NX), take(T, NX)
    rm = take(2, T)
    rf, rd, rp = take(T, 2), take(T), take(2, T)
    tgt = sb("tgt", [128, 1], I32)
    take = cutter(xn_flat)
    acc = [take(GT, D) for _ in (0, 1)]
    agg_c = take(GT, KR)
    agg_st = [take(GT, KR) for _ in (0, 1)]
    aggT = [take(GC, rows=64) for _ in (0, 1)]
    stages = (stage, gx[:, 0:GT, :])
    iota8 = sb("iota8", [128, NX])
    iota_lo, iota_b = sb("iota_lo", [128, BX]), sb("iota_b", [128, XB])
    nid1, dump = sb("nid1", [128, T]), sb("dump", [128, 1])
    take = cutter(xn_flat)
    ch0, ch1, chs, tot, rank, excl = (take(NX, T) for _ in range(6))
    slot, shi, slo, sfx = (take(2, T) for _ in range(4))
    sint = take(2, T, dt=I32)
    nblk, bend, bstart = take(NX), take(NX), take(NX)
    cmpb, cmpx = take(NX, T), take(XB, NX)
    b2row = take(NX, D)
    take = cutter(gx_flat)
    oh_lo, oh_v = [], []
    for _ in (0, 1):
        oh_lo.append(take(2, GT, BX))
        oh_v.append(take(2, GT, 2 * XB))
    take = cutter(wqT[:, :, :].rearrange("p k c -> p (k c)"))
    sid, sw, sfill, spos = take(XB), take(XB), take(XB), take(XB)
    gix, six, eix = take(XB + XQ, dt=I32), take(XB, dt=I32), take(XB, dt=I32)
    gst = [sb(f"gst{h}", [128, 1], I32) for h in range(XQ)]
    sst = [sb(f"sst{h}", [128, 1], I32) for h in range(XQ)]
    take = cutter(gx_flat)
    xg, xb = [take(D) for _ in range(XQ)], [take(2, BX) for _ in (0, 1)]
    hb, hT = [take(H) for _ in (0, 1)], [take(4, BX) for _ in (0, 1)]
    yb = [take(D) for _ in range(XQ)]

    ps = [ctx.enter_context(nc.psum_tensor(f"ps{i}", [128, 512], F32)) for i in range(8)]
    AHEAD = 3
    xT_ps = [ps[b][:, 0:2 * P].rearrange("p (k c) -> p k c", k=2) for b in (0, 1, 4, 5, 6)]
    kv_ps = [ps[b] for b in (0, 1, 4, 0, 1)]
    gx_ps = [ps[b][:, 0:D] for b in (2, 3, 5, 2, 3)]
    y_ps = [ps[b][:, 0:D] for b in (0, 1, 2, 3, 0)]
    zT_ps = [[ps[b][:, 0:P] for b in banks] for banks in ((0, 1, 2, 0, 1), (3, 4, 6, 3, 4))]
    mo_ps = [ps[b][:, 0:D] for b in (4, 5, 6, 7, 4)]

    yb_step = sem("yb_step")
    zfirst_in = sem("zfirst_in")
    kr_step, counted_block, y_used, cr_done, kv_summed = (
        sem("kr_step"), sem("counted_block"), sem("y_used"), sem("cr_done"), sem("kv_summed"))
    e_weight = sem("e_weight")
    x_added, xnT_ready, zT_act, relu_ready = sem("x_added"), sem("xnT_ready"), sem("zT_act"), sem("relu_ready")
    slot_known, oh_pool, oh_blocks = sem("slot_known"), sem("oh_pool"), sem("oh_blocks")
    z_outs = (sem("z_out0"), sem("z_out1"))
    x_in = [sem(f"x_in{g}") for g in range(NG)]
    u_in, edges_in, w_in, xw_in = sem("u_in"), sem("edges_in"), sem("w_in"), sem("xw_in")
    consts = sem("consts")
    pool_step, dve_step, act_step = sem("pool_step"), sem("dve_step"), sem("act_step")
    stats, stds = sem("stats"), sem("stds")
    xn_ready, xT_psum, xT_ready = sem("xn_ready"), sem("xT_psum"), sem("xT_ready")
    zu_psum, zu_ready, zu_stored = sem("zu_psum"), sem("zu_ready"), sem("zu_stored")
    zeroed, zeros_out = sem("zeroed"), sem("zeros_out")
    onehot, counted, counts_sb, based = sem("onehot"), sem("counted"), sem("counts_sb"), sem("based")
    places = sem("places")
    rows_psum, cols_ready = sem("rows_psum"), sem("cols_ready")
    wqT_psum, wqT_ready, dtd_psum, dtd_ready = sem("wqT_psum"), sem("wqT_ready"), sem("dtd_psum"), sem("dtd_ready")
    b_psum, gh_ready, ug_psum, hw_ready, hwe_ready, ug_ready = (
        sem("b_psum"), sem("gh_ready"), sem("ug_psum"), sem("hw_ready"), sem("hwe_ready"), sem("ug_ready"))
    wkv_ready = sem("wkv_ready")
    kx_ready, kv_psum, gx_psum, gx_ready = sem("kx_ready"), sem("kv_psum"), sem("gx_psum"), sem("gx_ready")
    sq_ready, ss_ready, ks_ready, kv_ready, kv_used = (
        sem("sq_ready"), sem("ss_ready"), sem("ks_ready"), sem("kv_ready"), sem("kv_used"))
    kvt_ready, t1_psum, t1_ready, we_psum, we_ready = (
        sem("kvt_ready"), sem("t1_psum"), sem("t1_ready"), sem("we_psum"), sem("we_ready"))
    mh_psum, mh_ready, mo_psum, mo_ready = sem("mh_psum"), sem("mh_ready"), sem("mo_psum"), sem("mo_ready")
    zd_scattered, zd_in, zraw_free = sem("zd_scattered"), sem("zd_in"), sem("zraw_free")
    g_in, g_free = [sem(f"g_in{h}") for h in range(GB)], [sem(f"g_free{h}") for h in range(GB)]
    fill_init, fill_ready, e_diff, e_exp = sem("fill_init"), sem("fill_ready"), sem("e_diff"), sem("e_exp")
    summed, so_ready, s_out = sem("summed"), sem("so_ready"), [sem("s_out0"), sem("s_out1")]
    fin_ready, fin_psum, q_ready, q_exp, cr_ready, cr_psum, cr_sb, cr_out = (
        sem("fin_ready"), sem("fin_psum"), sem("q_ready"), sem("q_exp"), sem("cr_ready"), sem("cr_psum"),
        sem("cr_sb"), sem("cr_out"))
    row_ready, row_psum, xt_init_ready, xt_init = sem("row_ready"), sem("row_psum"), sem("xt_init_ready"), sem("xt_init")
    ng_in = [sem(f"ng_in{g}") for g in range(NG)]
    xc_in, merge_d, merge_e = sem("xc_in"), sem("merge_d"), sem("merge_e")
    agg_ready, agg_psum, aggT_ready, y_psum, x2_ready = (
        sem("agg_ready"), sem("agg_psum"), sem("aggT_ready"), sem("y_psum"), sem("x2_ready"))
    stats2, stds2, z_ready, zT_psum, zT_ready = sem("stats2"), sem("stds2"), sem("z_ready"), sem("zT_psum"), sem("zT_ready")
    x2_out = sem("x2_out")
    r_psum, r_read, r_diff, r_exp = sem("r_psum"), sem("r_read"), sem("r_diff"), sem("r_exp")
    nodes_done, b1_in, b2_in = sem("nodes_done"), sem("b1_in"), sem("b2_in")
    choices, ranked_psum, oh_ready, oh_used, slots_psum, slots_ready = (
        sem("choices"), sem("ranked_psum"), sem("oh_ready"), sem("oh_used"), sem("slots_psum"), sem("slots_ready"))
    xg_in = [sem(f"xg_in{h}") for h in range(XQ)]
    xg_psum, xb_ready, h_psum, hb_ready, hg_ready, hT_psum, hT_ready, ye_psum, yb_ready, added = (
        sem("xg_psum"), sem("xb_ready"), sem("h_psum"), sem("hb_ready"), sem("hg_ready"), sem("hT_psum"),
        sem("hT_ready"), sem("ye_psum"), sem("yb_ready"), sem("added"))

    x_v = a["x"].rearrange("(p t) d -> p t d", t=T)
    out_v = out[0:N, :].rearrange("(p t) d -> p t d", t=T)
    z_v = z_t.rearrange("(p t) d -> p t d", t=T)
    zu_v = zu_t.rearrange("(p t) f -> p t f", t=T)
    zd_v = zd_t[0:EP, :].rearrange("(p j) f -> p j f", j=EC)
    st_v = st_t.rearrange("(p j) f -> p j f", j=EC)
    xt_v = xt_t[0:N, :].rearrange("(p t) f -> p t f", t=T)
    w_qkv = a["L0_mix_w_qkv"].rearrange("(k c) (h m) -> k c h m", k=2, m=3 * HC)
    b_qkv = a["L0_mix_b_qkv"].rearrange("(a h m) -> a h m", a=1, m=3 * HC)
    SPLIT = ((0, 112), (112, P))

    tables = sb("tables", [128, 10])
    spare2 = sb("spare2", [128, 2])
    spare = {name: sb(f"spare_{name}", [128, 1]) for name in ("dve", "pool")}

    def held(engine):
        if engine is nc.vector:
            nc.vector.memset(spare["dve"][:, :], 0.0)
        else:
            nc.gpsimd.tensor_tensor(spare["pool"][:, :], eps[:, :], eps[:, :], ALU.add)

    W_LOADS = []
    EARLY_BUFFERS = GB - 1
    EARLY = EARLY_BUFFERS * JB * KR // (2 * H)

    def load_w1(queue, k, first, last):
        queue.dma_start(W1[:, first:last, k, :],
                        a["L0_ffn_W1"][first:last, k * 128:(k + 1) * 128, :].rearrange("e c m -> c e m")).then_inc(xw_in, 16)

    def load_w2(queue, k):
        queue.dma_start(W2[:, :, k, :], a["L0_ffn_W2"][:, k * 128:(k + 1) * 128, :].rearrange("e c m -> c e m")).then_inc(xw_in, 16)

    block = ctx.enter_context(nc.Block())

    @block.sync
    def _(sp):
        for g in range(NG):
            for lo, hi in SPLIT:
                sp.dma_start(x_sb[lo:hi, g * GT:(g + 1) * GT, :], x_v[lo:hi, g * GT:(g + 1) * GT, :]).then_inc(x_in[g], 16)
        for k in range(2):
            sp.dma_start(u_sb[:, k, :].rearrange("c (h r) -> c h r", h=K),
                         a["L0_gnn_U"][:, k * 128:(k + 1) * 128, :].rearrange("h c r -> c h r")).then_inc(u_in, 16)

        def load(dst, src):
            sp.dma_start(dst, src).then_inc(w_in, 16)
            W_LOADS.append(1)

        for k in range(2):
            load(dm[:, k, :], a["L0_gnn_Dmat"][k * 128:(k + 1) * 128, :])
            load(wq[:, k, :].rearrange("c (h m) -> c h m", m=HC), w_qkv[k, :, :, 0:HC])
            for part in (0, 1):
                load(wkv[:, k, part * D:(part + 1) * D].rearrange("c (h m) -> c h m", m=HC),
                     w_qkv[k, :, :, (part + 1) * HC:(part + 2) * HC])
            load(w1[:, k, :], a["L0_mix_w1"][k * 128:(k + 1) * 128, :])
            load(w2[:, k, :], a["L0_mix_w2"][k * 128:(k + 1) * 128, :])
            load(wr[:, k, :], a["L0_ffn_Wr"][k * 128:(k + 1) * 128, :])
        for part in (0, 1):
            load(kvb[:, part * D:(part + 1) * D].rearrange("a (h m) -> a h m", m=HC),
                 b_qkv[:, :, (part + 1) * HC:(part + 2) * HC])
        load(rows[MB1:MB1 + 2, :], a["L0_mix_b1"].rearrange("(m p) -> m p", p=128))
        for k in range(2):
            load(rows[BQ + k:BQ + k + 1, :].rearrange("a (h m) -> a h m", m=HC), b_qkv[:, 4 * k:4 * k + 4, 0:HC])
        load(rows[GAM:GAM + 2, :], a["L0_ffn_gamma"].rearrange("(m p) -> m p", p=128))
        load(rows[BET:BET + 2, :], a["L0_ffn_beta"].rearrange("(m p) -> m p", p=128))
        for r in range(4):
            load(rows[VG:VG + 1, r * HC:(r + 1) * HC], a["L0_mix_vln_g"].rearrange("(a m) -> a m", a=1))
            load(rows[VB:VB + 1, r * HC:(r + 1) * HC], a["L0_mix_vln_b"].rearrange("(a m) -> a m", a=1))
            load(kgr[:, r * HC:(r + 1) * HC], a["L0_mix_kln_g"].partition_broadcast(128))
            load(kbr[:, r * HC:(r + 1) * HC], a["L0_mix_kln_b"].partition_broadcast(128))
        load(mb2, a["L0_mix_b2"].rearrange("(a m) -> a m", a=1))
        load(brr[:, :], a["L0_ffn_br"].partition_broadcast(128))
        load(hw[:, :], a["L0_gnn_head_w"].partition_broadcast(64))
        for k in range(K):
            load(hwo[k * R:(k + 1) * R, :], a["L0_gnn_head_w"][k:k + 1].partition_broadcast(R))
        sp.wait_ge(zu_ready, T + 1)
        for lo, hi in SPLIT:
            sp.dma_start(zu_v[lo:hi, :, :], zu_sb[lo:hi, :, :]).then_inc(zu_stored, 16)
        sp.wait_ge(zeroed, 1)
        for b in range(NB):
            sp.dma_start(zd_v[:, b * JB:(b + 1) * JB, :], zeros.rearrange("p (j f) -> p j f", f=KR)).then_inc(zeros_out, 16)
        sp.wait_ge(zd_scattered, 16 * T)
        sp.wait_ge(fill_init, 1)
        sp.dma_start(zraw, zd_v[:, 0:JB, :]).then_inc(zd_in, 16)
        sp.wait_ge(xt_init_ready, 2)
        for lo, hi in SPLIT:
            sp.dma_start(xt_v[lo:hi, :, :], xc[lo:hi, :, :]).then_inc(xt_init, 16)

        def block_io(i, h, load):
            if load:
                sp.wait_ge(zraw_free, i * GB + (h + 1))
                sp.dma_start(zraw, zd_v[:, bass.ds(i * (GB * JB) + (h + 1) * JB, JB), :]).then_inc(zd_in, 16)
            sp.wait_ge(so_ready, i * GB + (h + 1) + 1)
            sp.dma_start(st_v[:, bass.ds(i * (GB * JB) + h * JB, JB), :], so[h % 2]).then_inc(s_out[h % 2], 16)

        with sp.Fori(0, NI - 1) as i:
            for h in range(GB):
                block_io(i, h, True)
        for h in range(GB):
            block_io(NI - 1, h, h < GB - 1)
            if h == GB - 2:
                for b in range(EARLY_BUFFERS):
                    sp.wait_ge(g_free[b], NI)
                load_w1(sp, 0, 0, EARLY)
                load_w1(sp, 1, 0, EARLY)
        sp.wait_ge(cr_out, 16)
        for lo, hi in SPLIT:
            sp.dma_start(xc[lo:hi, :, :], xt_v[lo:hi, :, :]).then_inc(xc_in, 16)
        for g in range(NG):
            sp.wait_ge(x2_ready, GT * (g + 1))
            for lo, hi in SPLIT:
                sp.dma_start(out_v[lo:hi, g * GT:(g + 1) * GT, :], x_sb[lo:hi, g * GT:(g + 1) * GT, :]).then_inc(x2_out, 16)
        for g in range(NG):
            sp.wait_ge(z_ready, GT * (g + 1))
            for lo, hi in SPLIT:
                sp.dma_start(z_v[lo:hi, g * GT:(g + 1) * GT, :], stages[g % 2][lo:hi, :, :]).then_inc(z_outs[g % 2], 16)
        sp.wait_ge(agg_ready, NG)
        sp.dma_start(b1row, a["L0_ffn_b1"].partition_broadcast(128)).then_inc(b1_in, 16)
        sp.wait_ge(nodes_done, 1)
        sp.dma_start(b2row, a["L0_ffn_b2"].partition_broadcast(128)).then_inc(b2_in, 16)
        sp.wait_ge(x2_out, 2 * 16 * NG)
        sp.wait_ge(added, 16 * XB)


    def zu_copy(act, g, t):
        act.wait_ge(zu_psum, g * GT + (GT + t + 1))
        nc.scalar.copy(zu_sb[0:P, g * GT + t, :], ps[2 + t % 2][0:P, 0:KR]).then_inc(zu_ready, 1)

    @block.scalar
    def _(act):
        def load(dst, src, s):
            act.dma_start(dst, src).then_inc(s, 16)

        act.wait_ge(consts, 1)
        load(dst_ix[0:112, :], a["dst"][0:112 * EC].rearrange("(p j) -> p j", j=EC), edges_in)
        load(dst_ix[112:127, :], a["dst"][112 * EC:FULL].rearrange("(p j) -> p j", j=EC), edges_in)

        load(dst_ix[127:128, 0:E - FULL], a["dst"][FULL:E].rearrange("(p j) -> p j", p=1), edges_in)
        load(src_ix[0:112, :], a["src"][0:112 * EC].rearrange("(p j) -> p j", j=EC), edges_in)
        load(src_ix[112:127, :], a["src"][112 * EC:FULL].rearrange("(p j) -> p j", j=EC), edges_in)
        load(src_ix[127:128, 0:E - FULL], a["src"][FULL:E].rearrange("(p j) -> p j", p=1), edges_in)
        with nc.allow_non_contiguous_dma(reason="first and last dst of each partition: 255 words"):
            load(rowi[0:1, 0, :], a["dst"][0:1 + 127 * EC:EC].rearrange("(p j) -> p j", p=1), edges_in)
            load(rowi[0:1, 1, 0:127], a["dst"][EC - 1:FULL:EC].rearrange("(p j) -> p j", p=1), edges_in)
        act.wait_ge(consts, 2)
        for k, (free, count) in enumerate(((xnT_ready, GT), (zu_ready, 1), (gx_ready, 1), (mo_ready, 1), (so_ready, 1),
                                           (s_out[0], 16), (s_out[1], 16))):
            nc.scalar.copy(tables[:, 3 + k:4 + k], eps[:, :]).then_inc(free, count)
        act.wait_ge(stats, 1)
        nc.scalar.activation(std[0:P, :], mv[0:P, :, 1], ACT.Sqrt, bias=eps[0:P, :]).then_inc(stds, 1)
        with act.Fori(0, NG) as g:
            for t in range(GT):
                act.wait_ge(zu_psum, g * GT + (t + 1))
                act.wait_ge(xT_psum, g * GT + (GT + t + 1))
                src = xT_ps[t]
                nc.scalar.copy(xT_st[:, :, t * P:(t + 1) * P], src).then_inc(xT_ready, 1)
                nc.scalar.copy(xnT[:, g, :][:, 0:2 * GC].rearrange("p (k c) -> p k c", k=2)[:, :, t * P:(t + 1) * P],
                               src).then_inc(xnT_ready, 1)
                if t:
                    zu_copy(act, g, t - 1)
            zu_copy(act, g, GT - 1)

        act.wait_ge(rows_psum, 1)
        nc.scalar.copy(cols[:, :], ps[0][:, 0:NR]).then_inc(cols_ready, 1)
        act.wait_ge(wqT_psum, 1)
        nc.scalar.copy(wqT[:, :, :], ps[1][:, :].rearrange("p (k c) -> p k c", k=2)).then_inc(wqT_ready, 1)
        act.wait_ge(dtd_psum, 1)
        nc.scalar.copy(dtd, ps[2][:, :].rearrange("p (k c) -> p k c", k=2)).then_inc(dtd_ready, 1)
        act.wait_ge(hw_ready, 1)
        nc.scalar.activation(hws[:, 0:1], hwo[:, :], ACT.Exp, bias=hws[:, 3:4])
        nc.scalar.activation(hw[:, :], hw[:, :], ACT.Exp, bias=hws[:, 3:4], accum_out=hws[:, 1:2]).then_inc(hwe_ready, 1)

        act.wait_ge(zeros_out, 16 * NB)
        act.wait_ge(counted, 1)
        act.wait_ge(based, 1)
        act.wait_ge(x_added, GT + T)
        act.wait_ge(xT_psum, GT + T)
        def stationary(g, first=False):
            if not first:
                act.wait_ge(gx_psum, g * GT)
            for t in range(GT):
                nc.scalar.copy(xT_st[:, :, t * P:(t + 1) * P],
                               xnT[:, bass.ds(g, 1), :].rearrange("p g c -> p (g c)")[:, 0:2 * GC].rearrange(
                                   "p (k c) -> p k c", k=2)[:, :, t * P:(t + 1) * P]).then_inc(kx_ready, 1)

        def keys_values(g):
            for t in range(GT):
                act.wait_ge(kv_psum, g * GT + (t + 1))
                act.wait_ge(ss_ready, g * GT + (t - 1 if t >= 2 else 0))
                nc.scalar.square(sq[0:P, t % 2, :], kv_ps[t][0:P, :]).then_inc(sq_ready, 1)
                act.wait_ge(gx_psum, g * GT + (t + 1))
                nc.scalar.copy(gx[0:P, g * GT + t, :], gx_ps[t][0:P, :]).then_inc(gx_ready, 1)
                act.wait_ge(ss_ready, g * GT + (t + 1))
                nc.scalar.activation(kstd[0:P, t % 2, :], kss[0:P, t % 2, :], ACT.Sqrt,
                                     bias=eps[0:P, :], scale=1.0 / HC).then_inc(ks_ready, 1)
        stationary(0, True)
        keys_values(0)

        def feature(ap):
            return ap.rearrange("p j f -> p f j")

        def fill(i, h):
            at = bass.ds(i * (GB * JB) + h * JB, JB)
            act.wait_ge(zd_in, i * (16 * GB) + 16 * (h + 1))
            nc.scalar.copy(zt[:, :, 1:JC], feature(zraw)).then_inc(zraw_free, 1)
            nc.scalar.copy(keep[:, :, 1:JC], ns[:, at].unsqueeze(1).broadcast_to([128, KR, JB]))
            nc.scalar.activation(negx[:, :, 1:JC], ns[:, at].unsqueeze(1).broadcast_to([128, K, JB]), ACT.Copy,
                                 scale=BIG, bias=-BIG).then_inc(fill_ready, 1)

        def exps(i, h):
            act.wait_ge(e_diff, i * GB + (h + 1))
            nc.scalar.activation(wt[:, KR:SK, 1:JC], d1[:, :, :], ACT.Exp, scale=0.25).then_inc(e_weight, 1)
            nc.scalar.activation(decay[:, 0:KR, 1:JC].rearrange("p (k r) j -> p k r j", k=K),
                                 d2[:, :, :].unsqueeze(2).broadcast_to([128, K, R, JB]), ACT.Exp, scale=0.25)
            nc.scalar.activation(decay[:, KR:SK, 1:JC], d2[:, :, :], ACT.Exp, scale=0.25).then_inc(e_exp, 1)

        def sums_out(i, h):
            act.wait_ge(summed, i * GB + (h + 1))
            act.wait_ge(s_out[h % 2], i * (8 * GB) + 16 * (h // 2) + 16)
            nc.scalar.copy(feature(so[h % 2][:, :, 0:SK]), wt[:, :, 1:JC])
            nc.scalar.copy(feature(so[h % 2][:, :, SK:SW]), mx[:, :, 1:JC]).then_inc(so_ready, 1)

        def edge_block(i, h, more=True):
            exps(i, h)
            if more:
                fill(i, h + 1)
            sums_out(i, h)

        act.wait_ge(fill_init, 1)
        act.wait_ge(zfirst_in, 16)
        act.wait_ge(zd_in, 16)
        nc.scalar.copy(zraw[:, 0, :], zlast[:, :]).then_inc(act_step, 1)
        act.wait_ge(act_step, 1)
        fill(0, 0)
        def mix_out(g):
            for t in range(GT):
                act.wait_ge(mo_psum, g * GT + (t + 1))
                nc.scalar.copy(mix_sb[0:P, g, t * D:(t + 1) * D], mo_ps[t][0:P, :]).then_inc(mo_ready, 1)

        def mix_hidden(g):
            if g:
                act.wait_ge(mo_psum, g * GT)
            for m in range(2):
                for c, (lo, hi) in enumerate(CUTS):
                    act.wait_ge(mh_psum, g * 4 + (2 * m + c + 1))
                    nc.scalar.activation(mixh[:, m, lo:hi], ps[2 * m + c][:, 0:hi - lo], ACT.Gelu,
                                         bias=beff[:, m:m + 1]).then_inc(mh_ready, 1)

        with act.Fori(0, KV_TRIPS) as i:
            for h in range(GB):
                if h % 2 == 0:
                    stationary(i * 2 + (h // 2 + 1))
                edge_block(i, h)
                if h % 2:
                    keys_values(i * 2 + (h // 2 + 1))
        act.wait_ge(t1_psum, 1)
        nc.scalar.copy(t1, ps[4][:, :].rearrange("p (k c) -> p k c", k=2)).then_inc(t1_ready, 1)
        act.wait_ge(we_ready, 1)
        mix_hidden(0)
        for h in range(2 * GB):
            edge_block(KV_TRIPS + h // GB, h % GB, h < 2 * GB - 1)
            if h < NG:
                mix_out(h)
            if h < NG - 1:
                mix_hidden(h + 1)

        act.wait_ge(q_ready, 1)
        nc.scalar.activation(q[3][:, 0:128], q[3][:, 0:128], ACT.Exp, scale=0.25)
        nc.scalar.activation(q[4][:, 0:128], q[4][:, 0:128], ACT.Exp, scale=0.25).then_inc(q_exp, 1)
        act.wait_ge(cr_psum, 1)
        nc.scalar.copy(carry[:, 0:SK], ps[0][:, 0:SK])
        nc.scalar.copy(carry[:, SK:SW], ps[1][:, KR:SK]).then_inc(cr_sb, 1)
        act.wait_ge(s_out[0], 16 * NB // 2 + 16)
        act.wait_ge(s_out[1], 16 * NB // 2 + 16)
        load_w1(act, 0, EARLY, NX)

        def merge_weights(g):
            act.wait_ge(merge_d, g + 1)
            nc.scalar.activation(nw[0:P, :, :], nw[0:P, :, :], ACT.Exp, scale=0.25).then_inc(merge_e, 1)

        def transposed(g):
            act.wait_ge(agg_psum, g + 1)
            if g >= 2:
                act.wait_ge(y_psum, (g - 1) * GT)
            nc.scalar.copy(aggT[g % 2][:, 0:4 * P], ps[6][0:64, 0:4 * P])
            nc.scalar.copy(aggT[g % 2][:, 4 * P:GC], ps[7][0:64, 0:P]).then_inc(aggT_ready, 1)

        merge_weights(0)
        transposed(0)
        load_w1(act, 1, EARLY, NX)
        merge_weights(1)
        for g in range(NG):
            for t in range(GT):
                act.wait_ge(y_used, g * GT + t + 1)
                nc.scalar.activation(acc[g % 2][0:P, t, :], acc[g % 2][0:P, t, :], ACT.Relu, bias=shrink[0:P, :]).then_inc(relu_ready, 1)
            if g < NG - 1:
                transposed(g + 1)
            if g < NG - 2:
                merge_weights(g + 2)
            if g < 4:
                load_w2(act, g)

        nc.scalar.activation(tables[:, 0:1], eps[:, :], ACT.Sqrt)
        act.wait_ge(cols_ready, 1)
        act.wait_ge(stats2, 1)
        nc.scalar.activation(std[0:P, :], mv[0:P, :, 1], ACT.Sqrt, bias=eps[0:P, :]).then_inc(stds2, 1)
        act.wait_ge(r_read, 1)
        nc.scalar.activation(std2[0:P, :], fac[0:P, :], ACT.Sqrt, bias=eps[0:P, :]).then_inc(stds2, 1)
        for g in range(NG):
            for t in range(GT):
                act.wait_ge(zT_psum, g * GT + t + 1)
                if g:
                    act.wait_ge(r_psum, (g - 1) * GT + t + 1)
                nc.scalar.activation(xT_st[:, 0, t * P:(t + 1) * P], zT_ps[0][t], ACT.Identity,
                                     scale=cols[:, GAM:GAM + 1], bias=cols[:, BET:BET + 1]).then_inc(zT_act, 1)
        nc.scalar.activation(tables[:, 1:2], eps[:, :], ACT.Exp)
        act.wait_ge(r_diff, 1)
        nc.scalar.activation(rd[0:P, :], rd[0:P, :], ACT.Exp).then_inc(r_exp, 1)

        def hidden(i, h):
            act.wait_ge(hb_ready, i * XQ + (h + 1))
            nc.scalar.activation(hb[h % 2], hb[h % 2], ACT.Gelu).then_inc(hg_ready, 1)

        def hidden_T(i, h):
            act.wait_ge(hT_psum, i * XQ + (h + 1))
            nc.scalar.copy(hT[h % 2], ps[4 + h % 2][:, :].rearrange("p (m c) -> p m c", m=4)).then_inc(hT_ready, 1)

        nc.scalar.activation(tables[:, 2:3], eps[:, :], ACT.Gelu)
        hidden(0, 0)
        for h in range(1, XQ):
            hidden(0, h)
            hidden_T(0, h - 1)
        with act.Fori(1, XI) as i:
            for h in range(XQ):
                hidden(i, h)
                hidden_T(i, h - 1)
        hidden_T(XI - 1, XQ - 1)

    @block.gpsimd
    def _(pool):
        step = Steps(pool, pool_step)
        gp = nc.gpsimd
        step(gp.memset(dst_ix[:, :], N))
        step(gp.memset(src_ix[:, :], 0))
        step.settle()
        step(gp.memset(shrink[:, :], -ETA_LAM))
        gp.memset(eps[:, :], LN_EPS).then_inc(consts, 1)
        step(gp.memset(ident[:, :], 0.0))
        gp.memset(zeros, 0.0).then_inc(zeroed, 1)
        step(gp.memset(ones[:, :], 1.0))
        step(gp.memset(zero[:, :], 0.0))
        step.settle()
        step(gp.affine_select(out=ident[:, :], in_=ident[:, :], compare_op=ALU.not_equal, fill=1.0, base=0,
                              pattern=[[-1, 128]], channel_multiplier=1))
        step(gp.affine_select(out=tri[:, :], in_=ones[:, :], compare_op=ALU.is_gt, fill=0.0, base=0,
                              pattern=[[1, 128]], channel_multiplier=-1))
        step(gp.memset(blockd[:, :], 0.0))
        step.settle()
        for b in range(4):
            step(gp.memset(blockd[b * HC:(b + 1) * HC, b * HC:(b + 1) * HC], 1.0 / N))
            step.settle()
        step(gp.iota(iota_p, [[1, P]], base=0, channel_multiplier=0, allow_small_or_imprecise_dtypes=True))
        step(gp.iota(iota_t, [[1, T + 1]], base=0, channel_multiplier=0, allow_small_or_imprecise_dtypes=True))
        step(gp.iota(steps_b[:, :], [[BX, T]], base=0, channel_multiplier=0, allow_small_or_imprecise_dtypes=True))
        step(gp.iota(iota8[:, :], [[1, NX]], base=0, channel_multiplier=0, allow_small_or_imprecise_dtypes=True))
        step(gp.iota(nid[:, :], [[1, T]], base=0, channel_multiplier=T, allow_small_or_imprecise_dtypes=True))
        step.settle()
        step(gp.iota(dump_row, [[1, 128]], base=N, channel_multiplier=0, allow_small_or_imprecise_dtypes=True))
        step.settle()
        step(gp.iota(sidx[:, :], [[1, T]], base=EP, channel_multiplier=T))
        step(gp.memset(gidx[:, :], 0))
        step.settle()
        step(gp.memset(zu_sb[96:128, :, :], 0.0))
        step.settle()
        step(gp.memset(rowi[0:1, 1, 127:128], N))
        step.settle()
        step(gp.iota(iota_lo[:, :], [[1, BX]], base=0, channel_multiplier=0, allow_small_or_imprecise_dtypes=True))
        step(gp.iota(iota_b[:, :], [[1, XB]], base=0, channel_multiplier=0, allow_small_or_imprecise_dtypes=True))
        step(gp.iota(nid1[:, :], [[1, T]], base=1, channel_multiplier=T, allow_small_or_imprecise_dtypes=True))
        step(gp.iota(dump[:, :], [[1, 1]], base=N, channel_multiplier=1, allow_small_or_imprecise_dtypes=True))
        step(gp.memset(kh[:, :, :, 128:129], 1.0))
        step.settle()
        gp.memset(hws[:, :], 0.0).then_inc(consts, 1)

        def gathers(i, h, first):
            if not first:
                pool.wait_ge(g_free[h], i)
            step(gp.tensor_copy(idxst[h][:, :], src_ix[:, bass.ds(i * (GB * JB) + h * JB, JB)]))
            step.settle()
            if not first:
                held(nc.gpsimd)
            for j in range(JB):
                gp.indirect_dma_start(G[h][:, j, :], None, zu_t,
                                      bass.IndirectOffsetOnAxis(ap=idxst[h][:, j:j + 1], axis=0)).then_inc(g_in[h], 16)

        gp.memset(spare["pool"][:, :], 0.0).then_inc(x_added, GT)
        with pool.Fori(0, NG) as g:
            for t in range(GT):
                pool.wait_ge(xn_ready, g * GT + (t + 1))
                gp.tensor_tensor(x_sb[0:P, g * GT + t, :], x_sb[0:P, g * GT + t, :], stage[0:P, t, :], ALU.add).then_inc(x_added, 1)

        pool.wait_ge(edges_in, 8 * 16)
        pool.wait_ge(zu_stored, 2 * 16)
        gp.indirect_dma_start(zlast[:, :], None, zu_t,
                              bass.IndirectOffsetOnAxis(ap=dst_ix[:, 0:1], axis=0)).then_inc(zfirst_in, 16)
        for h in range(GB - 1):
            gathers(0, h, True)
        pool.wait_ge(zeros_out, 16 * NB)
        pool.wait_ge(places, 1)
        for t in range(T):
            gp.indirect_dma_start(zd_t, bass.IndirectOffsetOnAxis(ap=sidx[:, t:t + 1], axis=0),
                                  zu_sb[:, t, :], None).then_inc(zd_scattered, 16)
        gathers(0, GB - 1, True)
        pool.wait_ge(zd_scattered, 16 * T)
        gp.memset(xc[:, :, 0:SK], 0.0).then_inc(xt_init_ready, 1)
        gp.memset(xc[:, :, SK:SW], -BIG).then_inc(xt_init_ready, 1)
        with pool.Fori(1, NI) as i:
            step.enter(i, GB, 1)
            for h in range(GB):
                gathers(i, h, False)
            step.leave(NI)
        pool.wait_ge(s_out[0], 16 * NB // 2 + 16)
        pool.wait_ge(s_out[1], 16 * NB // 2 + 16)
        pool.wait_ge(mo_ready, T + 1)
        for t in range(T):
            if t == 1:
                pool.wait_ge(xt_init, 2 * 16)
                pool.wait_ge(cr_sb, 1)
                pool.wait_ge(cr_ready, 1)
                gp.indirect_dma_start(xt_t, bass.IndirectOffsetOnAxis(ap=tgt[:, 0:1], axis=0), carry[:, :], None).then_inc(cr_out, 16)
            gp.indirect_dma_start(ng[:, t, :], None, st_t,
                                  bass.IndirectOffsetOnAxis(ap=gidx[:, t:t + 1], axis=0)).then_inc(ng_in[t // GT], 16)
        pool.wait_ge(cr_out, 16)

        def rows_in(i, h, first=False):
            if not first:
                pool.wait_ge(xg_psum, i * XQ + (h - XQ + 1))
            step(gp.tensor_copy(gst[h % XQ][:, :], gix[:, bass.ds(i * XQ + h, 1)]))
            step.settle()
            if not first:
                held(nc.gpsimd)
            gp.indirect_dma_start(xg[h % XQ], None, z_t,
                                  bass.IndirectOffsetOnAxis(ap=gst[h % XQ][:, 0:1], axis=0)).then_inc(xg_in[h % XQ], 16)

        def rows_out(i, h):
            step(gp.tensor_copy(sst[h][:, :], six[:, bass.ds(i * XQ + h, 1)]))
            step.settle()
            pool.wait_ge(yb_ready, i * XQ + (h + 1))
            if not isinstance(i, int) or i or h:
                pool.wait_ge(added, i * (16 * XQ) + 16 * h)
            held(nc.gpsimd)
            gp.indirect_dma_start(out, bass.IndirectOffsetOnAxis(ap=sst[h][:, 0:1], axis=0), yb[h], None,
                                  compute_op=ALU.add, bounds_check=N + 127).then_inc(added, 16)

        for g in range(NG):
            for t in range(GT):
                xt = x_sb[0:P, g * GT + t, :]
                pool.wait_ge(relu_ready, g * GT + (t + 1))
                gp.tensor_tensor(xt, acc[g % 2][0:P, t, :], xt, ALU.add).then_inc(x2_ready, 1)

        pool.wait_ge(slot_known, 1)
        for g in range(NG):
            mine = slice(g * GT, (g + 1) * GT)
            for c in (0, 1):
                pool.wait_ge(oh_blocks, 2 * g + c + 1)
                nodes, weights = oh_v[g % 2][0:P, c, :, 0:XB], oh_v[g % 2][0:P, c, :, XB:2 * XB]
                step(gp.tensor_tensor(weights, nodes, rp[0:P, c, mine].unsqueeze(2).broadcast_to([P, GT, XB]), ALU.mult))
                step.settle()
                gp.tensor_tensor(nodes, nodes, nid1[0:P, mine].unsqueeze(2).broadcast_to([P, GT, XB]),
                                 ALU.mult).then_inc(oh_pool, 1)

        pool.wait_ge(slots_ready, 1)
        pool.wait_ge(z_outs[0], 32 * 3)
        pool.wait_ge(z_outs[1], 32 * 2)
        pool.wait_ge(x2_out, 2 * 16 * NG)
        AHEAD_IN = XQ + 2
        for h in range(AHEAD_IN):
            rows_in(0, h, h < XQ)
        for h in range(XQ):
            rows_in(0, h + AHEAD_IN)
            rows_out(0, h)
        with pool.Fori(1, XI - 1) as i:
            step.enter(i, 2 * XQ, 1)
            for h in range(XQ):
                rows_in(i, h + AHEAD_IN)
                rows_out(i, h)
            step.leave(XI - 1)
        for h in range(XQ):
            rows_out(XI - 1, h)
        for h in range(XQ):
            pool.wait_ge(xg_in[h], 16 * (XI + (h < AHEAD_IN - XQ)))
        pool.wait_ge(added, 16 * XB)

    @block.vector
    def _(dve):
        step = Steps(dve, dve_step)
        v = nc.vector

        def bc(ap, shape):
            return ap.broadcast_to(shape)

        for g in range(NG):
            dve.wait_ge(x_in[g], 2 * 16)
            for t in range(g * GT, (g + 1) * GT):
                step(v.bn_stats(st[0:P, t % (2 * GT), :], x_sb[0:P, t, :]))
            step.settle()
            for t in range(g * GT, (g + 1) * GT):
                step(v.bn_aggr(mv[0:P, t, :], st[0:P, t % (2 * GT), :]))
        step.settle()
        v.memset(spare["dve"][:, :], 0.0).then_inc(stats, 1)
        v.memset(spare2[:, 1:2], 0.0).then_inc(kv_ready, 1)
        dve.wait_ge(stds, 1)
        step(v.reciprocal(rstd[0:P, :], std[0:P, :]))
        step.settle()
        with dve.Fori(0, NG) as g:
            for t in range(GT):
                dve.wait_ge(xT_psum, g * GT + (t + 1))
                dve.wait_ge(x_added, g * GT + (t + 1))
                v.tensor_scalar(stage[0:P, t, :], x_sb[0:P, g * GT + t, :], mv[0:P, bass.ds(g * GT + t, 1), 0],
                                rstd[0:P, bass.ds(g * GT + t, 1)], ALU.subtract, ALU.mult).then_inc(xn_ready, 1)

        dve.wait_ge(edges_in, 8 * 16)
        step(v.tensor_copy(dstf, dst_ix[:, :]))
        step(v.memset(ns[:, 0:1], 0.0))
        step.settle()
        step(v.tensor_tensor(ns[:, 1:EC], dstf[:, 1:EC], dstf[:, 0:EC - 1], ALU.is_equal))
        step(v.tensor_scalar(dq, dstf, 1.0 / T, 0.5 / T - 0.5, ALU.mult, ALU.add))
        step.settle()
        step(v.tensor_copy(dfi, dq))
        step.settle()
        step(v.tensor_copy(dq, dfi))
        step.settle()
        step(v.scalar_tensor_tensor(dr, dq, -float(T), dstf, ALU.mult, ALU.add))
        step.settle()
        step(v.tensor_scalar(df, dr, 0.0, None, ALU.is_lt))
        step.settle()
        step(v.tensor_tensor(dq, dq, df, ALU.subtract))
        step(v.scalar_tensor_tensor(dr, df, float(T), dr, ALU.mult, ALU.add))
        step.settle()
        step(v.tensor_scalar(df, dr, float(T), None, ALU.is_ge))
        step.settle()
        step(v.tensor_tensor(dq, dq, df, ALU.add))
        step(v.scalar_tensor_tensor(dr, df, -float(T), dr, ALU.mult, ALU.add))
        step.settle()

        with dve.Fori(0, NB // 2) as i:
            for h in (0, 1):
                dve.wait_ge(counted_block, i * 2 + (h + 1))
                at = bass.ds(i * (2 * JB) + h * JB, JB)
                v.tensor_tensor(one_p[h], bc(iota_p.unsqueeze(1), [128, JB, P]),
                                bc(dq[:, at].unsqueeze(2), [128, JB, P]), ALU.is_equal).then_inc(onehot, 1)
                v.tensor_tensor(one_t[h][:, :, :], bc(iota_t.unsqueeze(1), [128, JB, T + 1]),
                                bc(dr[:, at].unsqueeze(2), [128, JB, T + 1]), ALU.is_ge).then_inc(onehot, 1)

        dve.wait_ge(counted, 1)
        v.tensor_copy(csb[0:P, :], ps[4][0:P, 0:T + 1]).then_inc(counts_sb, 1)
        dve.wait_ge(based, 1)
        dve.wait_ge(counts_sb, 1)
        step(v.tensor_copy(start[0:P, 0:1], ps[5][0:P, 0:1]))
        step.settle()
        step(v.tensor_scalar(ends[0:P, :], csb[0:P, 0:T], start[0:P, 0:1], None, ALU.add))
        step.settle()
        step(v.tensor_copy(start[0:P, 1:T], ends[0:P, 0:T - 1]))
        step.settle()
        step(v.tensor_tensor(full[0:P, :], ends[0:P, :], start[0:P, :], ALU.is_gt))
        step(v.tensor_tensor(tmpn[0:P, :], start[0:P, :], nid[0:P, :], ALU.subtract))
        step(v.tensor_scalar(gidx[0:P, :], ends[0:P, :], -1.0, 0.0, ALU.add, ALU.max))
        step.settle()
        step(v.tensor_scalar(tmpn[0:P, :], tmpn[0:P, :], -float(EP), None, ALU.add))
        step.settle()
        step(v.tensor_tensor(tmpn[0:P, :], tmpn[0:P, :], full[0:P, :], ALU.mult))
        step.settle()
        step(v.scalar_tensor_tensor(tmpn[0:P, :], tmpn[0:P, :], float(EP), nid[0:P, :], ALU.add, ALU.add))
        step.settle()
        v.tensor_copy(sidx[0:P, :], tmpn[0:P, :]).then_inc(places, 1)

        dve.wait_ge(w_in, 16 * len(W_LOADS))
        k4 = wkv[:, :, :].rearrange("c k (h m) -> c (k h) m", m=HC)
        b4 = kvb[:, :].rearrange("c (h m) -> c h m", m=HC)
        step(v.tensor_reduce(cm[:, :], k4, AX.X, ALU.add))
        step(v.tensor_reduce(cmb, b4, AX.X, ALU.add))
        step(v.tensor_reduce(hws[:, 2:3], hw[:, :], AX.X, ALU.max))
        step.settle()
        step(v.tensor_scalar(cm[:, :], cm[:, :], 1.0 / HC, None, ALU.mult))
        step(v.tensor_scalar(cmb, cmb, 1.0 / HC, None, ALU.mult))
        v.tensor_scalar(hws[:, 3:4], hws[:, 2:3], -1.0, None, ALU.mult).then_inc(hw_ready, 1)
        step.settle()
        v.tensor_tensor(k4, k4, bc(cm[:, :].unsqueeze(2), [128, 32, HC]), ALU.subtract).then_inc(wkv_ready, 1)
        v.tensor_tensor(b4, b4, bc(cmb.unsqueeze(2), [1, 16, HC]), ALU.subtract).then_inc(wkv_ready, 1)
        dve.wait_ge(b_psum, 1)
        step(v.tensor_tensor(gh[:, :, :], dm[:, :, :], ps[3][:, :].rearrange("p (k c) -> p k c", k=2), ALU.subtract))
        step.settle()
        step(v.tensor_scalar(gh[:, :, :], gh[:, :, :], 0.25, None, ALU.mult))
        step.settle()
        for k in range(2):
            d = gh[:, k, k * 128:(k + 1) * 128]
            v.scalar_tensor_tensor(d, ident[:, :], 0.5, d, ALU.mult, ALU.add).then_inc(gh_ready, 1)
        dve.wait_ge(hwe_ready, 1)
        step(v.reciprocal(hws[:, 2:3], hws[:, 1:2]))
        step.settle()
        step(v.tensor_tensor(hws[:, 3:4], hws[:, 0:1], hws[:, 2:3], ALU.mult))
        step.settle()
        dve.wait_ge(ug_psum, 1)
        v.tensor_scalar(ug[:, :], ps[7][0:64, 0:D], hws[:, 3:4], None, ALU.mult).then_inc(ug_ready, 1)

        def keys_values(g):
            for t in range(GT):
                dve.wait_ge(sq_ready, g * GT + (t + 1))
                v.tensor_reduce(kss[0:P, t % 2, :], sq[0:P, t % 2, :].rearrange("p (h m) -> p h m", m=HC),
                                AX.X, ALU.add).then_inc(ss_ready, 1)
                dve.wait_ge(ks_ready, g * GT + (t + 1))
                step_kr = v.reciprocal(krs[0:P, t % 2, :], kstd[0:P, t % 2, :])
                step_kr.then_inc(kr_step, 1)
                dve.wait_ge(kr_step, g * GT + (t + 1))
                dve.wait_ge(kv_used, g * GT + (t - 3 if t >= 4 else 0))
                k_ps = kv_ps[t][0:P, 0:D].rearrange("p (a h m) -> p a h m", a=2, m=HC)
                r_ap = krs[0:P, t % 2, :]
                for hg in (0, 1):
                    v.tensor_tensor(kh[0:P, t % 4, hg, 0:128].rearrange("p (h m) -> p h m", m=HC), k_ps[:, hg],
                                    bc(r_ap[:, 4 * hg:4 * hg + 4].unsqueeze(2), [P, 4, HC]), ALU.mult).then_inc(kv_ready, 1)
                v.tensor_tensor(vh[0:P, t % 4, :].rearrange("p (h m) -> p h m", m=HC),
                                kv_ps[t][0:P, D:2 * D].rearrange("p (h m) -> p h m", m=HC),
                                bc(r_ap[:, 8:16].unsqueeze(2), [P, 8, HC]), ALU.mult).then_inc(kv_ready, 1)

        def edges(i, h):
            n = i * GB + (h + 1)
            dve.wait_ge(fill_ready, n)
            step(v.tensor_tensor_scan(zt_f, keep_f, zt_f, 0.0, ALU.mult, ALU.add))
            dve.wait_ge(g_in[h], i * (16 * JB) + 16 * JB)
            dve.wait_ge(so_ready, i * GB + h + 1)
            step.settle()
            step(v.tensor_tensor(wt[:, 0:KR, 1:JC], G[h].rearrange("p j f -> p f j"), zt[:, :, 1:JC], ALU.mult))
            step(v.tensor_copy(zt[:, :, 0:1], zt[:, :, JB:JC]))
            step.settle()
            step(v.tensor_reduce(lg[:, :, 1:JC], wt[:, 0:KR, 1:JC].rearrange("p (k r) j -> p k j r", k=K), AX.X, ALU.add))
            step.settle()
            step(v.tensor_tensor_scan(mx_f, negx_f, lg_f, 0.0, ALU.add, ALU.max))
            step.settle()
            step(v.tensor_tensor(d2[:, :, :], mx[:, :, 0:JB], mx[:, :, 1:JC], ALU.subtract))
            step(v.tensor_tensor(d1[:, :, :], lg[:, :, 1:JC], mx[:, :, 1:JC], ALU.subtract))
            step.settle()
            v.tensor_tensor(d2[:, :, :], d2[:, :, :], negx[:, :, 1:JC], ALU.add).then_inc(e_diff, 1)
            step(v.tensor_copy(lg[:, :, 0:1], mx[:, :, JB:JC]))
            dve.wait_ge(e_weight, n)
            v.tensor_tensor(wt[:, 0:KR, 1:JC].rearrange("p (k r) j -> p k r j", k=K),
                            G[h].rearrange("p j (k r) -> p k r j", k=K),
                            bc(wt[:, KR:SK, 1:JC].unsqueeze(2), [128, K, R, JB]), ALU.mult).then_inc(g_free[h], 1)
            dve.wait_ge(g_free[h], i + 1)
            dve.wait_ge(e_exp, n)
            v.tensor_tensor_scan(wt_f, decay_f, wt_f, 0.0, ALU.mult, ALU.add).then_inc(summed, 1)
            dve.wait_ge(summed, n)
            step(v.tensor_copy(wt[:, :, 0:1], wt[:, :, JB:JC]))

        dve.wait_ge(zfirst_in, 16)
        for ap in (zt[:, :, 0:1], keep[:, :, 0:1], wt[:, :, 0:1], decay[:, :, 0:1], lg[:, :, 0:1]):
            step(v.memset(ap, 0.0))
        v.memset(negx[:, :, 0:1], -BIG).then_inc(fill_init, 1)
        keys_values(0)
        with dve.Fori(0, KV_TRIPS) as i:
            step.enter(i, EDGE_STEPS)
            for h in range(GB):
                edges(i, h)
                if h % 2:
                    keys_values(i * 2 + (h // 2 + 1))
            step.leave(KV_TRIPS)

        dve.wait_ge(kv_summed, 1)
        dve.wait_ge(cols_ready, 1)
        for hg in (0, 1):
            step(v.tensor_copy(kva[:, hg, :], ps[6 + hg][:, 0:129]))
            step(v.tensor_copy(sk[:, :], ps[6 + hg][:, 256:384]))
            step.settle()
            step(v.tensor_tensor(kvs[:, :], kva[:, hg, 0:128], kgr[:, :], ALU.mult))
            step(v.tensor_tensor(sk[:, :], sk[:, :], kgr[:, :], ALU.mult))
            step.settle()
            step(v.scalar_tensor_tensor(kvs[:, :], kbr[:, :], kva[:, hg, 128:129], kvs[:, :], ALU.mult, ALU.add))
            step(v.scalar_tensor_tensor(sk[:, :], kbr[:, :], float(N), sk[:, :], ALU.mult, ALU.add))
            step.settle()
            step(v.tensor_scalar(sk[:, :], sk[:, :], cols[:, VB:VB + 1], None, ALU.mult))
            step.settle()
            step(v.scalar_tensor_tensor(kvs[:, :], kvs[:, :], cols[:, VG:VG + 1], sk[:, :], ALU.mult, ALU.add))
            step.settle()
            v.tensor_tensor(kvc[:, hg, :], kvs[:, :], blockd[:, :], ALU.mult).then_inc(kvt_ready, 1)
            dve.wait_ge(kvt_ready, hg + 1)
        dve.wait_ge(we_psum, 1)
        w_ps = ps[5][:, :].rearrange("p (k c) -> p k c", k=2)
        step(v.tensor_tensor(weff[:, :, :], w1[:, :, :], w_ps, ALU.add))
        step.settle()
        v.tensor_tensor(beff[:, :], ps[4][:, 0:2], cols[:, MB1:MB1 + 2], ALU.add).then_inc(we_ready, 1)

        dve.wait_ge(xt_init, 2 * 16)
        F_, L_, C_, SAME, GO = range(5)
        step(v.tensor_copy(row[0:1, F_, :], rowi[0:1, 0, :]))
        step(v.tensor_copy(row[0:1, L_, :], rowi[0:1, 1, :]))
        step(v.memset(row[0:1, C_, 0:1], 0.0))
        step.settle()
        step(v.tensor_tensor(row[0:1, C_, 1:128], row[0:1, L_, 0:127], row[0:1, F_, 1:128], ALU.is_equal))
        step(v.tensor_tensor(row[0:1, SAME, :], row[0:1, F_, :], row[0:1, L_, :], ALU.is_equal))
        step.settle()
        step(v.memset(row[0:1, L_, 127:128], 0.0))
        step(v.tensor_tensor(row[0:1, GO, :], row[0:1, C_, :], row[0:1, SAME, :], ALU.mult))
        step(v.tensor_tensor(row[0:1, L_, 0:127], row[0:1, SAME, 0:127], row[0:1, C_, 1:128], ALU.mult))
        step(v.tensor_tensor(row[0:1, F_, :], row[0:1, F_, :], dump_row, ALU.subtract))
        step.settle()
        step(v.tensor_scalar(row[0:1, L_, :], row[0:1, L_, :], -1.0, 1.0, ALU.mult, ALU.add))
        step.settle()
        step(v.tensor_tensor(row[0:1, L_, :], row[0:1, L_, :], row[0:1, C_, :], ALU.mult))
        step.settle()
        step(v.tensor_tensor(row[0:1, F_, :], row[0:1, F_, :], row[0:1, L_, :], ALU.mult))
        step.settle()
        v.tensor_tensor(row[0:1, F_, :], row[0:1, F_, :], dump_row, ALU.add).then_inc(row_ready, 1)
        dve.wait_ge(row_psum, 1)
        step(v.tensor_copy(q[0][:, 0:128], ps[6][0:SK, 0:128]))
        v.tensor_copy(tgt[:, :], ps[7][:, 0:1]).then_inc(cr_ready, 1)

        for h in range(2 * GB):
            edges(KV_TRIPS + h // GB, h % GB)
            if h == GB + 1:
                dve.wait_ge(mo_ready, T + 1)
            if h in (GB + 1, GB + 2):
                for g in range(NG)[h - GB - 1::2]:
                    step(v.tensor_tensor(x_sb[0:P, g * GT:(g + 1) * GT, :].rearrange("p t d -> p (t d)"),
                                         x_sb[0:P, g * GT:(g + 1) * GT, :].rearrange("p t d -> p (t d)"),
                                         mix_sb[0:P, g, :], ALU.add))
        step.settle()

        step(v.tensor_copy(fin[:, 0:SK], wt[:, :, 0]))
        step(v.tensor_copy(fin[:, SK:SK + KR].rearrange("p (k r) -> p k r", r=R), bc(lg[:, :, 0:1], [128, K, R])))
        step(v.tensor_copy(fin[:, SK + KR:2 * SK], lg[:, :, 0]))
        step.settle()
        v.memset(q[6][:, 0:1], 0.0).then_inc(fin_ready, 1)
        dve.wait_ge(fin_psum, 1)
        step(v.tensor_copy(q[1][:, 0:128], ps[0][0:SK, 0:128]))
        step(v.tensor_copy(q[2][:, 0:128], ps[0][0:SK, 128:256]))
        step.settle()
        step(v.tensor_scalar(q[5][:, 0:128], q[0][:, 0:128], -1.0, BIG, ALU.add, ALU.mult))
        step(v.memset(q[6][:, 0:1], 0.0))
        step.settle()
        step(v.tensor_tensor_scan(q[6][:, 1:129], q[5][:, 0:128], q[2][:, 0:128], 0.0, ALU.add, ALU.max))
        step.settle()
        step(v.tensor_tensor(q[3][:, 0:128], q[6][:, 0:128], q[6][:, 1:129], ALU.subtract))
        step(v.tensor_tensor(q[4][:, 0:128], q[2][:, 0:128], q[6][:, 1:129], ALU.subtract))
        step.settle()
        v.tensor_tensor(q[3][:, 0:128], q[3][:, 0:128], q[5][:, 0:128], ALU.add).then_inc(q_ready, 1)
        dve.wait_ge(q_exp, 1)
        step(v.tensor_tensor(q[1][:, 0:128], q[1][:, 0:128], q[4][:, 0:128], ALU.mult))
        step(v.memset(q[2][:, 0:1], 0.0))
        step.settle()
        v.tensor_tensor_scan(q[2][:, 1:129], q[3][:, 0:128], q[1][:, 0:128], 0.0, ALU.mult, ALU.add).then_inc(cr_done, 1)

        dve.wait_ge(xc_in, 2 * 16)

        def merge(g):
            dve.wait_ge(ng_in[g], 16 * GT)
            mine = slice(g * GT, (g + 1) * GT)
            own, car = ng[0:P, mine, :], xc[0:P, mine, :]
            w = [nw[0:P, c, :].rearrange("p (t k) -> p t k", k=K) for c in (0, 1)]
            step(v.tensor_tensor(nm[0:P], own[:, :, SK:SW], car[:, :, SK:SW], ALU.max))
            step.settle()
            step(v.tensor_tensor(w[0], own[:, :, SK:SW], nm[0:P], ALU.subtract))
            v.tensor_tensor(w[1], car[:, :, SK:SW], nm[0:P], ALU.subtract).then_inc(merge_d, 1)
            dve.wait_ge(merge_e, g + 1)
            step(v.tensor_tensor(nden[0:P], own[:, :, KR:SK], w[0], ALU.mult))
            step(v.tensor_tensor(nden2[0:P], car[:, :, KR:SK], w[1], ALU.mult))
            step.settle()
            step(v.scalar_tensor_tensor(nden[0:P], nden[0:P], 1e-16, nden2[0:P], ALU.add, ALU.add))
            step.settle()
            step(v.reciprocal(nden[0:P], nden[0:P]))
            step.settle()
            step(v.tensor_tensor(nden[0:P], nden[0:P], bc(full[0:P, mine].unsqueeze(2), [P, GT, K]), ALU.mult))
            step.settle()
            for c in (0, 1):
                step(v.tensor_tensor(w[c], w[c], nden[0:P], ALU.mult))
            step.settle()
            if g >= 2:
                dve.wait_ge(agg_psum, g - 1)
            mine_st = agg_st[g % 2]
            for rows_, w_, to in ((own, w[0], mine_st), (car, w[1], agg_c)):
                step(v.tensor_tensor(to[0:P].rearrange("p t (k r) -> p t k r", r=R),
                                     rows_[:, :, 0:KR].rearrange("p t (k r) -> p t k r", r=R),
                                     bc(w_.unsqueeze(3), [P, GT, K, R]), ALU.mult))
            step.settle()
            v.tensor_tensor(mine_st[0:P], mine_st[0:P], agg_c[0:P], ALU.add).then_inc(agg_ready, 1)
            dve.wait_ge(agg_ready, g + 1)

        def graph_rows(g):
            if g >= 2:
                dve.wait_ge(x2_ready, (g - 1) * GT)
            for t in range(GT):
                dve.wait_ge(y_psum, g * GT + (t + 1))
                v.tensor_tensor(acc[g % 2][0:P, t, :], y_ps[t][0:P, :], gx[0:P, g * GT + t, :], ALU.add).then_inc(y_used, 1)

        def x2_stats(g):
            for t in range(GT):
                dve.wait_ge(x2_ready, g * GT + (t + 1))
                step(v.bn_stats(st[0:P, t, :], x_sb[0:P, g * GT + t, :]))
            step.settle()
            for t in range(GT):
                step(v.bn_aggr(mv[0:P, g * GT + t, :], st[0:P, t, :]))
            step.settle()

        merge(0)
        merge(1)
        for g in range(NG):
            graph_rows(g)
            if g:
                x2_stats(g - 1)
            if g < NG - 2:
                merge(g + 2)
        x2_stats(NG - 1)
        v.memset(spare["dve"][:, :], 0.0).then_inc(stats2, 1)

        dve.wait_ge(stds2, 1)
        step(v.reciprocal(rstd[0:P, :], std[0:P, :]))
        step.settle()
        step(v.tensor_tensor(fac[0:P, :], rstd[0:P, :], rstd[0:P, :], ALU.mult))
        step.settle()
        v.tensor_tensor(fac[0:P, :], fac[0:P, :], mv[0:P, :, 1], ALU.mult).then_inc(r_read, 1)
        dve.wait_ge(stds2, 2)
        step(v.reciprocal(std2[0:P, :], std2[0:P, :]))
        step.settle()
        step(v.tensor_tensor(rstd[0:P, :], rstd[0:P, :], std2[0:P, :], ALU.mult))
        step.settle()
        def z_tile(g, t):
            v.tensor_scalar(stages[g % 2][0:P, t, :], x_sb[0:P, g * GT + t, :], mv[0:P, g * GT + t, 0:1],
                            rstd[0:P, g * GT + t:g * GT + t + 1], ALU.subtract, ALU.mult).then_inc(z_ready, 1)

        for t in range(GT):
            z_tile(0, t)
        for g in range(NG):
            if 2 <= g + 1 < NG:
                dve.wait_ge(z_outs[(g + 1) % 2], 32 * ((g + 1) // 2))
            for t in range(GT):
                dve.wait_ge(zT_psum, g * GT + t + 1)
                if g:
                    dve.wait_ge(r_psum, (g - 1) * GT + t + 1)
                v.tensor_scalar(xT_st[:, 1, t * P:(t + 1) * P], zT_ps[1][t],
                                cols[:, GAM + 1:GAM + 2], cols[:, BET + 1:BET + 2], ALU.mult, ALU.add).then_inc(zT_ready, 1)
                if g + 1 < NG:
                    z_tile(g + 1, t)

        ix = bc(iota8[0:P, :].unsqueeze(1), [P, T, NX])
        chosen = [c_[0:P].rearrange("p e t -> p t e") for c_ in (ch0, ch1)]
        dve.wait_ge(r_psum, T)
        step(v.tensor_tensor(rl[0:P], ps[5][0:P, 0:T * NX].rearrange("p (t e) -> p t e", e=NX),
                             bc(brr[0:P, :].unsqueeze(1), [P, T, NX]), ALU.add))
        step.settle()
        for c in (0, 1):
            step(v.tensor_reduce(rm[0:P, c, :], rl[0:P], AX.X, ALU.max))
            step.settle()
            step(v.tensor_tensor(rt[0:P], rl[0:P], bc(rm[0:P, c, :].unsqueeze(2), [P, T, NX]), ALU.is_equal))
            step.settle()
            step(v.scalar_tensor_tensor(rt[0:P], ix, -float(NX), rt[0:P], ALU.add, ALU.mult))
            step.settle()
            step(v.tensor_reduce(rf[0:P, :, c], rt[0:P], AX.X, ALU.min))
            step.settle()
            step(v.tensor_scalar(rf[0:P, :, c], rf[0:P, :, c], float(NX), None, ALU.add))
            step.settle()
            step(v.tensor_tensor(chosen[c], ix, bc(rf[0:P, :, c:c + 1], [P, T, NX]), ALU.is_equal))
            step.settle()
            if c == 0:
                step(v.scalar_tensor_tensor(rl[0:P], chosen[0], -2 * BIG, rl[0:P], ALU.mult, ALU.add))
                step.settle()
        v.tensor_tensor(chs[0:P], ch0[0:P], ch1[0:P], ALU.add).then_inc(choices, 1)
        v.tensor_tensor(rd[0:P], rm[0:P, 1, :], rm[0:P, 0, :], ALU.subtract).then_inc(r_diff, 1)
        v.memset(spare["dve"][:, :], 0.0).then_inc(nodes_done, 1)

        step(v.memset(gix[:, :], 0))

        def te(ap):
            return ap.rearrange("p e t -> p t e")

        dve.wait_ge(ranked_psum, 1)
        step(v.tensor_copy(tot, ps[1][:, 0:TX].rearrange("p (e t) -> p e t", t=T)))
        step.settle()
        for e in range(NX):
            step(v.tensor_tensor_scan(excl[:, e, :], ones[:, 0:T], tot[:, e, :], 0.0, ALU.mult, ALU.add))
        step.settle()
        step(v.tensor_tensor(cmpb, bc(excl[:, :, T - 1:T], [128, NX, T]), bc(steps_b[:, :].unsqueeze(1), [128, NX, T]), ALU.is_gt))
        step(v.tensor_tensor(tot, excl, tot, ALU.subtract))
        step.settle()
        step(v.tensor_reduce(nblk, cmpb, AX.X, ALU.add))
        step(v.tensor_tensor(rank[0:P], ps[0][0:P, 0:TX].rearrange("p (e t) -> p e t", t=T), tot[0:P], ALU.add))
        step.settle()
        step(v.tensor_tensor_scan(bend, ones[:, 0:NX], nblk, 0.0, ALU.mult, ALU.add))
        step.settle()
        step(v.tensor_tensor(bstart, bend, nblk, ALU.subtract))
        step(v.tensor_tensor(cmpx, bc(iota_b[:, :].unsqueeze(2), [128, XB, NX]), bc(bend.unsqueeze(1), [128, XB, NX]), ALU.is_ge))
        step.settle()
        step(v.tensor_reduce(spos[:, :], cmpx, AX.X, ALU.add))
        step(v.tensor_scalar(bstart, bstart, float(BX), None, ALU.mult))
        step.settle()
        step(v.tensor_scalar(eix[:, :], spos[:, :], float(NX - 1), None, ALU.min))
        step(v.tensor_tensor(rank[0:P], rank[0:P], bc(bstart[0:P].unsqueeze(2), [P, NX, T]), ALU.add))
        step.settle()
        step(v.tensor_tensor(ch0[0:P], ch0[0:P], rank[0:P], ALU.mult))
        step(v.tensor_tensor(ch1[0:P], ch1[0:P], rank[0:P], ALU.mult))
        step.settle()
        step(v.tensor_reduce(slot[0:P, 0, :], te(ch0[0:P]), AX.X, ALU.add))
        step(v.tensor_reduce(slot[0:P, 1, :], te(ch1[0:P]), AX.X, ALU.add))
        step.settle()
        sl, hi_, lo_, fx = slot[0:P], shi[0:P], slo[0:P], sfx[0:P]
        step(v.tensor_scalar(hi_, sl, 1.0 / BX, 0.5 / BX - 0.5, ALU.mult, ALU.add))
        step.settle()
        step(v.tensor_copy(sint[0:P], hi_))
        step.settle()
        step(v.tensor_copy(hi_, sint[0:P]))
        step.settle()
        step(v.scalar_tensor_tensor(lo_, hi_, -float(BX), sl, ALU.mult, ALU.add))
        step.settle()
        step(v.tensor_scalar(fx, lo_, 0.0, None, ALU.is_lt))
        step.settle()
        step(v.tensor_tensor(hi_, hi_, fx, ALU.subtract))
        step(v.scalar_tensor_tensor(lo_, fx, float(BX), lo_, ALU.mult, ALU.add))
        step.settle()
        step(v.tensor_scalar(fx, lo_, float(BX), None, ALU.is_ge))
        step.settle()
        step(v.tensor_tensor(hi_, hi_, fx, ALU.add))
        step(v.scalar_tensor_tensor(lo_, fx, -float(BX), lo_, ALU.mult, ALU.add))
        step.settle()
        dve.wait_ge(r_exp, 1)
        step(v.tensor_scalar(fac[0:P, :], rd[0:P, :], 1.0, None, ALU.add))
        step.settle()
        step(v.reciprocal(rp[0:P, 0, :], fac[0:P, :]))
        step.settle()
        step(v.tensor_tensor(rp[0:P, 1, :], rd[0:P, :], rp[0:P, 0, :], ALU.mult))
        step.settle()
        v.memset(spare["dve"][:, :], 0.0).then_inc(slot_known, 1)
        dve.wait_ge(z_outs[0], 32 * 3)
        dve.wait_ge(z_outs[1], 32 * 2)
        for g in range(NG):
            if g >= 2:
                dve.wait_ge(oh_used, g - 1)
            mine = slice(g * GT, (g + 1) * GT)
            for c in (0, 1):
                v.tensor_tensor(oh_v[g % 2][0:P, c, :, 0:XB], bc(iota_b[0:P, :].unsqueeze(1), [P, GT, XB]),
                                bc(shi[0:P, c, mine].unsqueeze(2), [P, GT, XB]), ALU.is_equal).then_inc(oh_blocks, 1)
                v.tensor_tensor(oh_lo[g % 2][0:P, c], bc(iota_lo[0:P, :].unsqueeze(1), [P, GT, BX]),
                                bc(slo[0:P, c, mine].unsqueeze(2), [P, GT, BX]), ALU.is_equal).then_inc(oh_ready, 1)
        dve.wait_ge(slots_psum, 1)
        step(v.tensor_copy(sid[:, :], ps[2][:, 0:XB]))
        step(v.tensor_copy(sw[:, :], ps[2][:, XB:2 * XB]))
        step.settle()
        step(v.tensor_scalar(gix[:, 0:XB], sid[:, :], -1.0, 0.0, ALU.add, ALU.max))
        step(v.tensor_scalar(sfill[:, :], sid[:, :], 0.5, None, ALU.is_gt))
        step(v.tensor_scalar(spos[:, :], sid[:, :], dump[:, 0:1], 1.0, ALU.subtract, ALU.subtract))
        step.settle()
        step(v.tensor_tensor(spos[:, :], spos[:, :], sfill[:, :], ALU.mult))
        step.settle()
        v.tensor_scalar(six[:, :], spos[:, :], dump[:, 0:1], None, ALU.add).then_inc(slots_ready, 1)

        dve.wait_ge(b1_in, 16)
        dve.wait_ge(b2_in, 16)
        dve.wait_ge(slots_ready, 1)

        def rows_T(i, h):
            dve.wait_ge(xg_psum, i * XQ + (h + 1))
            for k in (0, 1):
                v.tensor_scalar(xb[h % 2][:, k, :], ps[h % 2][:, k * BX:(k + 1) * BX], cols[:, GAM + k:GAM + k + 1],
                                cols[:, BET + k:BET + k + 1], ALU.mult, ALU.add).then_inc(xb_ready, 1)

        def first_bias(i, h):
            e = dve.value_load(eix[0:1, bass.ds(i * XQ + h, 1)], min_val=0, max_val=NX - 1)
            dve.wait_ge(h_psum, i * XQ + (h + 1))
            v.tensor_tensor(hb[h % 2], ps[2 + h % 2][:, :], b1row[:, bass.ds(e, 1), :].rearrange("p e m -> p (e m)"),
                            ALU.add).then_inc(hb_ready, 1)

        def rows_y(i, h, first=False):
            e = dve.value_load(eix[0:1, bass.ds(i * XQ + h, 1)], min_val=0, max_val=NX - 1)
            dve.wait_ge(ye_psum, i * XQ + (h + 1))
            if not first:
                dve.wait_ge(added, i * (16 * XQ) + 16 * (h - XQ + 1))
            y = yb[h % XQ]
            v.tensor_tensor(y, ps[6 + h % 2][:, 0:D], b2row[:, bass.ds(e, 1), :].rearrange("p e m -> p (e m)"),
                            ALU.add).then_inc(yb_step, 1)
            dve.wait_ge(yb_step, i * XQ + (h + 1))
            v.tensor_scalar(y, y, sw[:, bass.ds(i * XQ + h, 1)], None, ALU.mult).then_inc(yb_ready, 1)

        rows_T(0, 0)
        for h in range(XQ):
            rows_T(0, h + 1)
            first_bias(0, h)
            if h >= 2:
                rows_y(0, h - 2, True)
        for h in range(XQ):
            rows_T(1, h + 1)
            first_bias(1, h)
            rows_y(1, h - 2, h < 2)
        with dve.Fori(2, XI) as i:
            for h in range(XQ):
                rows_T(i, h + 1)
                first_bias(i, h)
                rows_y(i, h - 2)
        rows_y(XI - 1, XQ - 2)
        rows_y(XI - 1, XQ - 1)

    @block.tensor
    def _(pe):
        mm, tr = nc.tensor.matmul, nc.tensor.transpose

        def warm(products):
            for _ in range(products):
                mm(ps[7][:, 0:384], zero[:, 0:128], zero[:, 0:384], start=True, stop=True)

        def x_tile(t, k):
            return xT_st[:, k, t * P:(t + 1) * P]

        pe.wait_ge(u_in, 2 * 16)
        pe.wait_ge(consts, 2)
        warm(6)
        mm(ps[7][:, 0:4], zero[:, 0:128], zero[:, 0:4], start=True, stop=True).then_inc(xT_psum, GT)
        mm(ps[7][:, 4:8], zero[:, 0:128], zero[:, 0:4], start=True, stop=True).then_inc(zu_psum, GT)
        with pe.Fori(0, NG) as g:
            def project(t):
                pe.wait_ge(xT_ready, g * GT + (t + 1))
                pe.wait_ge(zu_ready, g * GT + (t - 1 if t >= 2 else 0) + 1)
                for k in (0, 1):
                    ins = mm(ps[2 + t % 2][0:P, 0:KR], x_tile(t, k), u_sb[:, k, :], start=k == 0, stop=k == 1)
                ins.then_inc(zu_psum, 1)

            for t in range(GT):
                pe.wait_ge(xn_ready, g * GT + (t + 1))
                pe.wait_ge(xnT_ready, g * GT + (t + 1))
                for k in (0, 1):
                    ins = tr(xT_ps[t][:, k, :], stage[0:P, t, k * 128:(k + 1) * 128], ident[0:P, 0:P])
                ins.then_inc(xT_psum, 1)
                if t:
                    project(t - 1)
            project(GT - 1)

        pe.wait_ge(xnT_ready, GT + T)
        mm(ps[4][0:P, 0:T + 1], zero[:, 0:P], zero[:, 0:T + 1], start=True, stop=False,
           skip_group_check=True).then_inc(counted_block, 2)
        with pe.Fori(0, NB // 2) as i:
            for h in (0, 1):
                pe.wait_ge(onehot, i * 4 + 2 * (h + 1))
                for j in range(JB):
                    ins = mm(ps[4][0:P, 0:T + 1], one_p[h][:, j, :], one_t[h][:, j, :], start=False, stop=False, skip_group_check=True)
                ins.then_inc(counted_block, 1)
        mm(ps[4][0:P, 0:T + 1], zero[:, 0:P], zero[:, 0:T + 1], start=False, stop=True, skip_group_check=True).then_inc(counted, 1)
        pe.wait_ge(counts_sb, 1)
        mm(ps[5][0:P, 0:1], tri[0:P, 0:P], csb[0:P, T:T + 1], start=True, stop=True).then_inc(based, 1)

        pe.wait_ge(w_in, 16 * len(W_LOADS))
        pe.wait_ge(zu_ready, T + 1)
        tr(ps[0][:, 0:NR], rows[:, :], ident[0:NR, 0:NR]).then_inc(rows_psum, 1)
        for dt_ in (0, 1):
            for ct in (0, 1):
                ins = tr(ps[1][:, dt_ * D + ct * 128:dt_ * D + (ct + 1) * 128], wq[:, ct, dt_ * 128:(dt_ + 1) * 128], ident[:, :])
        ins.then_inc(wqT_psum, 1)
        for r in (0, 1):
            for k in (0, 1):
                ins = mm(ps[2][:, r * D:(r + 1) * D], dm[:, k, r * 128:(r + 1) * 128], dm[:, k, :], start=k == 0, stop=k == 1)
        ins.then_inc(dtd_psum, 1)
        pe.wait_ge(dtd_ready, 1)
        for r in (0, 1):
            for k in (0, 1):
                ins = mm(ps[3][:, r * D:(r + 1) * D], dtd[:, k, r * 128:(r + 1) * 128], dm[:, k, :], start=k == 0, stop=k == 1)
        ins.then_inc(b_psum, 1)

        pe.wait_ge(gh_ready, 2)
        for k in (0, 1):
            ins = mm(ps[7][0:64, 0:D], u_sb[:, k, :], gh[:, k, :], start=k == 0, stop=k == 1)
        ins.then_inc(ug_psum, 1)
        pe.wait_ge(ug_ready, 1)

        pe.wait_ge(places, 1)
        pe.wait_ge(wkv_ready, 2)
        pe.wait_ge(cols_ready, 1)
        pe.wait_ge(wqT_ready, 1)
        for hg in (0, 1):
            mm(ps[6 + hg][:, 0:384], zero[:, 0:128], zero[:, 0:384], start=True, stop=False, skip_group_check=True)
        with pe.Fori(0, NG) as g:
            def product(t):
                pe.wait_ge(kv_ready, g * (3 * GT) + 3 * (t + 1) + 1)
                for hg in (0, 1):
                    v_ = vh[0:P, t % 4, hg * 128:(hg + 1) * 128]
                    mm(ps[6 + hg][:, 0:129], v_, kh[0:P, t % 4, hg, :], start=False, stop=False, skip_group_check=True)
                    ins = mm(ps[6 + hg][:, 256:384], ones[0:P, :], kh[0:P, t % 4, hg, 0:128], start=False, stop=False, skip_group_check=True)
                ins.then_inc(kv_used, 1)

            for t in range(GT):
                pe.wait_ge(kx_ready, g * GT + (t + 1))
                pe.wait_ge(kv_ready, g * (3 * GT) + (3 * (t - AHEAD + 1) if t >= AHEAD else 0) + 1)
                mm(kv_ps[t][0:P, :], ones[32:33, 0:P], kvb[:, :], start=True, stop=False)
                for k in (0, 1):
                    ins = mm(kv_ps[t][0:P, :], x_tile(t, k), wkv[:, k, :], start=False, stop=k == 1)
                ins.then_inc(kv_psum, 1)
                pe.wait_ge(gx_ready, g * GT + (t - AHEAD + 1 if t >= AHEAD else 0) + 1)
                for k in (0, 1):
                    ins = mm(gx_ps[t][0:P, :], x_tile(t, k), gh[:, k, :], start=k == 0, stop=k == 1)
                ins.then_inc(gx_psum, 1)
                if t >= AHEAD - 1:
                    product(t - AHEAD + 1)
            for t in range(GT - AHEAD + 1, GT):
                product(t)
        for hg in (0, 1):
            ins = mm(ps[6 + hg][:, 0:384], zero[:, 0:128], zero[:, 0:384], start=False, stop=True, skip_group_check=True)
        ins.then_inc(kv_summed, 1)

        pe.wait_ge(kvt_ready, 2)
        for hg in (0, 1):
            ins = mm(ps[4][:, hg * D:(hg + 1) * D], kvc[:, hg, :], w1[:, hg, :], start=True, stop=True)
        ins.then_inc(t1_psum, 1)
        pe.wait_ge(t1_ready, 1)
        for c in (0, 1):
            for k in (0, 1):
                ins = mm(ps[5][:, c * D:(c + 1) * D], wqT[:, k, c * 128:(c + 1) * 128], t1[:, k, :], start=k == 0, stop=k == 1)
        for m in (0, 1):
            for k in (0, 1):
                ins = mm(ps[4][:, m:m + 1], t1[:, k, m * 128:(m + 1) * 128], cols[:, BQ + k:BQ + k + 1], start=k == 0, stop=k == 1)
        ins.then_inc(we_psum, 1)

        pe.wait_ge(we_ready, 1)
        def mix_hidden(g):
            for m in (0, 1):
                for c, (lo, hi) in enumerate(CUTS):
                    for k in (0, 1):
                        ins = mm(ps[2 * m + c][:, 0:hi - lo], weff[:, k, m * 128:(m + 1) * 128],
                                 xnT[:, bass.ds(g, 1), :].rearrange("p g c -> p (g c)")[:, k * GC + lo:k * GC + hi],
                                 start=k == 0, stop=k == 1)
                    ins.then_inc(mh_psum, 1)

        def mix_out(t):
            mm(mo_ps[t][0:P, :], ones[64:65, 0:P], mb2, start=True, stop=False)
            for m in (0, 1):
                ins = mm(mo_ps[t][0:P, :], mixh[:, m, t * P:(t + 1) * P], w2[:, m, :], start=False, stop=m == 1)
            ins.then_inc(mo_psum, 1)

        mix_hidden(0)
        pe.wait_ge(row_ready, 1)
        mm(ps[6][0:SK, 0:128], ones[0:1, 0:SK], row[0:1, 4, :], start=True, stop=True)
        mm(ps[7][:, 0:1], row[0:1, 0, :], ones[0:1, 0:1], start=True, stop=True).then_inc(row_psum, 1)
        pe.wait_ge(cr_ready, 1)
        with pe.Fori(0, NG - 1) as g:
            pe.wait_ge(mh_ready, g * 4 + 4)
            pe.wait_ge(mo_ready, g * GT + 1)
            for t in range(GT - 1):
                mix_out(t)
            mix_hidden(g + 1)
            pe.wait_ge(mo_ready, g * GT + 1 + 1)
            mix_out(GT - 1)
        pe.wait_ge(mh_ready, 4 * NG)
        pe.wait_ge(mo_ready, (NG - 1) * GT + 1)
        for t in range(GT - 1):
            mix_out(t)
        pe.wait_ge(mo_ready, (NG - 1) * GT + 1 + 1)
        mix_out(GT - 1)

        pe.wait_ge(mo_ready, T + 1)
        pe.wait_ge(fin_ready, 1)
        tr(ps[0][0:SK, 0:128], fin[:, 0:SK], ident[:, :])
        tr(ps[0][0:SK, 128:256], fin[:, SK:2 * SK], ident[:, :]).then_inc(fin_psum, 1)
        pe.wait_ge(cr_done, 1)
        tr(ps[0][:, 0:SK], q[2][:, 0:128], ident[0:SK, 0:SK])
        tr(ps[1][:, 0:SK], q[6][:, 0:128], ident[0:SK, 0:SK]).then_inc(cr_psum, 1)

        def aggregates_T(g):
            pe.wait_ge(agg_ready, g + 1)
            if g:
                pe.wait_ge(aggT_ready, g)
            for t in range(GT):
                ins = tr(ps[6 + t // 4][0:64, (t % 4) * P:(t % 4 + 1) * P], agg_st[g % 2][0:P, t, :], ident[0:P, 0:P])
            ins.then_inc(agg_psum, 1)

        aggregates_T(0)
        for g in range(NG):
            pe.wait_ge(aggT_ready, g + 1)
            for t in range(GT):
                if g or t >= 4:
                    pe.wait_ge(y_used, g * GT + (1 if t >= 4 else 0))
                mm(y_ps[t][0:P, :], aggT[g % 2][:, t * P:(t + 1) * P], ug[:, :], start=True, stop=True).then_inc(y_psum, 1)
            if g < NG - 1:
                aggregates_T(g + 1)

        pe.wait_ge(y_used, T)

        def router(g, t):
            pe.wait_ge(zT_ready, g * GT + t + 1)
            pe.wait_ge(zT_act, g * GT + t + 1)
            at = (g * GT + t) * NX
            for k in (0, 1):
                ins = mm(ps[5][0:P, at:at + NX], x_tile(t, k), wr[:, k, :], start=k == 0, stop=k == 1)
            ins.then_inc(r_psum, 1)

        for g in range(NG):
            for t in range(GT):
                pe.wait_ge(z_ready, g * GT + t + 1)
                if g or t >= 3:
                    pe.wait_ge(zT_ready, g * GT + max(t - 2, 0))
                    pe.wait_ge(zT_act, g * GT + max(t - 2, 0))
                for k in (0, 1):
                    ins = tr(zT_ps[k][t], stages[g % 2][0:P, t, k * 128:(k + 1) * 128], ident[0:P, 0:P])
                ins.then_inc(zT_psum, 1)
                if g or t >= 2:
                    router((g * GT + t - 2) // GT, (t - 2) % GT)
        router(NG - 1, GT - 2)
        router(NG - 1, GT - 1)

        pe.wait_ge(choices, 1)
        mm(ps[0][0:P, 0:TX], tri[0:P, 0:P], chs[0:P].rearrange("p e t -> p (e t)"), start=True, stop=True)
        mm(ps[1][:, 0:TX], ones[0:P, :], chs[0:P].rearrange("p e t -> p (e t)"), start=True, stop=True).then_inc(ranked_psum, 1)
        for g in range(NG):
            for c in (0, 1):
                pe.wait_ge(oh_ready, 2 * g + c + 1)
                pe.wait_ge(oh_pool, 2 * g + c + 1)
                for t in range(GT):
                    first, last = g == 0 and c == 0 and t == 0, g == NG - 1 and c == 1 and t == GT - 1
                    ins = mm(ps[2][:, 0:2 * XB], oh_lo[g % 2][0:P, c, t, :], oh_v[g % 2][0:P, c, t, :], start=first, stop=last)
            ins.then_inc(oh_used if g < NG - 1 else slots_psum, 1)

        pe.wait_ge(slots_ready, 1)
        pe.wait_ge(xw_in, 8 * 16)

        def rows_T(i, h, first=False):
            pe.wait_ge(xg_in[h % XQ], i * 16 + 16 * (h // XQ + 1))
            if not first:
                pe.wait_ge(xb_ready, i * (2 * XQ) + 2 * (h - 1))
            for k in (0, 1):
                ins = tr(ps[h % 2][:, k * BX:(k + 1) * BX], xg[h % XQ][:, k * 128:(k + 1) * 128], ident[:, :])
            ins.then_inc(xg_psum, 1)

        def expert(i, h):
            return pe.value_load(eix[0:1, bass.ds(i * XQ + h, 1)], min_val=0, max_val=NX - 1)

        def hidden(i, h, e, first=False):
            pe.wait_ge(xb_ready, i * (2 * XQ) + 2 * (h + 1))
            if not first:
                pe.wait_ge(hb_ready, i * XQ + (h - 1))
            for k in (0, 1):
                ins = mm(ps[2 + h % 2][:, :], xb[h % 2][:, k, :], W1[:, bass.ds(e, 1), k, :].rearrange("p e m -> p (e m)"),
                         start=k == 0, stop=k == 1)
            ins.then_inc(h_psum, 1)

        def hidden_T(i, h, first=False):
            pe.wait_ge(hg_ready, i * XQ + (h + 1))
            if not first:
                pe.wait_ge(hT_ready, i * XQ + (h - 1))
            for m in range(4):
                ins = tr(ps[4 + h % 2][:, m * BX:(m + 1) * BX], hb[h % 2][:, m * 128:(m + 1) * 128], ident[:, :])
            ins.then_inc(hT_psum, 1)

        def results(i, h, e, first=False):
            pe.wait_ge(hT_ready, i * XQ + (h + 1))
            if not first:
                pe.wait_ge(yb_step, i * XQ + (h - 1))
            for m in range(4):
                ins = mm(ps[6 + h % 2][:, 0:D], hT[h % 2][:, m, :], W2[:, bass.ds(e, 1), m, :].rearrange("p e m -> p (e m)"),
                         start=m == 0, stop=m == 3)
            ins.then_inc(ye_psum, 1)

        rows_T(0, 0, True)
        for h in range(XQ):
            rows_T(0, h + 1, h + 1 < 2)
            hidden(0, h, expert(0, h), h < 2)
            if h >= 1:
                hidden_T(0, h - 1, h < 3)
            if h >= 2:
                results(0, h - 2, expert(0, h - 2), h < 4)
        with pe.Fori(1, XI) as i:
            for h in range(XQ):
                e_hidden, e_results = expert(i, h), expert(i, h - 2)
                rows_T(i, h + 1)
                hidden(i, h, e_hidden)
                hidden_T(i, h - 1)
                results(i, h - 2, e_results)
        results(XI - 1, XQ - 2, expert(XI - 1, XQ - 2))
        hidden_T(XI - 1, XQ - 1)
        results(XI - 1, XQ - 1, expert(XI - 1, XQ - 1))


_INS = ['x', 'src', 'dst', 'L0_gnn_U', 'L0_gnn_Dmat', 'L0_gnn_head_w', 'L0_mix_w_qkv', 'L0_mix_b_qkv', 'L0_mix_kln_g',
        'L0_mix_kln_b', 'L0_mix_vln_g', 'L0_mix_vln_b', 'L0_mix_w1', 'L0_mix_b1', 'L0_mix_w2', 'L0_mix_b2',
        'L0_ffn_gamma', 'L0_ffn_beta', 'L0_ffn_Wr', 'L0_ffn_br', 'L0_ffn_W1', 'L0_ffn_b1', 'L0_ffn_W2', 'L0_ffn_b2']


def kernel(**inputs):
    import numpy as np
    import concourse.bacc as bacc
    from concourse import mybir as mb
    from concourse.bass_utils import run_bass_kernel_spmd

    nc = bacc.Bacc("TRN2", target_bir_lowering=False, num_devices=1)
    arrays, args = {}, {}
    for name in _INS:
        arr = np.ascontiguousarray(inputs[name])
        arrays[f"in_{name}"] = arr
        args[name] = nc.dram_tensor(f"in_{name}", arr.shape, mb.dt.from_np(arr.dtype), kind="ExternalInput").ap()
    out = nc.dram_tensor("out", (N + 128, D), F32, kind="ExternalOutput").ap()
    program(nc, args, out)
    r = run_bass_kernel_spmd(nc, [arrays], core_ids=[0])
    return r.results[0]["out"][0:N]
```
